# Optimizing a Trainium2 kernel written in Bass

```python
import numpy as np
import jax
import jax.numpy as jnp

def _softmax(x, axis=-1):
    return jax.nn.softmax(x, axis=axis)

def _gelu(x):
    return jax.nn.gelu(x, approximate=True)

def _silu(x):
    return jax.nn.silu(x)

def _sigmoid(x):
    return jax.nn.sigmoid(x)

def _layernorm(x, axis=-1, eps=1e-05):
    m = jnp.mean(x, axis=axis, keepdims=True)
    v = jnp.var(x, axis=axis, keepdims=True)
    return (x - m) / jnp.sqrt(v + eps)

def _scatter_add(tgt, idx, src, axis=0):
    return tgt.at[idx].add(src)

def _segment_sum(src, seg, n):
    return jax.ops.segment_sum(src, seg, n)
kernel_name = 'mk_decoder_preln_d2_seqx_r4_5ec2a1'

def setup_inputs(seed: int=0):
    np.random.seed(seed)
    _w = jnp.asarray

    def _rec_inputs():
        import jax
        import jax.numpy as jnp
        _rk = jax.random.key(seed)
        x = -0.000125 + 0.9999 * jax.random.normal(jax.random.fold_in(_rk, 1), (2, 512, 512), jnp.float32)
        _lenS = 512 - jax.random.randint(jax.random.fold_in(_rk, 7), (2,), 0, max(1, 512 // 4) + 1, jnp.int32)
        _lenS2 = 1024 - jax.random.randint(jax.random.fold_in(_rk, 8), (2,), 0, max(1, 1024 // 4) + 1, jnp.int32)
        _ctx_2048P = jax.random.normal(jax.random.fold_in(_rk, 11), (2, 16, 512), jnp.float32)
        _ctx_2048c = jax.random.dirichlet(jax.random.fold_in(_rk, 511), 0.3 * jnp.ones((16,), jnp.float32), (2, 1024))
        _ctx_2048t = jnp.einsum('bsk,bkd->bsd', _ctx_2048c, _ctx_2048P)
        _ctx_2048t = _ctx_2048t * jax.lax.rsqrt(jnp.mean(jnp.square(_ctx_2048t)) + 1e-12) * 0.953939
        ctx_2048 = -1.52775e-05 + 0.999936 * (_ctx_2048t + 0.3 * jax.random.normal(jax.random.fold_in(_rk, 611), (2, 1024, 512), jnp.float32))
        return (x, ctx_2048)
    x, ctx_2048 = _rec_inputs()

    def _L0_attn_setup():
        import jax, jax.numpy as jnp
        import numpy as np
        import math
        EMBED_DIM = 512
        NUM_HEADS = 16
        HEAD_DIM = EMBED_DIM // NUM_HEADS
        ROPE_BASE = 10000.0

        def apply_rope(x):
            B, S, H, D = x.shape
            half = D // 2
            positions = jnp.arange(S, dtype=x.dtype)
            inv_freq = 1.0 / ROPE_BASE ** (jnp.arange(0, D, 2, dtype=x.dtype) / D)
            angles = positions[:, None] * inv_freq[None, :]
            sin = jnp.sin(angles)[None, :, None, :]
            cos = jnp.cos(angles)[None, :, None, :]
            x1, x2 = (x[..., :half], x[..., half:])
            return jnp.concatenate([x1 * cos - x2 * sin, x1 * sin + x2 * cos], axis=-1)
        key = jax.random.key(seed)
        ks = jax.random.split(key, 5)
        B, S, E = (2, 512, EMBED_DIM)
        scale = 1.0 / math.sqrt(E)
        return {'x': jax.random.normal(ks[0], (B, S, E), dtype=jnp.float32), 'wq': jax.random.normal(ks[1], (E, E), dtype=jnp.float32) * scale, 'wk': jax.random.normal(ks[2], (E, E), dtype=jnp.float32) * scale, 'wv': jax.random.normal(ks[3], (E, E), dtype=jnp.float32) * scale, 'wo': jax.random.normal(ks[4], (E, E), dtype=jnp.float32) * scale}
    _L0_attn_all = _L0_attn_setup()
    _L0_attn_in = {k: v for k, v in _L0_attn_all.items() if k in ('wq', 'wk', 'wv', 'wo')}
    del _L0_attn_all

    def _L0_xattn_setup():
        import jax, jax.numpy as jnp
        import numpy as np
        EPS = 1e-06
        NUM_HEADS = 16

        def _feature_map(x):
            return jnp.where(x > 0, x + 1.0, jnp.exp(x))
        key = jax.random.key(seed)
        ks = jax.random.split(key, 7)
        B, L, S, D = (4, 1024, 1024, 512)
        sc = 1.0 / np.sqrt(D)
        return {'query': jax.random.normal(ks[0], (B, L, D), jnp.float32), 'kv': jax.random.normal(ks[1], (B, S, D), jnp.float32), 'Wq': jax.random.normal(ks[2], (D, D), jnp.float32) * sc, 'Wg': jax.random.normal(ks[3], (D, D), jnp.float32) * sc, 'bg': jnp.ones((D,), jnp.float32), 'Wkv': jax.random.normal(ks[4], (2 * D, D), jnp.float32) * sc, 'Wo': jax.random.normal(ks[5], (D, D), jnp.float32) * sc}
    _L0_xattn_all = _L0_xattn_setup()
    _L0_xattn_in = {k: v for k, v in _L0_xattn_all.items() if k in ('Wq', 'Wg', 'bg', 'Wkv', 'Wo')}
    del _L0_xattn_all

    def _L0_ffn_setup():
        import jax, jax.numpy as jnp
        import numpy as np
        ALPHA = 1.702
        LIMIT = 7.0
        TOP_K = 2
        E, H, I = (8, 512, 512)
        B, S = (2, 512)
        key = jax.random.key(seed)
        ks = jax.random.split(key, 7)
        return {'hidden_states': jax.random.normal(ks[0], (B, S, H), dtype=jnp.float32), 'router_weight': jax.random.normal(ks[1], (E, H), dtype=jnp.float32) * 0.02, 'router_bias': jax.random.normal(ks[2], (E,), dtype=jnp.float32) * 0.02, 'gate_up_proj': jax.random.normal(ks[3], (E, H, 2 * I), dtype=jnp.float32) * 0.02, 'gate_up_proj_bias': jax.random.normal(ks[4], (E, 2 * I), dtype=jnp.float32) * 0.02, 'down_proj': jax.random.normal(ks[5], (E, I, H), dtype=jnp.float32) * 0.02, 'down_proj_bias': jax.random.normal(ks[6], (E, H), dtype=jnp.float32) * 0.02}
    _L0_ffn_all = _L0_ffn_setup()
    _L0_ffn_in = {k: v for k, v in _L0_ffn_all.items() if k in ('router_weight', 'router_bias', 'gate_up_proj', 'gate_up_proj_bias', 'down_proj', 'down_proj_bias')}
    del _L0_ffn_all

    def _L1_attn_setup():
        import jax, jax.numpy as jnp
        import numpy as np
        B, N, DIM = (2, 512, 512)
        HEADS, DIM_HEAD, GQA = (16, 64, 4)
        KV_HEADS = HEADS // GQA
        DIM_INNER = HEADS * DIM_HEAD
        KV_INNER = KV_HEADS * DIM_HEAD
        THETA = 10000.0

        def _rotate_half(t):
            t1, t2 = jnp.split(t, 2, axis=-1)
            return jnp.concatenate([-t2, t1], axis=-1)
        key = jax.random.key(seed)
        k1, k2, k3 = jax.random.split(key, 3)
        x = jax.random.normal(k1, (B, N, DIM), dtype=jnp.float32)
        gamma = jnp.ones((DIM,), dtype=jnp.float32)
        w_qkv = jax.random.normal(k2, (DIM, DIM_INNER + 2 * KV_INNER), dtype=jnp.float32) * DIM ** (-0.5)
        w_out = jax.random.normal(k3, (DIM_INNER, DIM), dtype=jnp.float32) * DIM_INNER ** (-0.5)
        return {'x': x, 'gamma': gamma, 'w_qkv': w_qkv, 'w_out': w_out}
    _L1_attn_all = _L1_attn_setup()
    _L1_attn_in = {k: v for k, v in _L1_attn_all.items() if k in ('gamma', 'w_qkv', 'w_out')}
    del _L1_attn_all

    def _L1_xattn_setup():
        import jax, jax.numpy as jnp
        import numpy as np
        DIM = 512
        NH = 16
        HD = DIM // NH
        EPS = 1e-06
        IMG_LEN = 257

        def rms_norm(x, w, eps=EPS):
            xf = x.astype(jnp.float32)
            y = xf * jax.lax.rsqrt(jnp.mean(xf * xf, axis=-1, keepdims=True) + eps)
            return y.astype(x.dtype) * w

        def linear(x, w, b):
            return jnp.einsum('blc,oc->blo', x, w) + b

        def attention(q, k, v):
            scale = 1.0 / jnp.sqrt(jnp.asarray(HD, q.dtype))
            scores = jnp.einsum('bqhd,bkhd->bhqk', q, k) * scale
            probs = jax.nn.softmax(scores, axis=-1)
            return jnp.einsum('bhqk,bkhd->bqhd', probs, v)
        key = jax.random.key(seed)
        ks = jax.random.split(key, 12)
        B, L = (2, 2048)
        s = 0.02
        inp = {'x': jax.random.normal(ks[0], (B, L, DIM), jnp.float32), 'context': jax.random.normal(ks[1], (B, 769, DIM), jnp.float32), 'q_w': jax.random.normal(ks[2], (DIM, DIM), jnp.float32) * s, 'q_b': jnp.zeros((DIM,), jnp.float32), 'k_w': jax.random.normal(ks[3], (DIM, DIM), jnp.float32) * s, 'k_b': jnp.zeros((DIM,), jnp.float32), 'v_w': jax.random.normal(ks[4], (DIM, DIM), jnp.float32) * s, 'v_b': jnp.zeros((DIM,), jnp.float32), 'k_img_w': jax.random.normal(ks[5], (DIM, DIM), jnp.float32) * s, 'k_img_b': jnp.zeros((DIM,), jnp.float32), 'v_img_w': jax.random.normal(ks[6], (DIM, DIM), jnp.float32) * s, 'v_img_b': jnp.zeros((DIM,), jnp.float32), 'o_w': jax.random.normal(ks[7], (DIM, DIM), jnp.float32) * s, 'o_b': jnp.zeros((DIM,), jnp.float32), 'norm_q_w': jnp.ones((DIM,), jnp.float32), 'norm_k_w': jnp.ones((DIM,), jnp.float32), 'norm_k_img_w': jnp.ones((DIM,), jnp.float32)}
        return inp
    _L1_xattn_all = _L1_xattn_setup()
    _L1_xattn_in = {k: v for k, v in _L1_xattn_all.items() if k in ('q_w', 'q_b', 'k_w', 'k_b', 'v_w', 'v_b', 'k_img_w', 'k_img_b', 'v_img_w', 'v_img_b', 'o_w', 'o_b', 'norm_q_w', 'norm_k_w', 'norm_k_img_w')}
    del _L1_xattn_all

    def _L1_ffn_setup():
        import jax, jax.numpy as jnp
        import numpy as np
        TOP_K = 2
        NUM_EXPERTS = 8
        ROUTE_SCALE = 1.0
        key = jax.random.key(seed)
        ks = jax.random.split(key, 8)
        bs, slen, dim, hidden, E = (4, 256, 512, 256, NUM_EXPERTS)
        s = 0.02
        return {'x': jax.random.normal(ks[0], (bs, slen, dim), jnp.float32), 'gate_w': jax.random.normal(ks[1], (E, dim), jnp.float32) * s, 'w1': jax.random.normal(ks[2], (E, hidden, dim), jnp.float32) * s, 'w2': jax.random.normal(ks[3], (E, dim, hidden), jnp.float32) * s, 'w3': jax.random.normal(ks[4], (E, hidden, dim), jnp.float32) * s, 'ws1': jax.random.normal(ks[5], (hidden, dim), jnp.float32) * s, 'ws2': jax.random.normal(ks[6], (dim, hidden), jnp.float32) * s, 'ws3': jax.random.normal(ks[7], (hidden, dim), jnp.float32) * s}
    _L1_ffn_all = _L1_ffn_setup()
    _L1_ffn_in = {k: v for k, v in _L1_ffn_all.items() if k in ('gate_w', 'w1', 'w2', 'w3', 'ws1', 'ws2', 'ws3')}
    del _L1_ffn_all
    return {'x': x, 'ctx_2048': ctx_2048, 'L0_attn_wq': _L0_attn_in['wq'], 'L0_attn_wk': _L0_attn_in['wk'], 'L0_attn_wv': _L0_attn_in['wv'], 'L0_attn_wo': _L0_attn_in['wo'], 'L0_xattn_Wq': _L0_xattn_in['Wq'], 'L0_xattn_Wg': _L0_xattn_in['Wg'], 'L0_xattn_bg': _L0_xattn_in['bg'], 'L0_xattn_Wkv': _L0_xattn_in['Wkv'], 'L0_xattn_Wo': _L0_xattn_in['Wo'], 'L0_ffn_router_weight': _L0_ffn_in['router_weight'], 'L0_ffn_router_bias': _L0_ffn_in['router_bias'], 'L0_ffn_gate_up_proj': _L0_ffn_in['gate_up_proj'], 'L0_ffn_gate_up_proj_bias': _L0_ffn_in['gate_up_proj_bias'], 'L0_ffn_down_proj': _L0_ffn_in['down_proj'], 'L0_ffn_down_proj_bias': _L0_ffn_in['down_proj_bias'], 'L1_attn_gamma': _L1_attn_in['gamma'], 'L1_attn_w_qkv': _L1_attn_in['w_qkv'], 'L1_attn_w_out': _L1_attn_in['w_out'], 'L1_xattn_q_w': _L1_xattn_in['q_w'], 'L1_xattn_q_b': _L1_xattn_in['q_b'], 'L1_xattn_k_w': _L1_xattn_in['k_w'], 'L1_xattn_k_b': _L1_xattn_in['k_b'], 'L1_xattn_v_w': _L1_xattn_in['v_w'], 'L1_xattn_v_b': _L1_xattn_in['v_b'], 'L1_xattn_k_img_w': _L1_xattn_in['k_img_w'], 'L1_xattn_k_img_b': _L1_xattn_in['k_img_b'], 'L1_xattn_v_img_w': _L1_xattn_in['v_img_w'], 'L1_xattn_v_img_b': _L1_xattn_in['v_img_b'], 'L1_xattn_o_w': _L1_xattn_in['o_w'], 'L1_xattn_o_b': _L1_xattn_in['o_b'], 'L1_xattn_norm_q_w': _L1_xattn_in['norm_q_w'], 'L1_xattn_norm_k_w': _L1_xattn_in['norm_k_w'], 'L1_xattn_norm_k_img_w': _L1_xattn_in['norm_k_img_w'], 'L1_ffn_gate_w': _L1_ffn_in['gate_w'], 'L1_ffn_w1': _L1_ffn_in['w1'], 'L1_ffn_w2': _L1_ffn_in['w2'], 'L1_ffn_w3': _L1_ffn_in['w3'], 'L1_ffn_ws1': _L1_ffn_in['ws1'], 'L1_ffn_ws2': _L1_ffn_in['ws2'], 'L1_ffn_ws3': _L1_ffn_in['ws3']}

def reference(x, ctx_2048, L0_attn_wq, L0_attn_wk, L0_attn_wv, L0_attn_wo, L0_xattn_Wq, L0_xattn_Wg, L0_xattn_bg, L0_xattn_Wkv, L0_xattn_Wo, L0_ffn_router_weight, L0_ffn_router_bias, L0_ffn_gate_up_proj, L0_ffn_gate_up_proj_bias, L0_ffn_down_proj, L0_ffn_down_proj_bias, L1_attn_gamma, L1_attn_w_qkv, L1_attn_w_out, L1_xattn_q_w, L1_xattn_q_b, L1_xattn_k_w, L1_xattn_k_b, L1_xattn_v_w, L1_xattn_v_b, L1_xattn_k_img_w, L1_xattn_k_img_b, L1_xattn_v_img_w, L1_xattn_v_img_b, L1_xattn_o_w, L1_xattn_o_b, L1_xattn_norm_q_w, L1_xattn_norm_k_w, L1_xattn_norm_k_img_w, L1_ffn_gate_w, L1_ffn_w1, L1_ffn_w2, L1_ffn_w3, L1_ffn_ws1, L1_ffn_ws2, L1_ffn_ws3):
    import jax
    import jax.numpy as jnp

    def _L0_attn_ref(x, wq, wk, wv, wo):
        import jax, jax.numpy as jnp
        import numpy as np
        import math
        EMBED_DIM = 512
        NUM_HEADS = 16
        HEAD_DIM = EMBED_DIM // NUM_HEADS
        ROPE_BASE = 10000.0

        def apply_rope(x):
            B, S, H, D = x.shape
            half = D // 2
            positions = jnp.arange(S, dtype=x.dtype)
            inv_freq = 1.0 / ROPE_BASE ** (jnp.arange(0, D, 2, dtype=x.dtype) / D)
            angles = positions[:, None] * inv_freq[None, :]
            sin = jnp.sin(angles)[None, :, None, :]
            cos = jnp.cos(angles)[None, :, None, :]
            x1, x2 = (x[..., :half], x[..., half:])
            return jnp.concatenate([x1 * cos - x2 * sin, x1 * sin + x2 * cos], axis=-1)
        B, S, E = x.shape
        H, D = (NUM_HEADS, HEAD_DIM)
        q = (x @ wq).reshape(B, S, H, D)
        k = (x @ wk).reshape(B, S, H, D)
        v = (x @ wv).reshape(B, S, H, D)
        q = apply_rope(q)
        k = apply_rope(k)
        scores = jnp.einsum('bqhd,bkhd->bhqk', q, k) / math.sqrt(D)
        causal = jnp.triu(jnp.full((S, S), -jnp.inf, dtype=x.dtype), k=1)
        scores = scores + causal[None, None, :, :]
        attn = jax.nn.softmax(scores, axis=-1)
        out = jnp.einsum('bhqk,bkhd->bqhd', attn, v).reshape(B, S, E)
        return out @ wo

    def _L0_xattn_ref(query, kv, Wq, Wg, bg, Wkv, Wo):
        import jax, jax.numpy as jnp
        import numpy as np
        EPS = 1e-06
        NUM_HEADS = 16

        def _feature_map(x):
            return jnp.where(x > 0, x + 1.0, jnp.exp(x))
        B, L, D = query.shape
        S = kv.shape[1]
        H = NUM_HEADS
        hd = D // H
        q = query @ Wq.T
        gate = jax.nn.sigmoid(query @ Wg.T + bg)
        kvp = kv @ Wkv.T
        k, v = jnp.split(kvp, 2, axis=-1)
        q = _feature_map(q.reshape(B, L, H, hd).transpose(0, 2, 1, 3))
        k = _feature_map(k.reshape(B, S, H, hd).transpose(0, 2, 1, 3))
        v = v.reshape(B, S, H, hd).transpose(0, 2, 1, 3)
        kv_summary = jnp.einsum('bhsd,bhse->bhde', k, v)
        k_sum = k.sum(axis=-2)
        z = 1.0 / (jnp.einsum('bhld,bhd->bhl', q, k_sum)[..., None] + EPS)
        attn = jnp.einsum('bhld,bhde->bhle', q, kv_summary) * z
        attn = attn.transpose(0, 2, 1, 3).reshape(B, L, D)
        out = attn * gate @ Wo.T
        return out

    def _L0_ffn_ref(hidden_states, router_weight, router_bias, gate_up_proj, gate_up_proj_bias, down_proj, down_proj_bias):
        import jax, jax.numpy as jnp
        import numpy as np
        ALPHA = 1.702
        LIMIT = 7.0
        TOP_K = 2
        E, H, I = (8, 512, 512)
        B, S = (2, 512)
        bsz, seq_len, hidden = hidden_states.shape
        h = hidden_states.reshape(-1, hidden)
        T = h.shape[0]
        logits = h @ router_weight.T + router_bias
        top_vals, top_idx = jax.lax.top_k(logits, TOP_K)
        top_w = jax.nn.softmax(top_vals, axis=-1)
        scores = jnp.zeros_like(logits).at[jnp.arange(T)[:, None], top_idx].set(top_w)
        gate_up = jnp.einsum('th,ehj->etj', h, gate_up_proj) + gate_up_proj_bias[:, None, :]
        gate = gate_up[..., ::2]
        up = gate_up[..., 1::2]
        gate = jnp.minimum(gate, LIMIT)
        up = jnp.clip(up, -LIMIT, LIMIT)
        glu = gate * jax.nn.sigmoid(gate * ALPHA)
        act = (up + 1.0) * glu
        expert_out = jnp.einsum('eti,eih->eth', act, down_proj) + down_proj_bias[:, None, :]
        out = jnp.einsum('te,eth->th', scores, expert_out)
        return out.reshape(bsz, seq_len, hidden)

    def _L1_attn_ref(x, gamma, w_qkv, w_out):
        import jax, jax.numpy as jnp
        import numpy as np
        B, N, DIM = (2, 512, 512)
        HEADS, DIM_HEAD, GQA = (16, 64, 4)
        KV_HEADS = HEADS // GQA
        DIM_INNER = HEADS * DIM_HEAD
        KV_INNER = KV_HEADS * DIM_HEAD
        THETA = 10000.0

        def _rotate_half(t):
            t1, t2 = jnp.split(t, 2, axis=-1)
            return jnp.concatenate([-t2, t1], axis=-1)
        b, n, _ = x.shape
        norm = jnp.linalg.norm(x, axis=-1, keepdims=True)
        x_n = x / jnp.maximum(norm, 1e-12) * DIM ** 0.5 * gamma
        qkv = (x_n @ w_qkv).reshape(b, n, HEADS + 2 * KV_HEADS, DIM_HEAD)
        q = qkv[..., :HEADS, :]
        k = qkv[..., HEADS:HEADS + KV_HEADS, :]
        v = qkv[..., HEADS + KV_HEADS:, :]
        pos = jnp.arange(n, dtype=jnp.float32)
        inv_freq = THETA ** (-(jnp.arange(0, DIM_HEAD, 2, dtype=jnp.float32) / DIM_HEAD))
        freqs = pos[:, None] * inv_freq[None, :]
        rot = jnp.concatenate([freqs, freqs], axis=-1)[:, None, :]
        cos, sin = (jnp.cos(rot), jnp.sin(rot))
        q = q * cos + _rotate_half(q) * sin
        k = k * cos + _rotate_half(k) * sin
        k = jnp.tile(k, (1, 1, GQA, 1))
        v = jnp.tile(v, (1, 1, GQA, 1))
        q = q * DIM_HEAD ** (-0.5)
        sim = jnp.einsum('bihd,bjhd->bhij', q, k)
        causal_mask = jnp.triu(jnp.ones((n, n), dtype=bool), 1)
        sim = jnp.where(causal_mask, -jnp.finfo(sim.dtype).max, sim)
        attn = jax.nn.softmax(sim, axis=-1)
        out = jnp.einsum('bhij,bjhd->bihd', attn, v)
        out = out.reshape(b, n, DIM_INNER)
        return out @ w_out

    def _L1_xattn_ref(x, context, q_w, q_b, k_w, k_b, v_w, v_b, k_img_w, k_img_b, v_img_w, v_img_b, o_w, o_b, norm_q_w, norm_k_w, norm_k_img_w):
        import jax, jax.numpy as jnp
        import numpy as np
        DIM = 512
        NH = 16
        HD = DIM // NH
        EPS = 1e-06
        IMG_LEN = 257

        def rms_norm(x, w, eps=EPS):
            xf = x.astype(jnp.float32)
            y = xf * jax.lax.rsqrt(jnp.mean(xf * xf, axis=-1, keepdims=True) + eps)
            return y.astype(x.dtype) * w

        def linear(x, w, b):
            return jnp.einsum('blc,oc->blo', x, w) + b

        def attention(q, k, v):
            scale = 1.0 / jnp.sqrt(jnp.asarray(HD, q.dtype))
            scores = jnp.einsum('bqhd,bkhd->bhqk', q, k) * scale
            probs = jax.nn.softmax(scores, axis=-1)
            return jnp.einsum('bhqk,bkhd->bqhd', probs, v)
        B, L, _ = x.shape
        ctx_img = context[:, :IMG_LEN]
        ctx_txt = context[:, IMG_LEN:]
        q = rms_norm(linear(x, q_w, q_b), norm_q_w).reshape(B, L, NH, HD)
        k = rms_norm(linear(ctx_txt, k_w, k_b), norm_k_w).reshape(B, -1, NH, HD)
        v = linear(ctx_txt, v_w, v_b).reshape(B, -1, NH, HD)
        k_img = rms_norm(linear(ctx_img, k_img_w, k_img_b), norm_k_img_w).reshape(B, -1, NH, HD)
        v_img = linear(ctx_img, v_img_w, v_img_b).reshape(B, -1, NH, HD)
        img_x = attention(q, k_img, v_img)
        txt_x = attention(q, k, v)
        out = (txt_x + img_x).reshape(B, L, DIM)
        return linear(out, o_w, o_b)

    def _L1_ffn_ref(x, gate_w, w1, w2, w3, ws1, ws2, ws3):
        import jax, jax.numpy as jnp
        import numpy as np
        TOP_K = 2
        NUM_EXPERTS = 8
        ROUTE_SCALE = 1.0
        bs, slen, dim = x.shape
        xf = x.reshape(-1, dim)
        logits = (xf @ gate_w.T).astype(jnp.float32)
        scores = jax.nn.sigmoid(logits)
        top_scores, sel_idx = jax.lax.top_k(scores, TOP_K)
        top_scores = top_scores * ROUTE_SCALE
        routed = jnp.zeros_like(xf)
        for k in range(TOP_K):
            xs = xf * top_scores[:, k][:, None]
            h1 = jnp.einsum('td,ehd->teh', xs, w1)
            h3 = jnp.einsum('td,ehd->teh', xs, w3)
            h = jax.nn.silu(h1) * h3
            onehot = jax.nn.one_hot(sel_idx[:, k], NUM_EXPERTS, dtype=h.dtype)
            routed = routed + jnp.einsum('teh,te,edh->td', h, onehot, w2)
        shared = jax.nn.silu(xf @ ws1.T) * (xf @ ws3.T) @ ws2.T
        out = (shared + routed).reshape(bs, slen, dim)
        return out
    x = x + _L0_attn_ref(_layernorm(x, axis=-1), L0_attn_wq, L0_attn_wk, L0_attn_wv, L0_attn_wo)
    x = x + _L0_xattn_ref(_layernorm(x, axis=-1), ctx_2048, L0_xattn_Wq, L0_xattn_Wg, L0_xattn_bg, L0_xattn_Wkv, L0_xattn_Wo)
    x = x + _L0_ffn_ref(_layernorm(x, axis=-1), L0_ffn_router_weight, L0_ffn_router_bias, L0_ffn_gate_up_proj, L0_ffn_gate_up_proj_bias, L0_ffn_down_proj, L0_ffn_down_proj_bias)
    x = x + _L1_attn_ref(_layernorm(x, axis=-1), L1_attn_gamma, L1_attn_w_qkv, L1_attn_w_out)
    x = x + _L1_xattn_ref(_layernorm(x, axis=-1), ctx_2048, L1_xattn_q_w, L1_xattn_q_b, L1_xattn_k_w, L1_xattn_k_b, L1_xattn_v_w, L1_xattn_v_b, L1_xattn_k_img_w, L1_xattn_k_img_b, L1_xattn_v_img_w, L1_xattn_v_img_b, L1_xattn_o_w, L1_xattn_o_b, L1_xattn_norm_q_w, L1_xattn_norm_k_w, L1_xattn_norm_k_img_w)
    x = x + _L1_ffn_ref(_layernorm(x, axis=-1), L1_ffn_gate_w, L1_ffn_w1, L1_ffn_w2, L1_ffn_w3, L1_ffn_ws1, L1_ffn_ws2, L1_ffn_ws3)
    return x

_drawn_inputs = setup_inputs


def setup_inputs(seed=0):
    import zlib

    import numpy as np

    out = dict(_drawn_inputs(seed))
    spreads = {'L0_xattn_bg': (1.0, 0.6),
     'L1_attn_gamma': (1.0, 0.2),
     'L1_xattn_q_b': (0.0, 0.738),
     'L1_xattn_k_b': (0.0, 0.8),
     'L1_xattn_v_b': (0.0, 0.1),
     'L1_xattn_k_img_b': (0.0, 0.8),
     'L1_xattn_v_img_b': (0.0, 0.1),
     'L1_xattn_o_b': (0.0, 0.1),
     'L1_xattn_norm_q_w': (1.0, 0.6),
     'L1_xattn_norm_k_w': (1.0, 0.6),
     'L1_xattn_norm_k_img_w': (1.0, 0.6)}
    factors = {'L0_xattn_Wq': 4.633,
     'L0_ffn_router_bias': 4.146,
     'L0_ffn_gate_up_proj_bias': 8.0,
     'L0_ffn_down_proj_bias': 4.052,
     'L1_ffn_gate_w': 3.756,
     'L1_ffn_w1': 3.533,
     'L1_ffn_w2': 3.449,
     'L1_ffn_w3': 3.447,
     'L1_ffn_ws1': 3.511,
     'L1_ffn_ws2': 3.38,
     'L1_ffn_ws3': 3.446}
    for name, (base, spread) in spreads.items():
        noise = np.random.default_rng([zlib.crc32(name.encode()), seed]).standard_normal(out[name].shape)
        drawn = base * np.exp(spread * noise) if base else spread * noise
        out[name] = jnp.asarray(drawn.astype(out[name].dtype))
    for name, factor in factors.items():
        out[name] = (out[name] * factor).astype(out[name].dtype)
    return out
```

```python
from contextlib import ExitStack

import numpy as np

import concourse.bass as bass
from concourse import mybir

P = 128
F32, F32R, BF16, U32 = mybir.dt.float32, mybir.dt.float32r, mybir.dt.bfloat16, mybir.dt.uint32
ALU, ACT, AX = mybir.AluOpType, mybir.ActivationFunctionType, mybir.AxisListType

B, S, D = 2, 512, 512
NT = B * S // P
TB = NT // B
KB = D // P
SC = 1024
NC = SC // P
NH = 16
NE = 8
IMG = 257
MASKED = -1e30
SLOTS = 3
ALLB, LOW, MID = (0, 1, 2, 3, 4, 5, 6, 7), (0, 1), (2, 3)

CHUNKS = ["A0q", "A0k", "A0v", "A0o", "X0k", "X0v", "X0q", "X0g", "X0o", "F0r"]
CHUNKS += [f"F0{w}{e}" for e in range(NE) for w in "gud"]
CHUNKS += ["A1q0", "A1q1", "A1kv", "A1o0", "A1o1"]
CHUNKS += ["X1ki", "X1vi", "X1k", "X1v", "X1q", "X1o", "F1r", "F1h0"]
for _e in range(NE):
    CHUNKS += [f"F1h{_e + 1}", f"F1d{_e}"]
CHUNKS += [f"F1d{NE}"]
CI = {n: i for i, n in enumerate(CHUNKS)}

COL = dict(gb=0, ub=32, gam=64, wq=68, wk=72, wki=76, img=80, txt=81, rb=82, half=83, mhalf=84,
           mone=85, hm=88, iota=92, ub1=100)


def blocks_of(chunk):
    return 2 if chunk.startswith("F1d") else KB


class Counts:

    def __init__(self, noted=None):
        self.noted, self.now, self.at = noted, {}, {}

    def mark(self, name, key, by):
        self.now[name] = self.now.get(name, 0) + by
        self.at[(name, key)] = self.now[name]

    def place(self, name, key, value):
        assert (name, key) not in self.at, (name, key)
        self.at[(name, key)] = value

    def value(self, name, key):
        return 1 if self.noted is None else self.noted[(name, key)]


def decoder(nc, a, out, counts, upto=6):
    with ExitStack() as ctx:
        def sbuf(name, shape, dtype=F32):
            return ctx.enter_context(nc.sbuf_tensor(name, shape, dtype))

        sems = {}

        def sem(name):
            if name not in sems:
                sems[name] = ctx.enter_context(nc.semaphore(name))
            return sems[name]

        X = sbuf("X", [P, NT, D])
        XT = sbuf("XT", [P, 2, KB, B * S], F32R)
        WR = sbuf("WR", [P, SLOTS, 2, KB, 512], F32R)
        RAW = sbuf("RAW", [P, KB, 512])
        QS = sbuf("QS", [P, 8, 512], F32R)
        KS = sbuf("KS", [P, 8, 1024], F32R)
        SRC = sbuf("SRC", [P, 4, 2, 512], F32R)
        PB = sbuf("PB", [P, 8, 512])
        VB = sbuf("VB", [P, 2, 1152])
        XN = sbuf("XN", [P, 2, 512])
        NB = sbuf("NB", [P, 2, 512])
        MR = sbuf("MR", [P, 512])
        ident = sbuf("ident", [P, P])
        identb = sbuf("identb", [P, P], BF16)
        mask_qk = sbuf("mask_qk", [P, P], BF16)
        mask_kq = sbuf("mask_kq", [P, P], BF16)
        ones = sbuf("ones", [P, 64])
        onesm = sbuf("onesm", [P, 2, 32])
        small = sbuf("small", [P, 160])
        mv = sbuf("mv", [P, NT, 2])
        st6 = sbuf("st6", [P, NT, 6])
        rs = sbuf("rs", [P, 4, NT])
        ss = sbuf("ss", [P, 4])
        nmx = sbuf("nmx", [P, 4, 4, 2, 3])
        MS = sbuf("MS", [P, 4, 4, 8], F32R)
        KI = sbuf("KI", [P, B, 2, 4], F32R)
        LG = sbuf("LG", [P, NT, 8])
        i8 = sbuf("i8", [P, NT, 8], U32)
        tw = sbuf("tw", [P, 3, NT])
        SCR = sbuf("SCR", [P, NT, 16])
        PS = [ctx.enter_context(nc.psum_tensor(f"bank{i}", [P, 512], F32)) for i in range(8)]

        def flat(t):
            return t.rearrange("p a n -> p (a n)")

        EV = [XN[:, 0, :], XN[:, 1, :], NB[:, 0, :], NB[:, 1, :]]
        Q2 = KS[:, 4:8, :].rearrange("p a (c n) -> p (a c) n", n=512)
        K1 = [KS[:, 0:4, :], SRC[:, :, :, :].rearrange("p a c n -> p a (c n)")]
        AG = QS[:, :, :].rearrange("p (h g) n -> p h g n", h=2)
        AH = KS[:, :, :].rearrange("p (b h c) n -> p b h (c n)", b=2, h=2)
        VX = VB.rearrange("p a n -> p (a n)")[:, 0:1040].rearrange("p (s g n) -> p s g n", s=2, g=4)
        BD = VB.rearrange("p a n -> p (a n)")[:, 1040:2096].rearrange("p (b g n) -> p b g n", b=2, g=4)

        def cs(name, i=0, n=1):
            return small[:, COL[name] + i:COL[name] + i + n]

        def dram(name, shape):
            return nc.dram_tensor(name, shape, F32, kind="Internal").ap()

        QD = {0: dram("q0_hl", (B, 2, 512, 512)), 1: dram("q1_hl", (B, 2, 1024, 512)), 2: dram("q2_hl", (B, 2, 512, 512))}
        KD = {0: dram("k0_hl", (B, 2, 512, 512)), 1: dram("k1_hl", (B, 2, 256, 512)), 2: dram("k2_hl", (B, 2, 512, 1024))}
        VD = {0: dram("v0_d", (B, 4, P, 512)), 1: dram("v1_d", (B, 4, P, 256)), 2: dram("v2_d", (B, 9, P, 512))}

        def mark(name, key, by=1):
            counts.mark(name, key, by)
            return sem(name), by

        def when(name, key):
            return sem(name), counts.value(name, key)

        bank_of, turns, opened, freed_keys = {}, {}, {}, set()

        def next_bank(key, ring):
            b = ring[turns.get(ring, 0) % len(ring)]
            turns[ring] = turns.get(ring, 0) + 1
            bank_of[key] = b
            opened[b] = opened.get(b, 0) + 1
            counts.place(f"freed{b}", key, opened[b])
            return sem(f"freed{b}"), opened[b] - 1

        def bank(key):
            return PS[bank_of[key]]

        def fills(key):
            return mark(f"filled{bank_of[key]}", key)

        def filled(key):
            return when(f"filled{bank_of[key]}", key)

        def frees(key):
            assert key not in freed_keys
            freed_keys.add(key)
            return sem(f"freed{bank_of[key]}"), 1

        def freed(key):
            return when(f"freed{bank_of[key]}", key)

        last_use = {}

        def w(chunk, lo=0, hi=512):
            return lambda hl, kb: WR[:, CI[chunk] % SLOTS, hl, kb, lo:hi]

        def load_chunk(sp, chunk):
            c, n = CI[chunk], blocks_of(chunk)
            if c:
                sp.wait_ge(*when("w_hi", CHUNKS[c - 1]))
                sp.wait_ge(*when("w_lo", CHUNKS[c - 1]))
            sp.dma_start(RAW[:, 0:n, :], a["weights"][c, :, 0:n * 512].rearrange("p (k n) -> p k n", k=n)).then_inc(
                *mark("raw", chunk, 16))

        def scaled(chunk):
            return chunk in ("A1q0", "A1q1", "A1kv")

        def split_hi(v, chunk):
            c, n = CI[chunk], blocks_of(chunk)
            v.wait_ge(*when("raw", chunk))
            if c >= SLOTS:
                v.wait_ge(*filled(last_use[CHUNKS[c - SLOTS]]))
            dst = WR[:, c % SLOTS, 0, 0:n, :]
            if scaled(chunk):
                for kb in range(n):
                    ins = v.tensor_scalar(dst[:, kb, :], RAW[:, kb, :], cs("gam", kb), None, ALU.mult)
            else:
                ins = v.tensor_copy(dst, RAW[:, 0:n, :])
            ins.then_inc(*mark("w_hi", chunk))
            if scaled(chunk):
                split_lo(v, chunk)

        def split_lo(eng, chunk):
            c, n = CI[chunk], blocks_of(chunk)
            eng.wait_ge(*when("w_hi", chunk))
            dst, hi = WR[:, c % SLOTS, 1, 0:n, :], WR[:, c % SLOTS, 0, 0:n, :].bitcast(F32)
            if scaled(chunk):
                for kb in range(n):
                    ins = eng.scalar_tensor_tensor(out=dst[:, kb, :], in0=RAW[:, kb, :], scalar=cs("gam", kb),
                                                   in1=hi[:, kb, :], op0=ALU.mult, op1=ALU.subtract)
            else:
                ins = eng.tensor_tensor(dst, RAW[:, 0:n, :], hi, ALU.subtract)
            ins.then_inc(sem("w_lo"), 1)
            counts.place("w_lo", chunk, c + 1)

        def split_lo_pool(pool, chunk):
            if not scaled(chunk):
                split_lo(pool, chunk)

        def product(pe, dst, lhs, rhs, blocks=KB, first=True, last=True):
            for kb in range(blocks):
                for n, (l, r) in enumerate(((0, 0), (0, 1), (1, 0))):
                    ins = pe.matmul(dst, lhs(l, kb), rhs(r, kb), start=first and kb == 0 and n == 0,
                                    stop=last and kb == blocks - 1 and n == 2)
            return ins

        def xt(b):
            return lambda hl, kb: XT[:, hl, kb, b * S:(b + 1) * S]

        def xtile(t):
            return lambda hl, kb: XT[:, hl, kb, t * P:(t + 1) * P]

        def grid(ps):
            return ps[:, :].rearrange("p (g n) -> p g n", g=KB)

        STAGES = ["A0", "X0", "F0", "A1", "X1", "F1"][:upto]
        before = dict(zip(STAGES[1:], STAGES))
        tiles = lambda b: range(b * TB, (b + 1) * TB)
        xt_last = {}

        def ln_pe(pe, s, b):
            for t in tiles(b):
                pe.wait_ge(*when("xn", (s, t)))
                pe.wait_ge(*next_bank((s, "T", t), ALLB))
                ps = bank((s, "T", t))
                for g in range(KB):
                    ins = pe.transpose(ps[:, g * P:(g + 1) * P], XN[:, t % 2, g * P:(g + 1) * P], ident[:])
                ins.then_inc(*fills((s, "T", t)))

        def ln_act(act, s, b):
            if s in before:
                act.wait_ge(*filled(xt_last[(before[s], b)]))
            for t in tiles(b):
                act.wait_ge(*filled((s, "T", t)))
                ps = bank((s, "T", t))
                act.activation(XT[:, 0, :, t * P:(t + 1) * P], grid(ps), ACT.Copy).then_inc(*mark("hi", (s, "T", t)))

        x_key = {t: (f"x_in{t}", t) for t in range(NT)}

        def ln_dve(v, s, b):
            for t in tiles(b):
                v.wait_ge(*when(*x_key[t]))
                v.bn_stats(st6[:, t, :], X[:, t, :]).then_inc(*mark("bn", (s, t)))
            for t in tiles(b):
                v.wait_ge(*when("bn", (s, t)))
                v.bn_aggr(mv[:, t, :], st6[:, t, :]).then_inc(*mark("mv", (s, t)))

            def lo(t):
                v.wait_ge(*when("hi", (s, "T", t)))
                v.wait_ge(*filled((s, "T", t)))
                ps = bank((s, "T", t))
                v.tensor_tensor(XT[:, 1, :, t * P:(t + 1) * P], grid(ps),
                                      XT[:, 0, :, t * P:(t + 1) * P].bitcast(F32), ALU.subtract).then_inc(
                                          *frees((s, "T", t)))

            for t in tiles(b):
                v.wait_ge(*when("rs", (s, b)))
                v.wait_ge(*when("mv", (s, t)))
                if t >= 2:
                    v.wait_ge(*filled((s, "T", t - 2)))
                elif s == "X1":
                    v.wait_ge(*filled(("X1", "nT", len(JOBS) - 2 + t)))
                v.tensor_scalar(XN[:, t % 2, :], X[:, t, :], mv[:, t, 0:1], rs[:, 0, t:t + 1],
                                       ALU.subtract, ALU.mult).then_inc(*mark("xn", (s, t)))
                if t % TB:
                    lo(t - 1)
            lo((b + 1) * TB - 1)

        def ln_pool(pool, s, b):
            tt = slice(b * TB, (b + 1) * TB)
            pool.wait_ge(*when("mv", (s, (b + 1) * TB - 1)))
            var = mv[:, tt, 1]
            half, mhalf, mone = (cs(n).broadcast_to([P, TB]) for n in ("half", "mhalf", "mone"))

            def link(n, ins):
                ins.then_inc(*mark("rs_step", (s, b, n)))
                pool.wait_ge(*when("rs_step", (s, b, n)))

            link(0, pool.tensor_scalar(rs[:, 1, tt], var, 1e-5, None, ALU.add))
            if s != "A1":
                pool.tensor_tensor(rs[:, 0, tt], rs[:, 1, tt], mhalf, ALU.pow).then_inc(*mark("rs", (s, b)))
                return
            link(1, pool.tensor_tensor(rs[:, 0, tt], rs[:, 1, tt], mhalf, ALU.pow))
            link(2, pool.tensor_scalar(rs[:, 2, tt], var, float(D), None, ALU.mult))
            link(3, pool.tensor_tensor(rs[:, 3, tt], rs[:, 2, tt], half, ALU.pow))
            link(4, pool.tensor_tensor(rs[:, 2, tt], rs[:, 3, tt], rs[:, 0, tt], ALU.mult))
            link(5, pool.tensor_scalar(rs[:, 3, tt], rs[:, 2, tt], 1e-12, None, ALU.max))
            link(6, pool.tensor_tensor(rs[:, 2, tt], rs[:, 3, tt], mone, ALU.pow))
            link(7, pool.tensor_tensor(rs[:, 3, tt], rs[:, 2, tt], rs[:, 0, tt], ALU.mult))
            pool.tensor_scalar(rs[:, 0, tt], rs[:, 3, tt], float(D) ** 0.5, None, ALU.mult).then_inc(
                *mark("rs", (s, b)))

        def ln_ready(pe, s, b):
            for t in tiles(b):
                pe.wait_ge(*freed((s, "T", t)))

        def add_to_x(v, t, key, scale=None):
            v.wait_ge(*filled(key))
            ps = bank(key)
            v.wait_ge(*when(*x_key[t]))
            if scale is None:
                ins = v.tensor_tensor(X[:, t, :], ps[:, :], X[:, t, :], ALU.add)
            else:
                ins = v.scalar_tensor_tensor(out=X[:, t, :], in0=ps[:, :], scalar=scale, in1=X[:, t, :],
                                             op0=ALU.mult, op1=ALU.add)
            ins.then_inc(*frees(key))
            x_key[t] = (f"freed{bank_of[key]}", key)

        NX = B * NH // 2
        CFG = {0: dict(st="A0", nk=512, scale=32 ** -0.5, o=["A0o"]),
               1: dict(st="A1", nk=512, scale=64 ** -0.5, o=["A1o0", "A1o1"]),
               2: dict(st="X1", nk=1024, scale=32 ** -0.5, o=["X1o"])}

        def steps(at):
            return [(kt, jj) for kt in range(CFG[at]["nk"] // P) for jj in range(2)]

        def max_products(at):
            return [(i, jj, h) for i in range(4) for jj in range(2) for h in range(2 if at == 2 else 1)]

        def group(at, x):
            return x if at == 1 else x // 2

        def group_end(at, x):
            return at == 1 or x % 2 == 1

        def slot(x, jj):
            return x % 4 * 2 + jj

        def kslot(at, x, jj):
            return (K1[x // 8], (2 * x + jj) % 4) if at == 1 else (KS, slot(x, jj))

        def pb_slot(at, x, n):
            return (x * len(steps(at)) + n) % 8

        def at_pe_max(pe, at, x, prods):
            st = CFG[at]["st"]
            for i, jj, h in prods:
                if (i, jj, h) == (0, 0, 0):
                    pe.wait_ge(*when(f"stack{x % 4}", (at, x)))
                    if at == 1 and x % 8 == 0:
                        pe.wait_ge(*when(f"kstack{x // 8}", (at, x // 8)))
                key = (st, "max", x, i, jj, h)
                pe.wait_ge(*next_bank(key, LOW))
                ps = bank(key)
                kt_, ki = kslot(at, x, jj)
                n0, n = (h * 512, 512) if at == 2 else (0, (i + 1) * P)
                q = slice(i * P, (i + 1) * P)
                if at == 1:
                    pe.matmul(ps[:, 0:n], QS[:, slot(x, jj), q], kt_[:, ki, 0:n], start=True, stop=False)
                    ins = pe.matmul(ps[:, 0:n], Q2[0:64, slot(x, jj), q], kt_[0:64, ki, 512:512 + n], start=False, stop=False)
                else:
                    ins = pe.matmul(ps[:, 0:n], QS[0:96, slot(x, jj), q], kt_[0:96, ki, n0:n0 + n], start=True, stop=at == 2)
                if at != 2:
                    ins = pe.matmul(ps[:, i * P:n], identb[:], mask_qk[:], start=False, stop=True)
                ins.then_inc(*fills(key))

        def at_pe_turn(pe, at, x):
            key = (CFG[at]["st"], "mt", x)
            pe.wait_ge(*when("ms", (at, x)))
            n = 8 if at == 2 else 4
            pe.wait_ge(*next_bank(key, LOW))
            ps = bank(key)
            for i in range(4):
                ins = pe.transpose(ps[0:n, i * P:(i + 1) * P], MS[:, x % 4, i, 0:n].bitcast(F32), ident[:])
            ins.then_inc(*fills(key))

        def at_pe_scores(pe, at, x, n):
            st, (kt, jj) = CFG[at]["st"], steps(at)[n]
            if n == 0:
                pe.wait_ge(*when(f"mrow{x % 4}", (at, x)))
            key = (st, "s", x, n)
            pe.wait_ge(*next_bank(key, MID))
            ps = bank(key)
            c0 = 0 if at == 2 else kt * P
            kt_, ki = kslot(at, x, jj)
            k, q = slice(kt * P, (kt + 1) * P), slice(c0, 512)
            if at == 1:
                pe.matmul(ps[:, q], kt_[:, ki, k], QS[:, slot(x, jj), q], start=True, stop=False)
                ins = pe.matmul(ps[:, q], kt_[0:66, ki, 512 + kt * P:512 + (kt + 1) * P], Q2[0:66, slot(x, jj), q],
                                start=False, stop=False)
            else:
                rows = 100 if at == 2 else 98
                ins = pe.matmul(ps[:, q], kt_[0:rows, ki, k], QS[0:rows, slot(x, jj), q], start=True, stop=at == 2)
            if at != 2:
                ins = pe.matmul(ps[:, c0:c0 + P], identb[:], mask_kq[:], start=False, stop=True)
            ins.then_inc(*fills(key))

        acc = {}

        def at_pe_values(pe, at, x, n):
            st, (kt, jj) = CFG[at]["st"], steps(at)[n]
            gx, last_kt = group(at, x), CFG[at]["nk"] // P - 1
            if n == 0 and (at == 1 or x % 2 == 0):
                if at == 1:
                    if x % 8 == 0:
                        pe.wait_ge(*when(f"vb{x // 8}", (at, x // 8)))
                else:
                    pe.wait_ge(*when(f"vb{gx % 2}", (at, gx)))
                names = [("o", (4,)), ("l", (5,)), ("o2", (6,)), ("l2", (7,))] if at == 2 else [("o", (4, 6)), ("l", (5, 7))]
                for name, ring in names:
                    pe.wait_ge(*next_bank((st, name, gx), ring))
                    acc[name] = bank((st, name, gx))
            pe.wait_ge(*freed((st, "s", x, n)))
            c0 = 0 if at == 2 else kt * P
            prob = PB[:, pb_slot(at, x, n), c0:512]
            width = 64 if at == 1 else 32
            r0 = 64 * jj if at == 1 else 32 * ((2 * x + jj) % 4)
            if at == 2:
                parts = [("", kt, kt == 0, False, ones[:, 0:32])] if kt < 2 else \
                    [("2", kt + 1, False, kt == last_kt, ones[:, 0:32])] if kt > 2 else \
                    [("", 2, False, True, onesm[:, 0, :]), ("2", 3, True, False, onesm[:, 1, :])]
            else:
                parts = [("", kt, kt == 0, kt == last_kt, ones[:, 0:width])]
            for suffix, vt, first, last, one in parts:
                if at == 1:
                    v = VB[:, x // 8, vt * 256 + (2 * x + jj) % 4 * 64:vt * 256 + (2 * x + jj) % 4 * 64 + 64]
                else:
                    v = VB[:, gx % 2, vt * P + r0:vt * P + r0 + 32]
                pe.matmul(acc["o" + suffix][r0:r0 + width, c0:512], v, prob, start=first, stop=last)
                ins = pe.matmul(acc["l" + suffix][r0:r0 + width, c0:512], one, prob, start=first, stop=last)
            ins.then_inc(*mark("pv", (at, x, n)))

        def at_out(at, b):
            return [(CFG[at]["st"], "y", t, part) for part in range(len(CFG[at]["o"])) for t in tiles(b)]

        def at_pe_out(pe, at, b):
            chunks = CFG[at]["o"]
            pe.wait_ge(*when("att_lo", (at, NX // 2 * (b + 1) - 1 if at == 1 else NX // 4 * (b + 1) - 1)))
            for key in at_out(at, b):
                _, _, t, part = key
                pe.wait_ge(*when("w_hi", chunks[part]))
                pe.wait_ge(*when("w_lo", chunks[part]))
                pe.wait_ge(*next_bank(key, LOW))
                ps = bank(key)
                half = t % TB * P + (part if at == 1 else b) * S
                product(pe, ps[:, :], lambda hl, kb: XT[:, hl, kb, half:half + P], w(chunks[part])).then_inc(
                    *fills(key))
                last_use[chunks[part]] = key
                xt_last[(CFG[at]["st"], b)] = key
            if at == 1:
                xt_last[("A1", 0)] = key

        def at_pe(pe, at):
            N, M = len(steps(at)), len(max_products(at))
            for x in range(-2, NX + 1):
                prods = max_products(at) if x + 2 < NX else []
                if 0 <= x < NX:
                    for n in range(N):
                        at_pe_scores(pe, at, x, n)
                        if n >= 2:
                            at_pe_values(pe, at, x, n - 2)
                        at_pe_max(pe, at, x + 2, prods[n * M // N:(n + 1) * M // N])
                        if n == 3 and x + 1 < NX:
                            at_pe_turn(pe, at, x + 1)
                    at_pe_values(pe, at, x, N - 2)
                    at_pe_values(pe, at, x, N - 1)
                else:
                    at_pe_max(pe, at, x + 2, prods)
                    if x == -1:
                        at_pe_turn(pe, at, 0)
                if x > 0 and x % 8 == 0:
                    at_pe_out(pe, at, x // 8 - 1)

        def at_dve_max(v, at, x, prods):
            for i, jj, h in prods:
                key = (CFG[at]["st"], "max", x, i, jj, h)
                v.wait_ge(*filled(key))
                ps = bank(key)
                cut = [(0, IMG, 0), (IMG, 512, 1)] if at == 2 and h == 0 else [(0, 512, 2)] if at == 2 else [(0, (i + 1) * P, 0)]
                for lo, hi, c in cut:
                    ins = v.tensor_reduce(nmx[:, x % 4, i, jj, c:c + 1], ps[:, lo:hi], AX.X, ALU.max)
                ins.then_inc(*frees(key))

        def at_dve_minus(v, at, x):
            slot_ = x % 4
            for jj in range(2):
                for h in range(2 if at == 2 else 1):
                    v.wait_ge(*freed((CFG[at]["st"], "max", x, 3, jj, h)))
            kinds = 1
            if at == 2:
                kinds = 2
                v.tensor_tensor(nmx[:, slot_, :, :, 1], nmx[:, slot_, :, :, 1], nmx[:, slot_, :, :, 2], ALU.max).then_inc(
                    *mark("nmax", (at, x)))
                v.wait_ge(*when("nmax", (at, x)))
            for k in range(kinds):
                ins = v.tensor_scalar(MS[:, slot_, :, 4 * k:4 * k + 2], nmx[:, slot_, :, :, k], -1.0, None, ALU.mult)
            ins.then_inc(*mark("ms_hi", (at, x)))
            v.wait_ge(*when("ms_hi", (at, x)))
            for k in range(kinds):
                ins = v.scalar_tensor_tensor(out=MS[:, slot_, :, 4 * k + 2:4 * k + 4], in0=nmx[:, slot_, :, :, k], scalar=-1.0,
                                             in1=MS[:, slot_, :, 4 * k:4 * k + 2].bitcast(F32), op0=ALU.mult, op1=ALU.subtract)
            ins.then_inc(*mark("ms", (at, x)))

        def ev(at, gx):
            return [(EV[0], EV[1]), (EV[2], EV[3])] if at == 2 else [(EV[gx % 2 * 2], EV[gx % 2 * 2 + 1])]

        def at_dve_norm(v, at, gx):
            for n, (_, l) in enumerate(ev(at, gx)):
                v.wait_ge(*freed((CFG[at]["st"], "l" + "2" * n, gx)))
                v.reciprocal(l, l).then_inc(*mark("rcp", (at, gx, n)))

        def at_pool_norm(pool, at, gx):
            pairs = ev(at, gx)
            for n, (o, l) in enumerate(pairs):
                pool.wait_ge(*when("rcp", (at, gx, n)))
                pool.wait_ge(*freed((CFG[at]["st"], "o" + "2" * n, gx)))
                pool.tensor_tensor(o, o, l, ALU.mult).then_inc(
                    *mark("att" if len(pairs) == 1 else "att_part", (at, gx, n)))
            if at == 2:
                pool.wait_ge(*when("att_part", (at, gx, 1)))
                pool.tensor_tensor(pairs[0][0], pairs[0][0], pairs[1][0], ALU.add).then_inc(*mark("att", (at, gx, 0)))
            pool.wait_ge(*when("hi", (at, "att", gx)))
            pool.tensor_tensor(at_dst(at, gx, 1), pairs[0][0], at_dst(at, gx, 0).bitcast(F32), ALU.subtract).then_inc(
                *mark("att_lo", (at, gx)))

        def at_dst(at, gx, hl):
            if at == 1:
                g = gx % 8
                return XT[:, hl, g % 4, g // 4 * S:(g // 4 + 1) * S]
            return XT[:, hl, gx % 4, gx // 4 * S:(gx // 4 + 1) * S]

        def at_act_hi(act, at, gx):
            act.wait_ge(*when("att", (at, gx, 0)))
            if gx == 0:
                for b in range(B):
                    act.wait_ge(*filled(proj_last[(at, b)]))
            if at == 1 and gx == 8:
                act.wait_ge(*filled(at_out(at, 0)[-1]))
            act.activation(at_dst(at, gx, 0), ev(at, gx)[0][0], ACT.Copy).then_inc(*mark("hi", (at, "att", gx)))

        proj_last = {}

        def at_act(act, at):
            st, N = CFG[at]["st"], len(steps(at))
            for x in range(-2, NX + 1):
                def turn():
                    key = (st, "mt", x + 1)
                    act.wait_ge(*filled(key))
                    ps = bank(key)
                    if x + 1 > 0:
                        act.wait_ge(*when(f"mrow{x % 4}", (at, x)))
                    n = 8 if at == 2 else 4
                    act.activation(MR[0:n, :], ps[0:n, :], ACT.Copy).then_inc(*frees(key))

                def hi():
                    if x > 0 and group_end(at, x - 1):
                        at_act_hi(act, at, group(at, x - 1))

                if x == -1:
                    turn()
                if 0 <= x < NX:
                    for n in range(N):
                        kt, jj = steps(at)[n]
                        c0 = 0 if at == 2 else kt * P
                        act.wait_ge(*filled((st, "s", x, n)))
                        ps = bank((st, "s", x, n))
                        if x * N + n >= 8:
                            back = x * N + n - 8
                            act.wait_ge(*when("pv", (at, back // N, back % N)))
                        act.activation(PB[:, pb_slot(at, x, n), c0:512], ps[:, c0:512], ACT.Exp,
                                             scale=CFG[at]["scale"]).then_inc(*frees((st, "s", x, n)))
                        if n == 3 and x + 1 < NX:
                            turn()
                        if n == N - 2:
                            hi()
                    if group_end(at, x):
                        gx = group(at, x)
                        back = gx - 1 if at == 2 else gx - 2
                        if back >= 0:
                            act.wait_ge(*when("att_lo", (at, back)))
                        act.wait_ge(*when("pv", (at, x, N - 1)))
                        for k, (o, l) in enumerate(ev(at, gx)):
                            sfx = "" if k == 0 else "2"
                            act.activation(o, bank((st, "o" + sfx, gx))[:, :], ACT.Copy).then_inc(
                                *frees((st, "o" + sfx, gx)))
                            ins = act.activation(l, bank((st, "l" + sfx, gx))[:, :], ACT.Copy)
                            ins.then_inc(*frees((st, "l" + sfx, gx)))
                elif x == NX:
                    hi()

        def at_dve(v, at):
            for x in range(-2, NX + 1):
                prods = max_products(at) if x + 2 < NX else []
                at_dve_max(v, at, x + 2, prods[:len(prods) // 4])
                if x > 0 and group_end(at, x - 1):
                    at_dve_norm(v, at, group(at, x - 1))
                at_dve_max(v, at, x + 2, prods[len(prods) // 4:])
                if prods:
                    at_dve_minus(v, at, x + 2)
                if x > 0 and x % 8 == 0:
                    for key in at_out(at, x // 8 - 1):
                        add_to_x(v, key[2], key)

        def at_pool(pool, at):
            for gx in range(NX if at == 1 else NX // 2):
                at_pool_norm(pool, at, gx)

        def src_order(at):
            if at == 2:
                return []
            return [(T, b, 2 * mp + h) for T, b, mp in rope_pairs(at) for h in range(2)]

        def rope_pairs(at):
            return [(T, b, m // 2) for T, _, ms in PROJ[at] for b in range(B) for m, _ in ms[::2]]

        PROJ = {0: [("q", "A0q", [(m, m * P) for m in range(4)]), ("k", "A0k", [(m, m * P) for m in range(4)])],
                1: [("q", "A1q0", [(m, m * P) for m in range(4)]), ("q", "A1q1", [(m + 4, m * P) for m in range(4)]),
                    ("k", "A1kv", [(m, m * P) for m in range(2)])]}
        VPROJ = {0: ("A0v", 0, 512), 1: ("A1kv", 256, 512)}

        def src_slot(at, T, b, m):
            return src_order(at).index((T, b, m)) % 4

        def wait_stored(eng, at, T, b):
            if T == "v":
                if at == 2:
                    for c, (jb, tt, kind) in enumerate(JOBS):
                        if jb == b:
                            eng.wait_ge(*when(f"v_stored{c % 2}", (2, c)))
                else:
                    for t in tiles(b):
                        eng.wait_ge(*when(f"v_stored{t % 4}", (at, t)))
            elif at == 2:
                for c, (jb, tt, kind) in enumerate(JOBS + QJOBS):
                    if jb == b and (kind == "q") == (T == "q") and (tt, kind) != (2, "i"):
                        eng.wait_ge(*when(f"src_stored{2 + c % 2}", (2, c)))
            else:
                for (T_, b_, m) in src_order(at):
                    if (T_, b_) == (T, b):
                        eng.wait_ge(*when(f"src_stored{src_slot(at, T, b, m)}", (at, T, b, m)))

        def at_sp_stack(sp, at, x):
            b, h0 = x // 8, x % 8 * 2
            if x >= 4:
                sp.wait_ge(*filled((CFG[at]["st"], "s", x - 4, len(steps(at)) - 1)))
            if x % 8 == 0:
                wait_stored(sp, at, "q", b)
                wait_stored(sp, at, "k", b)
            s0, hd = slot(x, 0), 64 if at == 1 else 32

            def heads(t, hl, h, n):
                return t[b, hl, h * hd:(h + n) * hd, :].rearrange("(h r) t -> r h t", h=n)

            if at == 1:
                if x % 8 == 0:
                    for dst, src in [
                        (K1[b][0:64, :, 0:512].bitcast(F32), heads(KD[1], 0, 0, 4)),
                        (K1[b][64:128, :, 0:512].bitcast(F32), heads(KD[1], 1, 0, 4)),
                        (K1[b][0:64, :, 512:1024].bitcast(F32), heads(KD[1], 0, 0, 4))]:
                        sp.dma_start(dst, src).then_inc(*mark(f"kstack{b}", (at, b), 16))
                for dst, src in [
                    (QS[0:64, s0:s0 + 2, :].bitcast(F32), heads(QD[1], 0, h0, 2)),
                    (QS[64:128, s0:s0 + 2, :].bitcast(F32), heads(QD[1], 0, h0, 2)),
                    (Q2[0:64, s0:s0 + 2, :].bitcast(F32), heads(QD[1], 1, h0, 2))]:
                    sp.dma_start(dst, src).then_inc(*mark(f"stack{x % 4}", (at, x), 16))
                return
            nk = CFG[at]["nk"]
            for dst, src in ([(QS[32 * n:32 * n + 32, s0:s0 + 2, :].bitcast(F32), heads(QD[at], hl, h0, 2)) for n, hl in enumerate((0, 0, 1))]
                 + [(KS[32 * n:32 * n + 32, s0:s0 + 2, 0:nk].bitcast(F32), heads(KD[at], hl, h0, 2)) for n, hl in enumerate((0, 1, 0))]):
                sp.dma_start(dst, src).then_inc(*mark(f"stack{x % 4}", (at, x), 16))

        def at_sp_values(sp, at, x):
            b = x // 8
            if at == 1:
                if x % 8 == 0:
                    wait_stored(sp, at, "v", b)
                    sp.dma_start(VB[:, b, 0:1024].rearrange("p (k n) -> p k n", k=4), VD[1][b].rearrange("k p n -> p k n")).then_inc(
                        *mark(f"vb{b}", (at, b), 16))
            elif x % 2 == 0:
                gx = x // 2
                if x % 8 == 0:
                    wait_stored(sp, at, "v", b)
                if gx >= 2:
                    sp.wait_ge(*when("pv", (at, x - 3, len(steps(at)) - 1)))
                nv = 9 if at == 2 else 4
                sp.dma_start(VB[:, gx % 2, 0:nv * P].rearrange("p (k n) -> p k n", k=nv), VD[at][b, :, :, gx % 4 * P:(gx % 4 + 1) * P].rearrange("k p n -> p k n")).then_inc(
                    *mark(f"vb{gx % 2}", (at, gx), 16))

        def at_sp_rows(sp, at, x):
            s0 = slot(x, 0)
            sp.wait_ge(*freed((CFG[at]["st"], "mt", x)))
            dst, r0 = (Q2, 64) if at == 1 else (QS, 96)
            for dst, src in ([(dst[r0 + r:r0 + r + 1, s0:s0 + 2, :].bitcast(F32), MR[2 * r:2 * r + 2, :])
                                               for r in range(4 if at == 2 else 2)]):
                sp.dma_start(dst, src).then_inc(*mark(f"mrow{x % 4}", (at, x), 16))

        def at_sp(sp, at):
            for x in range(-3, NX):
                if x + 3 < NX:
                    at_sp_stack(sp, at, x + 3)
                if 0 <= x + 1 < NX:
                    at_sp_values(sp, at, x + 1)
                    at_sp_rows(sp, at, x + 1)

        def qkv_pe(pe, at):
            st = CFG[at]["st"]
            for T, chunk, ms in PROJ[at]:
                pe.wait_ge(*when("w_hi", chunk))
                pe.wait_ge(*when("w_lo", chunk))
                for b in range(B):
                    ln_ready(pe, st, b)
                    for m, col in ms:
                        key = (st, T, b, m)
                        pe.wait_ge(*next_bank(key, ALLB))
                        ps = bank(key)
                        product(pe, ps[:, :], w(chunk, col, col + P), xt(b)).then_inc(*fills(key))
                        last_use[chunk] = key
            chunk, lo, hi = VPROJ[at]
            pe.wait_ge(*when("w_hi", chunk))
            pe.wait_ge(*when("w_lo", chunk))
            for t in range(NT):
                key = (st, "v", t)
                pe.wait_ge(*next_bank(key, ALLB))
                ps = bank(key)
                product(pe, ps[:, 0:hi - lo], xtile(t), w(chunk, lo, hi)).then_inc(*fills(key))
                last_use[chunk] = key
                proj_last[(at, t // TB)] = key

        def qkv_dve(v, at, chunks_after):
            st = CFG[at]["st"]
            cos, sin = PB[:, 0, :], PB[:, 1, :]
            v.wait_ge(*when("rope_tables", at))
            pairs = rope_pairs(at)

            def lo(n):
                T, b, mp = pairs[n]
                for h in range(2):
                    sl = src_slot(at, T, b, 2 * mp + h)
                    v.wait_ge(*when("hi", (at, T, b, 2 * mp + h)))
                    v.tensor_tensor(SRC[:, sl, 1, :], PB[:, 6 + h, :], SRC[:, sl, 0, :].bitcast(F32), ALU.subtract).then_inc(
                        *mark("src_lo", (at, n, h)))

            for n, (T, b, mp) in enumerate(pairs):
                if n:
                    v.wait_ge(*when("rope_sum", (at, n - 1, 1)))
                for h, (c, s_) in enumerate(((2, 4), (5, 3))):
                    key = (st, T, b, 2 * mp + h)
                    v.wait_ge(*filled(key))
                    ps = bank(key)
                    v.tensor_tensor(PB[:, c, :], ps[:, :], cos, ALU.mult)
                    v.tensor_tensor(PB[:, s_, :], ps[:, :], sin, ALU.mult).then_inc(*frees(key))
                if n:
                    lo(n - 1)
                if n + 1 == len(pairs) or pairs[n + 1][0] != T or (T == "q" and at == 1 and mp == 1 and b == 1):
                    for chunk in chunks_after.pop(0):
                        split_hi(v, chunk)
            lo(len(pairs) - 1)

        def qkv_pool(pool, at, chunks_after):
            st = CFG[at]["st"]
            pairs = rope_pairs(at)
            for n, (T, b, mp) in enumerate(pairs):
                for h in range(2):
                    pool.wait_ge(*freed((st, T, b, 2 * mp + h)))
                if n:
                    pool.wait_ge(*when("src_lo", (at, n - 1, 1)))
                pool.tensor_tensor(PB[:, 6, :], PB[:, 2, :], PB[:, 3, :], ALU.subtract).then_inc(
                    *mark("rope_sum", (at, n, 0)))
                pool.tensor_tensor(PB[:, 7, :], PB[:, 4, :], PB[:, 5, :], ALU.add).then_inc(
                    *mark("rope_sum", (at, n, 1)))
                if n + 1 == len(pairs) or pairs[n + 1][0] != T or (T == "q" and at == 1 and mp == 1 and b == 1):
                    for chunk in chunks_after.pop(0):
                        split_lo_pool(pool, chunk)

        def qkv_act(act, at):
            st, order = CFG[at]["st"], src_order(at)
            for n, (T, b, m) in enumerate(order):
                act.wait_ge(*when("rope_sum", (at, n // 2, n % 2)))
                if n >= 4:
                    act.wait_ge(*when(f"src_stored{n % 4}", (at, *order[n - 4])))
                act.activation(SRC[:, n % 4, 0, :], PB[:, 6 + n % 2, :], ACT.Copy).then_inc(*mark("hi", (at, T, b, m)))
            width = VPROJ[at][2] - VPROJ[at][1]
            for t in range(NT):
                act.wait_ge(*filled((st, "v", t)))
                ps = bank((st, "v", t))
                if t >= 4:
                    act.wait_ge(*when(f"v_stored{t % 4}", (at, t - 4)))
                act.activation(EV[t % 4][:, 0:width], ps[:, 0:width], ACT.Copy).then_inc(*frees((st, "v", t)))

        def qkv_sp(sp, at, loads):
            hd2 = CFG[at]["nk"] // 32 if at == 0 else 32
            for n, (T, b, m) in enumerate(src_order(at)):
                sp.wait_ge(*when("src_lo", (at, n // 2, n % 2)))
                dram_t = (QD if T == "q" else KD)[at]
                heads = P // hd2
                rows = slice(m // 2 * heads * 2 * hd2, (m // 2 + 1) * heads * 2 * hd2)
                dst = lambda hl: dram_t[b, hl, rows, :].rearrange("(h c f) t -> c h f t", h=heads, c=2)[m % 2]
                for dst, src in ([(dst(hl), SRC[:, n % 4, hl, :].bitcast(F32)) for hl in range(2)]):
                    sp.dma_start(dst, src).then_inc(*mark(f"src_stored{n % 4}", (at, T, b, m), 16))
                if n in loads:
                    load_chunk(sp, loads[n])
            width = VPROJ[at][2] - VPROJ[at][1]
            for t in range(NT):
                sp.wait_ge(*freed((CFG[at]["st"], "v", t)))
                sp.dma_start(VD[at][t // TB, t % TB], EV[t % 4][:, 0:width]).then_inc(
                    *mark(f"v_stored{t % 4}", (at, t), 16))

        NCT = B * NC

        def x0_pe(pe):
            ctile = lambda c: (lambda hl, kb: SRC[:, c % 4, hl, kb * P:(kb + 1) * P])
            pe.wait_ge(*when("w_hi", "X0k"))
            pe.wait_ge(*when("w_lo", "X0k"))
            pe.wait_ge(*when("w_hi", "X0v"))
            pe.wait_ge(*when("w_lo", "X0v"))

            def summary(c):
                pe.wait_ge(*freed(("X0", "k", c)))
                pe.wait_ge(*freed(("X0", "v", c)))
                if c % NC == 0:
                    for g in range(KB):
                        pe.wait_ge(*next_bank(("X0", "kv", c // NC, g), (4 + g,)))
                        acc[g] = bank(("X0", "kv", c // NC, g))
                for g in range(KB):
                    ins = pe.matmul(acc[g][:, 0:130], PB[:, 4 + c % 2, g * P:(g + 1) * P], VX[:, c % 2, g, :],
                                    start=c % NC == 0, stop=c % NC == NC - 1)
                ins.then_inc(*mark("kv_step", c))

            for c in range(NCT + 1):
                if c < NCT:
                    pe.wait_ge(*when("ct_lo", ("X0", c)))
                    for T, ring, chunk in (("k", LOW, "X0k"), ("v", MID, "X0v")):
                        key = ("X0", T, c)
                        pe.wait_ge(*next_bank(key, ring))
                        ps = bank(key)
                        product(pe, ps[:, :], ctile(c), w(chunk)).then_inc(*fills(key))
                        last_use[chunk] = key
                if c:
                    summary(c - 1)
            for b in range(B):
                ln_pe(pe, "X0", b)
            for b in range(B):
                ln_ready(pe, "X0", b)
                pe.wait_ge(*when("w_hi", "X0q"))
                pe.wait_ge(*when("w_lo", "X0q"))
                for m in range(KB):
                    key = ("X0", "q", b, m)
                    pe.wait_ge(*next_bank(key, LOW + MID))
                    ps = bank(key)
                    product(pe, ps[:, :], w("X0q", m * P, (m + 1) * P), xt(b)).then_inc(*fills(key))
                    last_use["X0q"] = key
                pe.wait_ge(*when("w_hi", "X0g"))
                pe.wait_ge(*when("w_lo", "X0g"))

                def gate(t):
                    key = ("X0", "g", t)
                    pe.wait_ge(*next_bank(key, LOW + MID))
                    ps = bank(key)
                    product(pe, ps[:, :], xtile(t), w("X0g")).then_inc(*fills(key))
                    last_use["X0g"] = xt_last[("X0", b)] = key

                def attend(t):
                    if t % TB == 0:
                        for g in range(KB):
                            pe.wait_ge(*freed(("X0", "q", b, g)))
                            pe.wait_ge(*freed(("X0", "kv", b, g)))
                    for h in range(2):
                        key = ("X0", "a", t, h)
                        pe.wait_ge(*next_bank(key, (4, 5, 6, 7)))
                        ps = bank(key)
                        for g in range(2):
                            ins = pe.matmul(ps[:, 132 * g:132 * g + 132], PB[:, 4 + 2 * h + g, t % TB * P:(t % TB + 1) * P],
                                            BD[:, b, 2 * h + g, :], start=True, stop=True)
                        ins.then_inc(*fills(key))

                def turn(t):
                    pe.wait_ge(*when("gated", t))
                    key = ("X0", "agT", t)
                    pe.wait_ge(*next_bank(key, (4, 5, 6, 7)))
                    ps = bank(key)
                    for g in range(KB):
                        ins = pe.transpose(ps[:, g * P:(g + 1) * P], XN[:, t % 2, g * P:(g + 1) * P], ident[:])
                    ins.then_inc(*fills(key))

                for t in tiles(b):
                    gate(t)
                    attend(t)
                    if t % TB:
                        turn(t - 1)
                turn(b * TB + TB - 1)
                pe.wait_ge(*when("w_hi", "X0o"))
                pe.wait_ge(*when("w_lo", "X0o"))
                for t in tiles(b):
                    pe.wait_ge(*freed(("X0", "agT", t)))
                    key = ("X0", "y", t)
                    pe.wait_ge(*next_bank(key, LOW + MID))
                    ps = bank(key)
                    q = slice(t % TB * P, (t % TB + 1) * P)
                    product(pe, ps[:, :], lambda hl, kb: AG[:, hl, kb, q], w("X0o")).then_inc(*fills(key))
                    last_use["X0o"] = key

        def ctile_dve(v, s, c, slots, free_key):
            v.wait_ge(*when(f"ct{c % 2}", (s, c)))
            if free_key is not None:
                v.wait_ge(*filled(free_key))
            dst = SRC[:, c % slots]
            v.tensor_copy(dst[:, 0, :], PB[:, c % 2, :]).then_inc(*mark("ct_hi", (s, c)))
            v.wait_ge(*when("ct_hi", (s, c)))
            v.tensor_tensor(dst[:, 1, :], PB[:, c % 2, :], dst[:, 0, :].bitcast(F32), ALU.subtract).then_inc(
                *mark("ct_lo", (s, c)))

        def x0_dve(v):
            v.wait_ge(*when("pv", (0, NX - 1, len(steps(0)) - 1)))
            v.memset(VX[:, :, :, 128:130], 1.0).then_inc(*mark("vx_ones", 0))
            split_hi(v, "X0q")

            def ct(c):
                ctile_dve(v, "X0", c, 4, ("X0", "v", c - 4) if c >= 4 else None)

            ct(0)
            for c in range(NCT):
                v.wait_ge(*filled(("X0", "k", c)))
                ps = bank(("X0", "k", c))
                v.tensor_scalar(PB[:, 2, :], ps[:, :], 0.0, None, ALU.min).then_inc(*mark("k_min", c))
                if c + 1 < NCT:
                    ct(c + 1)
                v.wait_ge(*when("k_exp", c))
                if c >= 2:
                    v.wait_ge(*when("kv_step", c - 2))
                v.scalar_tensor_tensor(out=PB[:, 4 + c % 2, :], in0=ps[:, :], scalar=0.0, in1=PB[:, 3, :],
                                             op0=ALU.max, op1=ALU.add).then_inc(*frees(("X0", "k", c)))
                if c % NC == 0 and c:
                    blocks(c // NC - 1, v)
            split_hi(v, "X0g")
            blocks(B - 1, v)
            split_hi(v, "X0o")
            for b in range(B):
                ln_dve(v, "X0", b)
            for b in range(B):
                for m in range(KB):
                    key = ("X0", "q", b, m)
                    v.wait_ge(*filled(key))
                    ps = bank(key)
                    v.tensor_scalar(PB[:, 2, :], ps[:, :], 0.0, None, ALU.min).then_inc(*mark("q_min", (b, m)))
                    v.wait_ge(*when("q_exp", (b, m)))
                    if b and m == 0:
                        v.wait_ge(*filled(("X0", "a", TB - 1, 1)))
                    elif m == 0:
                        v.wait_ge(*when("kv_step", NCT - 1))
                    v.scalar_tensor_tensor(out=PB[:, 4 + m, :], in0=ps[:, :], scalar=0.0, in1=PB[:, 3, :],
                                                 op0=ALU.max, op1=ALU.add).then_inc(*frees(key))
                if b == B - 1:
                    split_hi(v, "F0r")
                for t in tiles(b):
                    v.wait_ge(*filled(("X0", "g", t)))
                    ps = bank(("X0", "g", t))
                    if t:
                        v.wait_ge(*when("sigm", t - 1))
                    else:
                        v.wait_ge(*when("bg_in", 0))
                    v.tensor_tensor(PB[:, 0, :], ps[:, :], NB[:, 0, :], ALU.add).then_inc(*frees(("X0", "g", t)))
                    z = NB[:, 1, 0:16]
                    for h in range(2):
                        if t:
                            v.wait_ge(*freed(("X0", "a", t - 1, h)))
                        v.wait_ge(*filled(("X0", "a", t, h)))
                        ps = bank(("X0", "a", t, h))
                        pv_ = ps[:, 0:264].rearrange("p (g n) -> p g n", g=2)
                        v.tensor_scalar(z[:, 8 * h:8 * h + 8].rearrange("p (g n) -> p g n", g=2), pv_[:, :, 128:132],
                                               1e-6, None, ALU.add).then_inc(*mark("z_den", (t, h)))
                    v.wait_ge(*when("z_den", (t, 1)))
                    v.reciprocal(z, z).then_inc(*mark("z", t))
                    v.wait_ge(*when("z", t))
                    if t >= 2:
                        v.wait_ge(*filled(("X0", "agT", t - 2)))
                    else:
                        v.wait_ge(*filled(("X0", "T", NT - 2 + t)))
                    for h in range(2):
                        ps = bank(("X0", "a", t, h))
                        for g in range(2):
                            src = ps[:, 132 * g:132 * g + P].rearrange("p (j n) -> p j n", j=4)
                            zz = z[:, 8 * h + 4 * g:8 * h + 4 * g + 4].unsqueeze(2).broadcast_to([P, 4, 32])
                            dst = XN[:, t % 2, (2 * h + g) * P:(2 * h + g + 1) * P].rearrange("p (j n) -> p j n", j=4)
                            ins = v.tensor_tensor(dst, src, zz, ALU.mult)
                        ins.then_inc(*frees(("X0", "a", t, h)))
                    if t % TB:
                        lo_ag(t - 1, v)
                lo_ag(b * TB + TB - 1, v)
                for t in tiles(b):
                    add_to_x(v, t, ("X0", "y", t))

        def blocks(b, v):
            v.wait_ge(*when("kv_step", b * NC + NC - 1))
            for g in range(KB):
                ps = bank(("X0", "kv", b, g))
                v.tensor_tensor(BD[:, b, g, 0:P], ps[:, 0:P], MR[:, 0:P], ALU.mult)
                v.tensor_scalar(BD[:, b, g, P:132], cs("hm", 0, 4), ps[:, P:P + 1], None, ALU.mult).then_inc(
                    *frees(("X0", "kv", b, g)))

        def lo_ag(t, v):
            q = slice(t % TB * P, (t % TB + 1) * P)
            v.wait_ge(*when("hi", ("X0", "agT", t)))
            v.wait_ge(*filled(("X0", "agT", t)))
            ps = bank(("X0", "agT", t))
            v.tensor_tensor(AG[:, 1, :, q], grid(ps), AG[:, 0, :, q].bitcast(F32), ALU.subtract).then_inc(
                *frees(("X0", "agT", t)))

        def x0_act(act):
            for c in range(NCT):
                act.wait_ge(*when("k_min", c))
                if c:
                    act.wait_ge(*freed(("X0", "k", c - 1)))
                act.activation(PB[:, 3, :], PB[:, 2, :], ACT.Exp).then_inc(*mark("k_exp", c))
                act.wait_ge(*filled(("X0", "v", c)))
                ps = bank(("X0", "v", c))
                if c == 0:
                    act.wait_ge(*when("vx_ones", 0))
                if c >= 2:
                    act.wait_ge(*when("kv_step", c - 2))
                act.activation(VX[:, c % 2, :, 0:P], grid(ps), ACT.Copy).then_inc(*frees(("X0", "v", c)))
            for b in range(B):
                ln_act(act, "X0", b)

            def hi(t):
                q = slice(t % TB * P, (t % TB + 1) * P)
                act.wait_ge(*filled(("X0", "agT", t)))
                ps = bank(("X0", "agT", t))
                if t == TB:
                    act.wait_ge(*filled(("X0", "y", TB - 1)))
                if t == 0:
                    act.wait_ge(*filled(("A0", "s", NX - 1, len(steps(0)) - 1)))
                act.activation(AG[:, 0, :, q], grid(ps), ACT.Copy).then_inc(*mark("hi", ("X0", "agT", t)))

            for b in range(B):
                for m in range(KB):
                    act.wait_ge(*when("q_min", (b, m)))
                    if b or m:
                        act.wait_ge(*freed(("X0", "q", b, m - 1) if m else ("X0", "q", b - 1, KB - 1)))
                    act.activation(PB[:, 3, :], PB[:, 2, :], ACT.Exp).then_inc(*mark("q_exp", (b, m)))
                for t in tiles(b):
                    act.wait_ge(*freed(("X0", "g", t)))
                    if t:
                        act.wait_ge(*when("gated", t - 1))
                    act.activation(PB[:, 1, :], PB[:, 0, :], ACT.Sigmoid).then_inc(*mark("sigm", t))
                    if t % TB:
                        hi(t - 1)
                hi(b * TB + TB - 1)

        def x0_pool(pool):
            split_lo_pool(pool, "X0q")
            split_lo_pool(pool, "X0g")
            split_lo_pool(pool, "X0o")
            for b in range(B):
                ln_pool(pool, "X0", b)
            for b in range(B):
                if b == B - 1:
                    split_lo_pool(pool, "F0r")
                for t in tiles(b):
                    pool.wait_ge(*when("sigm", t))
                    for h in range(2):
                        pool.wait_ge(*freed(("X0", "a", t, h)))
                    pool.tensor_tensor(XN[:, t % 2, :], XN[:, t % 2, :], PB[:, 1, :], ALU.mult).then_inc(
                        *mark("gated", t))

        def load_ctile(sp, s, c, b, tt):
            sp.dma_start(grid(PB[:, c % 2, :]), a["ctxT"][b, :, :, tt * P:(tt + 1) * P]).then_inc(
                *mark(f"ct{c % 2}", (s, c), 16))

        def x0_sp(sp):
            sp.wait_ge(*when("pv", (0, NX - 1, len(steps(0)) - 1)))
            sp.dma_start(MR[:, 0:P], a["bdmask"]).then_inc(*mark("bdmask_in", 0, 16))
            for c in range(NCT):
                if c >= 2:
                    sp.wait_ge(*when("ct_lo", ("X0", c - 2)))
                load_ctile(sp, "X0", c, c // NC, c % NC)
                if c == 1:
                    load_chunk(sp, "X0g")
            sp.wait_ge(*when("att_lo", (0, NX // 2 - 1)))
            sp.dma_start(NB[:, 0, :], a["bg"]).then_inc(*mark("bg_in", 0, 16))
            load_chunk(sp, "X0o")
            load_chunk(sp, "F0r")
            load_chunk(sp, "F0g0")

        m8 = PB[:, 1, 0:64].rearrange("p (t e) -> p t e", t=NT)
        i8f = PB[:, 1, 64:128].rearrange("p (t e) -> p t e", t=NT)
        oh = PB[:, 1, 128:256].rearrange("p (k t e) -> p k t e", k=2, t=NT)
        SCP = PB[:, 2, :].rearrange("p (t e) -> p t e", t=TB)
        LT = PB[0:8, 0, :]

        def router_pe(pe, s):
            chunk = s + "r"
            for b in range(B):
                ln_ready(pe, s, b)
                pe.wait_ge(*when("w_hi", chunk))
                pe.wait_ge(*when("w_lo", chunk))
                pe.wait_ge(*next_bank((s, "lg", b), ALLB))
                ps = bank((s, "lg", b))
                product(pe, ps[:, :], w(chunk, 0, P), xt(b)).then_inc(*fills((s, "lg", b)))
                last_use[chunk] = (s, "lg", b)
            for b in range(B):
                pe.wait_ge(*freed((s, "lg", b)))
                pe.wait_ge(*next_bank((s, "lt", b), ALLB))
                ps = bank((s, "lt", b))
                for i in range(TB):
                    ins = pe.transpose(ps[:, 8 * i:8 * i + 8], LT[:, i * P:(i + 1) * P], ident[0:8, 0:8])
                ins.then_inc(*fills((s, "lt", b)))

        def router_act(act, s):
            for b in range(B):
                act.wait_ge(*filled((s, "lg", b)))
                ps = bank((s, "lg", b))
                if b:
                    act.wait_ge(*filled((s, "lt", b - 1)))
                if s == "F0":
                    ins = act.activation(LT, ps[0:8, :], ACT.Identity, bias=cs("rb")[0:8, :])
                else:
                    ins = act.activation(LT, ps[0:8, :], ACT.Sigmoid)
                ins.then_inc(*frees((s, "lg", b)))

        def router_dve(v, s):
            step = [0]

            def link(ins):
                step[0] += 1
                ins.then_inc(*mark("route", (s, step[0])))
                v.wait_ge(*when("route", (s, step[0])))

            for b in range(B):
                v.wait_ge(*filled((s, "lt", b)))
                ps = bank((s, "lt", b))
                v.tensor_copy(LG[:, b * TB:(b + 1) * TB, :], ps[:, 0:8 * TB].rearrange("p (t e) -> p t e", t=TB)).then_inc(
                    *frees((s, "lt", b)))
            for b in range(B):
                v.wait_ge(*freed((s, "lt", b)))
            for t in range(NT):
                ins = v.max(m8[:, t, :], LG[:, t, :])
            link(ins)
            for t in range(NT):
                ins = v.max_index(i8[:, t, :], m8[:, t, :], LG[:, t, :])
            link(ins)
            link(v.tensor_copy(i8f, i8[:, :, :]))
            iota = cs("iota", 0, 8).unsqueeze(1).broadcast_to([P, NT, 8])
            for k in range(2):
                ins = v.tensor_tensor(oh[:, k], iota, i8f[:, :, k:k + 1].broadcast_to([P, NT, 8]), ALU.is_equal)
            link(ins)
            best, second = m8[:, :, 0:1], m8[:, :, 1:2]
            if s == "F0":
                link(v.tensor_tensor(tw[:, 0, :], m8[:, :, 1], m8[:, :, 0], ALU.subtract))
                v.wait_ge(*when("tw_exp", 0))
                link(v.tensor_scalar(tw[:, 2, :], tw[:, 1, :], 1.0, None, ALU.add))
                link(v.reciprocal(tw[:, 0, :], tw[:, 2, :]))
                link(v.tensor_tensor(tw[:, 2, :], tw[:, 1, :], tw[:, 0, :], ALU.mult))
                best, second = tw[:, 0, :].unsqueeze(2), tw[:, 2, :].unsqueeze(2)
            for k, weight in enumerate((best, second)):
                ins = v.tensor_tensor(oh[:, k], oh[:, k], weight.broadcast_to([P, NT, 8]), ALU.mult)
            link(ins)
            ins = v.tensor_tensor(SCR[:, :, 0:8], oh[:, 0], oh[:, 1], ALU.add)
            link(ins)
            v.memset(SCR[:, :, 8:9], 1.0).then_inc(*mark("scores", s))

        F0N = [(e, b, m) for e in range(NE) for b in range(B) for m in range(KB)]

        def f0_pe(pe):
            for b in range(B):
                ln_pe(pe, "F0", b)
            router_pe(pe, "F0")
            for b in range(B):
                pe.wait_ge(*when("scp", b))
                pe.wait_ge(*next_bank(("F0", "scT", b), ALLB))
                ps = bank(("F0", "scT", b))
                for i in range(TB):
                    ins = pe.transpose(ps[:, i * P:(i + 1) * P], SCP[:, i, :], ident[:])
                ins.then_inc(*fills(("F0", "scT", b)))
                pe.wait_ge(*freed(("F0", "scT", b)))
                for t in tiles(b):
                    if t == 0:
                        pe.wait_ge(*when("db_in", 0))
                    pe.wait_ge(*next_bank(("F0", "db", t), ALLB))
                    ps = bank(("F0", "db", t))
                    pe.matmul(ps[:, :], NB[:, 1, t % TB * P:(t % TB + 1) * P], NB[:, 0, :], start=True, stop=True).then_inc(
                        *fills(("F0", "db", t)))
            for e in range(NE):
                for b in range(B):
                    for m in range(KB):
                        for T in "gu":
                            chunk, key = f"F0{T}{e}", ("F0", T, e, b, m)
                            pe.wait_ge(*when("w_hi", chunk))
                            pe.wait_ge(*when("w_lo", chunk))
                            pe.wait_ge(*next_bank(key, ALLB))
                            ps = bank(key)
                            product(pe, ps[:, :], w(chunk, m * P, (m + 1) * P), xt(b)).then_inc(*fills(key))
                            last_use[chunk] = xt_last[("F0", b)] = key
                for b in range(B):
                    chunk = f"F0d{e}"
                    pe.wait_ge(*when("w_hi", chunk))
                    pe.wait_ge(*when("w_lo", chunk))
                    pe.wait_ge(*when("act_lo", (e, b, KB - 1)))
                    for t in tiles(b):
                        key = ("F0", "d", e, t)
                        pe.wait_ge(*next_bank(key, ALLB))
                        ps = bank(key)
                        lhs = lambda hl, kb: AH[:, b, hl, kb * 512 + t % TB * P:kb * 512 + (t % TB + 1) * P]
                        product(pe, ps[:, :], lhs, w(chunk)).then_inc(*fills(key))
                        last_use[chunk] = key

        def f0_dve(v):
            for b in range(B):
                ln_dve(v, "F0", b)
                if b == 0:
                    split_hi(v, "F0g0")
            split_hi(v, "F0u0")
            v.tensor_scalar(cs("ub1", 0, 32), cs("ub", 0, 32), 1.0, None, ALU.add).then_inc(*mark("ub1", 0))
            router_dve(v, "F0")
            split_hi(v, "F0d0")
            for b in range(B):
                if b:
                    v.wait_ge(*filled(("F0", "scT", 0)))
                else:
                    v.memset(PB[:, 2, :], 0.0).then_inc(*mark("scp0", 0))
                    v.wait_ge(*when("scp0", 0))
                    v.wait_ge(*when("scores", "F0"))
                v.tensor_copy(SCP[:, :, 0:8], SCR[:, b * TB:(b + 1) * TB, 0:8]).then_inc(*mark("scp", b))
            for t in range(NT):
                add_to_x(v, t, ("F0", "db", t))

            def product_of(n):
                e, b, m = F0N[n]
                k = n % 2
                v.wait_ge(*when("glu", n))
                v.wait_ge(*freed(("F0", "u", e, b, m)))
                if n >= 2:
                    v.wait_ge(*when("act_lo", F0N[n - 2]))
                v.scalar_tensor_tensor(out=PB[:, 6 + k, :], in0=PB[:, 4 + k, :], scalar=8.0, in1=PB[:, 2 + k, :],
                                              op0=ALU.min, op1=ALU.mult).then_inc(*mark("act_f", n))

            for n, (e, b, m) in enumerate(F0N):
                k = n % 2
                v.wait_ge(*filled(("F0", "g", e, b, m)))
                ps = bank(("F0", "g", e, b, m))
                if n >= 2:
                    v.wait_ge(*when("glu", n - 2))
                v.tensor_scalar(PB[:, k, :], ps[:, :], cs("gb", e * 4 + m), 7.0, ALU.add, ALU.min).then_inc(
                    *frees(("F0", "g", e, b, m)))
                v.wait_ge(*filled(("F0", "u", e, b, m)))
                ps = bank(("F0", "u", e, b, m))
                if n >= 2:
                    v.wait_ge(*when("act_f", n - 2))
                else:
                    v.wait_ge(*when("ub1", 0))
                v.tensor_scalar(PB[:, 4 + k, :], ps[:, :], cs("ub1", e * 4 + m), -6.0, ALU.add, ALU.max).then_inc(
                    *frees(("F0", "u", e, b, m)))
                if b or m:
                    product_of(n - 1)
                if (b, m) == (B - 1, KB - 1):
                    product_of(n)
                    nxt = CHUNKS[CI[f"F0g{e}"] + 3:CI[f"F0g{e}"] + 6]
                    split_hi(v, nxt[0])
                    split_hi(v, nxt[1])
                    for t in range(NT):
                        add_to_x(v, t, ("F0", "d", e, t), SCR[:, t, e:e + 1])
                    split_hi(v, nxt[2])

        def f0_act(act):
            for b in range(B):
                ln_act(act, "F0", b)
            router_act(act, "F0")
            act.wait_ge(*when("route", ("F0", 5)))
            act.activation(tw[:, 1, :], tw[:, 0, :], ACT.Exp).then_inc(*mark("tw_exp", 0))
            for b in range(B):
                act.wait_ge(*filled(("F0", "scT", b)))
                ps = bank(("F0", "scT", b))
                if b:
                    act.wait_ge(*filled(("F0", "db", TB - 1)))
                act.activation(NB[:, 1, :], ps[:, :], ACT.Copy).then_inc(*frees(("F0", "scT", b)))

            def hi(n):
                e, b, m = F0N[n]
                act.wait_ge(*when("act_f", n))
                if e and m == 0:
                    act.wait_ge(*filled(("F0", "d", e - 1, b * TB + TB - 1)))
                if n == 0:
                    act.wait_ge(*filled(("A0", "s", NX - 1, len(steps(0)) - 1)))
                act.activation(AH[:, b, 0, m * 512:(m + 1) * 512], PB[:, 6 + n % 2, :], ACT.Copy).then_inc(
                    *mark("act_hi", n))

            for n, (e, b, m) in enumerate(F0N):
                act.wait_ge(*freed(("F0", "g", e, b, m)))
                if n >= 2:
                    act.wait_ge(*when("act_f", n - 2))
                act.activation(PB[:, 2 + n % 2, :], PB[:, n % 2, :], ACT.Sigmoid, scale=1.702).then_inc(*mark("sig", n))
                if b or m:
                    hi(n - 1)
                if (b, m) == (B - 1, KB - 1):
                    hi(n)

        def f0_pool(pool):
            for b in range(B):
                ln_pool(pool, "F0", b)
                if b == 0:
                    split_lo_pool(pool, "F0g0")
            split_lo_pool(pool, "F0u0")
            split_lo_pool(pool, "F0d0")

            def lo(n):
                e, b, m = F0N[n]
                pool.wait_ge(*when("act_hi", n))
                pool.tensor_tensor(AH[:, b, 1, m * 512:(m + 1) * 512], PB[:, 6 + n % 2, :],
                                          AH[:, b, 0, m * 512:(m + 1) * 512].bitcast(F32), ALU.subtract).then_inc(
                                              *mark("act_lo", (e, b, m)))

            for n, (e, b, m) in enumerate(F0N):
                pool.wait_ge(*when("sig", n))
                pool.tensor_tensor(PB[:, 2 + n % 2, :], PB[:, 2 + n % 2, :], PB[:, n % 2, :], ALU.mult).then_inc(
                    *mark("glu", n))
                if b or m:
                    lo(n - 1)
                if (b, m) == (B - 1, KB - 1):
                    lo(n)
                    for chunk in CHUNKS[CI[f"F0g{e}"] + 3:CI[f"F0g{e}"] + 6]:
                        split_lo_pool(pool, chunk)

        def f0_sp(sp):
            sp.wait_ge(*filled(("X0", "agT", NT - 1)))
            sp.wait_ge(*when("z", NT - 1))
            sp.wait_ge(*freed(("X0", "a", NT - 1, 1)))
            sp.wait_ge(*freed(("X0", "g", NT - 1)))
            sp.dma_start(NB[:, 0, :], a["down_bias"]).then_inc(*mark("db_in", 0, 16))
            for c in range(CI["F0g0"] + 1, CI["A1kv"] + 1):
                load_chunk(sp, CHUNKS[c])

        JOBS = [(b, t, "i") for b in range(B) for t in range(3)] + [(b, t, "t") for b in range(B) for t in range(2, NC)]
        QJOBS = [(t // TB, t % TB, "q") for t in range(NT)]
        ALLJ = JOBS + QJOBS

        def x1_pe(pe):
            def turn(c):
                pe.wait_ge(*when("n", c))
                key = ("X1", "nT", c)
                pe.wait_ge(*next_bank(key, (4, 5, 6, 7)))
                ps = bank(key)
                for g in range(KB):
                    ins = pe.transpose(ps[:, g * P:(g + 1) * P], XN[:, c % 2, g * P:(g + 1) * P], ident[:])
                ins.then_inc(*fills(key))

            for c, (b, tt, kind) in enumerate(ALLJ):
                if kind == "q":
                    if c == len(JOBS):
                        turn(c - 1)
                        for bb in range(B):
                            ln_pe(pe, "X1", bb)
                    if tt == 0:
                        ln_ready(pe, "X1", b)
                    parts = [("k", "X1q", xtile(c - len(JOBS)))]
                else:
                    pe.wait_ge(*when("ct_lo", ("X1", c)))
                    ct = (lambda c: lambda hl, kb: SRC[:, c % 2, hl, kb * P:(kb + 1) * P])(c)
                    parts = [(T, f"X1{T}i" if kind == "i" else f"X1{T}", ct) for T in "kv"]
                for T, chunk, lhs in parts:
                    pe.wait_ge(*when("w_hi", chunk))
                    pe.wait_ge(*when("w_lo", chunk))
                    key = ("X1", T, c)
                    pe.wait_ge(*next_bank(key, LOW if T == "k" else MID))
                    ps = bank(key)
                    product(pe, ps[:, :], lhs, w(chunk)).then_inc(*fills(key))
                    last_use[chunk] = key
                    if kind == "q":
                        proj_last[(2, b)] = key
                if c and c != len(JOBS):
                    turn(c - 1)
            turn(len(ALLJ) - 1)

        def x1_dve(v):
            v.wait_ge(*when("pattern_in", 0))
            v.wait_ge(*filled(("A1", "s", NX - 1, len(steps(1)) - 1)))
            v.tensor_copy(KS[96:100, :, :], PB[96:100, 0:2, :].rearrange("p a n -> p (a n)").unsqueeze(1)
                                 .broadcast_to([4, 8, 1024])).then_inc(*mark("pattern", 2))
            v.wait_ge(*when("att_lo", (1, NX - 1)))
            v.wait_ge(*when("pv", (1, NX - 1, len(steps(1)) - 1)))
            v.wait_ge(*when("kvb_in", 0))
            split_hi(v, "X1k")

            def ct(c):
                ctile_dve(v, "X1", c, 2, ("X1", "v", c - 2) if c >= 2 else None)

            def norm_weight(c):
                b, tt, kind = ALLJ[c]
                v.wait_ge(*filled(("X1", "nT", c)))
                ps = bank(("X1", "nT", c))
                if c:
                    if ALLJ[c - 1][1:] != (2, "i"):
                        v.wait_ge(*when("src_lo", (2, c - 1)))
                wt = cs({"i": "wki", "t": "wk", "q": "wq"}[kind], 0, 4).unsqueeze(2).broadcast_to([P, KB, P])
                v.tensor_tensor(grid(PB[:, 7, :]), grid(ps), wt, ALU.mult).then_inc(*frees(("X1", "nT", c)))
                if (tt, kind) == (2, "i"):
                    v.wait_ge(*freed(("X1", "nT", c)))
                    col = grid(PB[:, 7, :])[:, :, 0]
                    v.tensor_copy(KI[:, b, 0, :], col).then_inc(*mark("ki_hi", b))
                    v.wait_ge(*when("ki_hi", b))
                    v.tensor_tensor(KI[:, b, 1, :], col, KI[:, b, 0, :].bitcast(F32), ALU.subtract).then_inc(
                        *mark("ki", b))
                    return

            def norm_lo(c):
                b, tt, kind = ALLJ[c]
                if (tt, kind) == (2, "i"):
                    return
                dst = SRC[:, 2 + c % 2]
                v.wait_ge(*when("hi", (2, c)))
                ins = v.tensor_tensor(dst[:, 1, :], PB[:, 7, :], dst[:, 0, :].bitcast(F32), ALU.subtract)
                if (tt, kind) == (2, "t"):
                    ins.then_inc(*mark("lo_first", c))
                    v.wait_ge(*when("lo_first", c))
                    v.wait_ge(*when("ki", b))
                    for hl in range(2):
                        ins = v.tensor_copy(grid(dst[:, hl, :])[:, :, 0], KI[:, b, hl, :].bitcast(F32))
                ins.then_inc(*mark("src_lo", (2, c)))

            ct(0)
            for c, (b, tt, kind) in enumerate(ALLJ):
                if c == len(JOBS):
                    norm_weight(c - 1)
                    norm_lo(c - 1)
                    for bb in range(B):
                        ln_dve(v, "X1", bb)
                    v.wait_ge(*when("ob_in", 0))
                    for t in range(NT):
                        v.wait_ge(*when("xn", ("X1", t)))
                        v.tensor_tensor(X[:, t, :], X[:, t, :], PB[:, 3, :], ALU.add).then_inc(*mark("x_bias", t))
                        x_key[t] = ("x_bias", t)
                    v.wait_ge(*when("qb_in", 0))
                bias = {"i": 2, "t": 4, "q": 2}[kind]
                v.wait_ge(*filled(("X1", "k", c)))
                ps = bank(("X1", "k", c))
                if c:
                    v.wait_ge(*when("n", c - 1))
                v.tensor_tensor(PB[:, 6, :], ps[:, :], PB[:, bias, :], ALU.add).then_inc(*frees(("X1", "k", c)))
                if kind != "q":
                    if c + 1 < len(JOBS):
                        ct(c + 1)
                    v.wait_ge(*filled(("X1", "v", c)))
                    ps = bank(("X1", "v", c))
                    if c >= 2:
                        v.wait_ge(*when(f"v_stored{c % 2}", (2, c - 2)))
                    if tt == 2:
                        v.tensor_tensor(NB[:, c % 2, :], ps[:, :], PB[:, bias + 1, :], ALU.add).then_inc(
                            *mark("v_row", c))
                        v.wait_ge(*when("v_row", c))
                        ins = v.tensor_scalar(NB[:, c % 2, :], NB[:, c % 2, :], cs("img" if kind == "i" else "txt"), None, ALU.mult)
                    else:
                        ins = v.tensor_tensor(NB[:, c % 2, :], ps[:, :], PB[:, bias + 1, :], ALU.add)
                    ins.then_inc(*frees(("X1", "v", c)))
                if c and c != len(JOBS):
                    norm_weight(c - 1)
                v.wait_ge(*when("rk", c))
                if c >= 2:
                    v.wait_ge(*filled(("X1", "nT", c - 2)))
                if c >= len(JOBS):
                    v.wait_ge(*filled(("X1", "T", NT - 2 + c % 2) if c < len(JOBS) + 2 else ("X1", "nT", c - 2)))
                v.tensor_scalar(XN[:, c % 2, :], PB[:, 6, :], ss[:, 2:3], None, ALU.mult).then_inc(*mark("n", c))
                if c and c != len(JOBS):
                    norm_lo(c - 1)
                if c == 5:
                    split_hi(v, "X1v")
                    split_hi(v, "X1q")
                if c == len(JOBS) - 1:
                    split_hi(v, "X1o")
                    split_hi(v, "F1r")
            norm_weight(len(ALLJ) - 1)
            norm_lo(len(ALLJ) - 1)
            split_hi(v, "F1h0")

        def x1_act(act):
            def hi(c):
                if ALLJ[c][1:] == (2, "i"):
                    return
                act.wait_ge(*freed(("X1", "nT", c)))
                prev = [p for p in range(c) if p % 2 == c % 2 and ALLJ[p][1:] != (2, "i")]
                if prev:
                    act.wait_ge(*when(f"src_stored{2 + c % 2}", (2, prev[-1])))
                act.activation(SRC[:, 2 + c % 2, 0, :], PB[:, 7, :], ACT.Copy).then_inc(*mark("hi", (2, c)))

            act.wait_ge(*freed(("A1", "mt", NX - 1)))
            for c in range(len(ALLJ)):
                if c == len(JOBS):
                    hi(c - 1)
                    for b in range(B):
                        ln_act(act, "X1", b)
                act.wait_ge(*freed(("X1", "k", c)))
                if c:
                    act.wait_ge(*when("rk", c - 1))
                elif True:
                    act.wait_ge(*when(f"mrow{(NX - 1) % 4}", (1, NX - 1)))
                act.activation(MR[:, :], PB[:, 6, :], ACT.Square, accum_out=ss[:, 0:1]).then_inc(*mark("sq", c))
                if c and c != len(JOBS):
                    hi(c - 1)
            hi(len(ALLJ) - 1)

        def x1_pool(pool):
            split_lo_pool(pool, "X1k")
            for c in range(len(ALLJ)):
                if c == len(JOBS):
                    for b in range(B):
                        ln_pool(pool, "X1", b)
                pool.wait_ge(*when("sq", c))
                pool.tensor_scalar(ss[:, 1:2], ss[:, 0:1], 1.0 / D, 1e-6, ALU.mult, ALU.add).then_inc(*mark("ms2", c))
                pool.wait_ge(*when("ms2", c))
                if c:
                    pool.wait_ge(*when("n", c - 1))
                pool.tensor_tensor(ss[:, 2:3], ss[:, 1:2], cs("mhalf"), ALU.pow).then_inc(*mark("rk", c))
                if c == 5:
                    split_lo_pool(pool, "X1v")
                    split_lo_pool(pool, "X1q")
                if c == len(JOBS) - 1:
                    split_lo_pool(pool, "X1o")
                    split_lo_pool(pool, "F1r")
            split_lo_pool(pool, "F1h0")

        def x1_sp(sp):
            sp.wait_ge(*when("pv", (1, NX - 1, len(steps(1)) - 1)))
            sp.dma_start(PB[96:100, 0:2, :].rearrange("p a n -> p (a n)"), a["pattern"]).then_inc(
                *mark("pattern_in", 0, 16))
            for dst, src in ([(PB[:, 2 + n, :], a[x]) for n, x in enumerate(("ki_b", "vi_b", "k_b", "v_b"))]):
                sp.dma_start(dst, src).then_inc(*mark("kvb_in", 0, 16))
            sp.wait_ge(*when("pattern", 2))

            def store(c):
                b, tt, kind = ALLJ[c]
                if (tt, kind) != (2, "i"):
                    sp.wait_ge(*when("src_lo", (2, c)))
                    dram_t = (QD if kind == "q" else KD)[2]
                    for dst, src in ([(dram_t[b, hl, :, tt * P:(tt + 1) * P].rearrange("(g p) t -> p g t", g=KB),
                           grid(SRC[:, 2 + c % 2, hl, :]).bitcast(F32)) for hl in range(2)]):
                        sp.dma_start(dst, src).then_inc(*mark(f"src_stored{2 + c % 2}", (2, c), 16))

            for c in range(2):
                load_ctile(sp, "X1", c, *JOBS[c][:2])
            for c, (b, tt, kind) in enumerate(JOBS):
                if c + 2 < len(JOBS):
                    sp.wait_ge(*when("ct_lo", ("X1", c)))
                    load_ctile(sp, "X1", c + 2, *JOBS[c + 2][:2])
                sp.wait_ge(*freed(("X1", "v", c)))
                sp.dma_start(VD[2][b, tt + (kind == "t")], NB[:, c % 2, :]).then_inc(
                    *mark(f"v_stored{c % 2}", (2, c), 16))
                if c:
                    store(c - 1)
                if c == 0:
                    load_chunk(sp, "X1v")
                if c == 5:
                    sp.wait_ge(*freed(("X1", "k", 5)))
                    sp.dma_start(PB[:, 2, :], a["q_b"]).then_inc(*mark("qb_in", 0, 16))
                    sp.dma_start(PB[:, 3, :], a["o_b"]).then_inc(*mark("ob_in", 0, 16))
                    load_chunk(sp, "X1q")
                if c == 8:
                    load_chunk(sp, "X1o")
            load_chunk(sp, "F1r")
            store(len(JOBS) - 1)
            for c in range(len(JOBS), len(ALLJ)):
                store(c)
                if c == len(JOBS):
                    load_chunk(sp, "F1h0")

        def f1_pe(pe):
            for b in range(B):
                ln_pe(pe, "F1", b)
            router_pe(pe, "F1")

            def turn(e, tp):
                key = ("F1", "aT", e, tp)
                for t in (2 * tp, 2 * tp + 1):
                    pe.wait_ge(*freed(("F1", "h", e, t)))
                pe.wait_ge(*next_bank(key, ALLB))
                ps = bank(key)
                for kb in range(2):
                    for t in (2 * tp, 2 * tp + 1):
                        ins = pe.transpose(ps[:, kb * 256 + t % 2 * P:kb * 256 + t % 2 * P + P],
                                           PB[:, 2 + t % 4, kb * P:(kb + 1) * P], ident[:])
                ins.then_inc(*fills(key))

            for e in range(NE + 2):
                for t in range(NT):
                    if e <= NE:
                        pe.wait_ge(*when("w_hi", f"F1h{e}"))
                        pe.wait_ge(*when("w_lo", f"F1h{e}"))
                        key = ("F1", "h", e, t)
                        pe.wait_ge(*next_bank(key, ALLB))
                        ps = bank(key)
                        product(pe, ps[:, :], xtile(t), w(f"F1h{e}")).then_inc(*fills(key))
                        last_use[f"F1h{e}"] = key
                    n = e * NT + t
                    if t % 2 and 3 <= n <= NE * NT + NT + 1:
                        turn((n - 3) // NT, (n - 3) % NT // 2)
                    if e:
                        chunk, key = f"F1d{e - 1}", ("F1", "d", e - 1, t)
                        pe.wait_ge(*when("w_hi", chunk))
                        pe.wait_ge(*when("w_lo", chunk))
                        pe.wait_ge(*freed(("F1", "aT", e - 1, t // 2)))
                        pe.wait_ge(*next_bank(key, ALLB))
                        ps = bank(key)
                        par = (e - 1) % 2
                        lhs = lambda hl, kb: AH[:, par, hl, kb * 1024 + t * P:kb * 1024 + (t + 1) * P]
                        product(pe, ps[:, :], lhs, w(chunk), blocks=2).then_inc(*fills(key))
                        last_use[chunk] = key

        def f1_ah(e, hl, tp):
            return AH[:, e % 2, hl, :].rearrange("p (k n) -> p k n", k=2)[:, :, tp * 256:(tp + 1) * 256]

        def f1_dve(v):
            for b in range(B):
                ln_dve(v, "F1", b)
            split_hi(v, "F1h1")
            router_dve(v, "F1")
            v.wait_ge(*when("scores", "F1"))
            for e in range(NE + 2):
                if e:
                    split_hi(v, f"F1d{e - 1}") if e > 1 else None
                for t in range(NT):
                    if e <= NE:
                        v.wait_ge(*filled(("F1", "h", e, t)))
                        ps = bank(("F1", "h", e, t))
                        v.wait_ge(*when("silu", (e, t)))
                        n = e * NT + t
                        if n >= 4:
                            v.wait_ge(*filled(("F1", "aT", (n - 4) // NT, (n - 4) % NT // 2)))
                        v.scalar_tensor_tensor(out=PB[:, 2 + t % 4, 0:256], in0=ps[:, 256:512], scalar=SCR[:, t, e:e + 1],
                                                     in1=PB[:, t % 2, 0:256], op0=ALU.mult, op1=ALU.mult).then_inc(
                                                         *frees(("F1", "h", e, t)))
                    n = e * NT + t
                    if t % 2 and 3 <= n <= NE * NT + NT + 1:
                        e2, tp = (n - 3) // NT, (n - 3) % NT // 2
                        key = ("F1", "aT", e2, tp)
                        v.wait_ge(*when("hi", key))
                        v.wait_ge(*filled(key))
                        ps = bank(key)
                        v.tensor_tensor(f1_ah(e2, 1, tp), ps[:, :].rearrange("p (k n) -> p k n", k=2),
                                              f1_ah(e2, 0, tp).bitcast(F32), ALU.subtract).then_inc(*frees(key))
                    if e:
                        add_to_x(v, t, ("F1", "d", e - 1, t))
                    if e == 0 and t == 0:
                        split_hi(v, "F1d0")
                    if e and t == 1 and e + 1 <= NE:
                        split_hi(v, f"F1h{e + 1}")

        def f1_act(act):
            for b in range(B):
                ln_act(act, "F1", b)
            router_act(act, "F1")
            act.wait_ge(*when("scores", "F1"))
            for e in range(NE + 2):
                for t in range(NT):
                    n = e * NT + t
                    if e <= NE:
                        act.wait_ge(*filled(("F1", "h", e, t)))
                        ps = bank(("F1", "h", e, t))
                        if n >= 2:
                            act.wait_ge(*freed(("F1", "h", (n - 2) // NT, (n - 2) % NT)))
                        act.activation(PB[:, t % 2, 0:256], ps[:, 0:256], ACT.Silu, scale=SCR[:, t, e:e + 1]).then_inc(
                            *mark("silu", (e, t)))
                    if t % 2 and 3 <= n <= NE * NT + NT + 1:
                        e2, tp = (n - 3) // NT, (n - 3) % NT // 2
                        key = ("F1", "aT", e2, tp)
                        act.wait_ge(*filled(key))
                        ps = bank(key)
                        if e2 >= 2 and tp == 0:
                            act.wait_ge(*filled(("F1", "d", e2 - 2, NT - 1)))
                        if n == 3:
                            act.wait_ge(*filled(("X1", "s", NX - 1, len(steps(2)) - 1)))
                        act.activation(f1_ah(e2, 0, tp), ps[:, :].rearrange("p (k n) -> p k n", k=2), ACT.Copy).then_inc(
                            *mark("hi", key))

        def f1_pool(pool):
            for b in range(B):
                ln_pool(pool, "F1", b)
            split_lo_pool(pool, "F1h1")
            split_lo_pool(pool, "F1d0")
            for e in range(1, NE + 1):
                if e > 1:
                    split_lo_pool(pool, f"F1d{e - 1}")
                if e + 1 <= NE:
                    split_lo_pool(pool, f"F1h{e + 1}")
            split_lo_pool(pool, f"F1d{NE}")

        block = ctx.enter_context(nc.Block())

        @block.tensor
        def _(pe):
            pe.wait_ge(*when("const", "pool"))
            if "A0" in STAGES:
                for b in range(B):
                    ln_pe(pe, "A0", b)
                qkv_pe(pe, 0)
                at_pe(pe, 0)
            if "X0" in STAGES:
                x0_pe(pe)
            if "F0" in STAGES:
                f0_pe(pe)
            if "A1" in STAGES:
                for b in range(B):
                    ln_pe(pe, "A1", b)
                qkv_pe(pe, 1)
                at_pe(pe, 1)
            if "X1" in STAGES:
                x1_pe(pe)
                at_pe(pe, 2)
            if "F1" in STAGES:
                f1_pe(pe)

        @block.vector
        def _(v):
            v.wait_ge(*when("small_in", 0))
            split_hi(v, "A0q")
            ln_dve(v, "A0", 0)
            split_hi(v, "A0k")
            ln_dve(v, "A0", 1)
            split_hi(v, "A0v")
            v.wait_ge(*when("const", "pool"))
            v.tensor_copy(KS[96:98, :, 0:512], ones[96:98, 0:1].unsqueeze(1).broadcast_to([2, 8, 512])).then_inc(
                *mark("pattern", 0))
            qkv_dve(v, 0, [["A0o"], ["X0k"]])
            split_hi(v, "X0v")
            at_dve(v, 0)
            if "X0" in STAGES:
                x0_dve(v)
            if "F0" in STAGES:
                f0_dve(v)
            if "A1" in STAGES:
                for b in range(B):
                    ln_dve(v, "A1", b)
                v.wait_ge(*filled(("F0", "d", NE - 1, NT - 1)))
                o = ones[64:66, 0:1].unsqueeze(1).broadcast_to([2, 4, 512])
                v.tensor_copy(K1[0][64:66, :, 512:1024], o)
                qkv_dve(v, 1, [["A1o0"], ["A1o1"], []])
                for T, b in (("q", 0), ("q", 1), ("k", 0), ("k", 1)):
                    wait_stored(v, 1, T, b)
                v.tensor_copy(K1[1][64:66, :, 512:1024], o).then_inc(*mark("pattern", 1))
                split_hi(v, "X1ki")
                at_dve(v, 1)
                if "X1" in STAGES:
                    split_hi(v, "X1vi")
            if "X1" in STAGES:
                x1_dve(v)
                at_dve(v, 2)
            if "F1" in STAGES:
                f1_dve(v)

        @block.scalar
        def _(act):
            act.wait_ge(*when("small_in", 0))
            for b in range(B):
                ln_act(act, "A0", b)
            qkv_act(act, 0)
            at_act(act, 0)
            if "X0" in STAGES:
                x0_act(act)
            if "F0" in STAGES:
                f0_act(act)
            if "A1" in STAGES:
                for b in range(B):
                    ln_act(act, "A1", b)
                qkv_act(act, 1)
                at_act(act, 1)
            if "X1" in STAGES:
                x1_act(act)
                at_act(act, 2)
            if "F1" in STAGES:
                f1_act(act)

        @block.gpsimd
        def _(pool):
            step = [0]

            def link(ins):
                step[0] += 1
                ins.then_inc(*mark("const_step", step[0]))
                pool.wait_ge(*when("const_step", step[0]))

            for t, value in ((ident, 0.0), (identb, 0.0), (mask_qk, 0.0), (mask_kq, 0.0), (ones, 1.0)):
                link(pool.memset(t[:], value))
            for t in (ident, identb):
                link(pool.affine_select(out=t[:], in_=t[:], compare_op=ALU.not_equal, fill=1.0, base=0,
                                        pattern=[[-1, P]], channel_multiplier=1))
            link(pool.affine_select(out=mask_qk[:], in_=mask_qk[:], compare_op=ALU.is_ge, fill=MASKED, base=0,
                                    pattern=[[-1, P]], channel_multiplier=1))
            link(pool.affine_select(out=mask_kq[:], in_=mask_kq[:], compare_op=ALU.is_ge, fill=MASKED, base=0,
                                    pattern=[[1, P]], channel_multiplier=-1))
            pool.wait_ge(*when("small_in", 0))
            for k, name in enumerate(("img", "txt")):
                ins = pool.tensor_scalar(onesm[:, k, :], ones[:, 0:32], cs(name), None, ALU.mult)
            ins.then_inc(*mark("const", "pool"))
            split_lo_pool(pool, "A0q")
            ln_pool(pool, "A0", 0)
            split_lo_pool(pool, "A0k")
            ln_pool(pool, "A0", 1)
            split_lo_pool(pool, "A0v")
            qkv_pool(pool, 0, [["A0o"], ["X0k"]])
            split_lo_pool(pool, "X0v")
            at_pool(pool, 0)
            if "X0" in STAGES:
                x0_pool(pool)
            if "F0" in STAGES:
                f0_pool(pool)
            if "A1" in STAGES:
                for b in range(B):
                    ln_pool(pool, "A1", b)
                qkv_pool(pool, 1, [["A1o0"], ["A1o1"], []])
                split_lo_pool(pool, "X1ki")
                at_pool(pool, 1)
                if "X1" in STAGES:
                    split_lo_pool(pool, "X1vi")
            if "X1" in STAGES:
                x1_pool(pool)
                at_pool(pool, 2)
            if "F1" in STAGES:
                f1_pool(pool)

        @block.sync
        def _(sp):
            sp.dma_start(small[:, 0:100], a["small"]).then_inc(*mark("small_in", 0, 16))
            load_chunk(sp, "A0q")
            for t in range(NT):
                sp.dma_start(X[:, t, :], a["x"][t]).then_inc(*mark(f"x_in{t}", t, 16))
            sp.dma_start(PB[:, 0:2, :], a["rope0"]).then_inc(*mark("rope_tables", 0, 16))
            for c in ("A0k", "A0v", "A0o"):
                load_chunk(sp, c)
            qkv_sp(sp, 0, {7: "X0k", 15: "X0v"})
            at_sp(sp, 0)
            load_chunk(sp, "X0q")
            if "X0" in STAGES:
                x0_sp(sp)
            if "F0" in STAGES:
                f0_sp(sp)
            if "A1" in STAGES:
                sp.wait_ge(*when("act_lo", F0N[-1]))
                sp.dma_start(PB[:, 0:2, :], a["rope1"]).then_inc(*mark("rope_tables", 1, 16))
                qkv_sp(sp, 1, {5: "A1o0", 13: "A1o1"})
                load_chunk(sp, "X1ki")
                at_sp(sp, 1)
            if "X1" in STAGES:
                load_chunk(sp, "X1vi")
                load_chunk(sp, "X1k")
                x1_sp(sp)
                at_sp(sp, 2)
            if "F1" in STAGES:
                for c in range(CI["F1h0"] + 1, len(CHUNKS)):
                    load_chunk(sp, CHUNKS[c])
            for t in range(NT):
                sp.wait_ge(*when(*x_key[t]))
                sp.dma_start(out[t], X[:, t, :]).then_inc(*mark("out_stored", t, 16))
            sp.wait_ge(*when("out_stored", NT - 1))
            assert freed_keys == set(bank_of), set(bank_of) - freed_keys


def rope_table(dim, rows, base=10000.0):
    f32 = np.float32
    if dim == 32:
        inv = f32(1.0) / np.power(f32(base), np.arange(0, dim, 2, dtype=f32) / f32(dim))
    else:
        inv = np.power(f32(base), -(np.arange(0, dim, 2, dtype=f32) / f32(dim)))
    angle = np.arange(S, dtype=f32)[:, None] * inv.astype(f32)[None, :]
    table = np.stack([np.cos(angle).T, np.sin(angle).T], axis=1).astype(f32)
    return np.ascontiguousarray(np.tile(table, (P // (dim // 2), 1, 1)))


def laid_out(i):
    def chunk(m):
        k = m.shape[0] // P
        c = np.ascontiguousarray(m.reshape(k, P, 512).transpose(1, 0, 2)).reshape(P, k * 512)
        if k < KB:
            c = np.concatenate([c, np.zeros((P, (KB - k) * 512), c.dtype)], axis=1)
        return c

    def halves(m, heads, dim, per):
        return m.reshape(m.shape[0], heads // per, per, 2, dim // 2).transpose(0, 1, 3, 2, 4).reshape(m.shape[0], -1)

    w = {}
    w["A0q"], w["A0k"] = halves(i["L0_attn_wq"], 16, 32, 8), halves(i["L0_attn_wk"], 16, 32, 8)
    w["A0v"], w["A0o"] = i["L0_attn_wv"], i["L0_attn_wo"]
    w["X0k"], w["X0v"] = i["L0_xattn_Wkv"][:512].T, i["L0_xattn_Wkv"][512:].T
    w["X0q"], w["X0g"], w["X0o"] = i["L0_xattn_Wq"].T, i["L0_xattn_Wg"].T, i["L0_xattn_Wo"].T

    def router(m):
        r = np.zeros((512, 512), m.dtype)
        r[:, :8] = m.T
        return r

    w["F0r"], w["F1r"] = router(i["L0_ffn_router_weight"]), router(i["L1_ffn_gate_w"])
    for e in range(NE):
        w[f"F0g{e}"], w[f"F0u{e}"] = i["L0_ffn_gate_up_proj"][e][:, 0::2], i["L0_ffn_gate_up_proj"][e][:, 1::2]
        w[f"F0d{e}"] = i["L0_ffn_down_proj"][e]
        w[f"F1h{e}"] = np.concatenate([i["L1_ffn_w1"][e].T, i["L1_ffn_w3"][e].T], axis=1)
        w[f"F1d{e}"] = i["L1_ffn_w2"][e].T
    w[f"F1h{NE}"] = np.concatenate([i["L1_ffn_ws1"].T, i["L1_ffn_ws3"].T], axis=1)
    w[f"F1d{NE}"] = i["L1_ffn_ws2"].T
    qkv = i["L1_attn_w_qkv"]
    q = halves(qkv[:, :1024], 16, 64, 4)
    w["A1q0"], w["A1q1"] = q[:, :512], q[:, 512:]
    w["A1kv"] = np.concatenate([halves(qkv[:, 1024:1280], 4, 64, 4), qkv[:, 1280:]], axis=1)
    w["A1o0"], w["A1o1"] = i["L1_attn_w_out"][:512], i["L1_attn_w_out"][512:]
    for n, k in (("ki", "k_img_w"), ("vi", "v_img_w"), ("k", "k_w"), ("v", "v_w"), ("q", "q_w"), ("o", "o_w")):
        w["X1" + n] = i["L1_xattn_" + k].T

    f32 = np.float32
    small = np.zeros((P, 100), f32)

    def by_block(name, v):
        small[:, COL[name]:COL[name] + v.size // P] = v.reshape(-1, P).T

    gu = i["L0_ffn_gate_up_proj_bias"]
    by_block("gb", np.ascontiguousarray(gu[:, 0::2]))
    by_block("ub", np.ascontiguousarray(gu[:, 1::2]))
    for name, key in (("gam", "L1_attn_gamma"), ("wq", "L1_xattn_norm_q_w"), ("wk", "L1_xattn_norm_k_w"),
                      ("wki", "L1_xattn_norm_k_img_w")):
        by_block(name, i[key])
    small[0, COL["img"]] = 1
    small[1:, COL["txt"]] = 1
    small[:8, COL["rb"]] = i["L0_ffn_router_bias"]
    small[:, COL["half"]], small[:, COL["mhalf"]], small[:, COL["mone"]] = 0.5, -0.5, -1.0
    for j in range(4):
        small[32 * j:32 * j + 32, COL["hm"] + j] = 1
    small[:, COL["iota"]:COL["iota"] + 8] = np.arange(8)
    pattern = np.zeros((4, SC), f32)
    pattern[0:2, :IMG] = 1
    pattern[2:4, IMG:] = 1
    bdmask = np.zeros((P, P), f32)
    for j in range(4):
        bdmask[32 * j:32 * j + 32, 32 * j:32 * j + 32] = 1
    down_bias = np.zeros((P, 512), f32)
    down_bias[:NE] = i["L0_ffn_down_proj_bias"]
    rows = lambda v: np.ascontiguousarray(np.broadcast_to(v, (P, 512)))
    return {
        "x": i["x"].reshape(NT, P, D), "ctxT": np.ascontiguousarray(
            i["ctx_2048"].transpose(0, 2, 1).reshape(B, KB, P, SC).transpose(0, 2, 1, 3)),
        "weights": np.stack([chunk(np.ascontiguousarray(w[n])) for n in CHUNKS]),
        "small": small, "pattern": pattern, "bdmask": bdmask, "down_bias": down_bias,
        "rope0": rope_table(32, 8), "rope1": rope_table(64, 4),
        "bg": rows(i["L0_xattn_bg"]), "q_b": rows(i["L1_xattn_q_b"]), "o_b": rows(i["L1_xattn_o_b"]),
        "k_b": rows(i["L1_xattn_k_b"]), "v_b": rows(i["L1_xattn_v_b"]),
        "ki_b": rows(i["L1_xattn_k_img_b"]), "vi_b": rows(i["L1_xattn_v_img_b"]),
    }


def build(arrays, upto=6, make=None):
    noted = None
    for _ in range(2):
        nc = make()
        args = {n: nc.dram_tensor(n + "_in", v.shape, F32, kind="ExternalInput").ap() for n, v in arrays.items()}
        out = nc.dram_tensor("out_0_dram", (NT, P, D), F32, kind="ExternalOutput").ap()
        counts = Counts(noted)
        decoder(nc, args, out, counts, upto)
        assert noted is None or noted == counts.at
        noted = counts.at
    return nc


def kernel(**inputs):
    import concourse.bacc as bacc
    from concourse.bass_utils import run_bass_kernel_spmd

    arrays = laid_out({k: np.asarray(v) for k, v in inputs.items()})
    nc = build(arrays, make=lambda: bacc.Bacc("TRN2", target_bir_lowering=False, num_devices=1))
    r = run_bass_kernel_spmd(nc, [{n + "_in": v for n, v in arrays.items()}], core_ids=[0])
    return r.results[0]["out_0_dram"].reshape(B, S, D)
```

```python
from contextlib import ExitStack

import numpy as np

import concourse.bass as bass
from concourse import mybir

P = 128
F32, F32R, BF16, U32 = mybir.dt.float32, mybir.dt.float32r, mybir.dt.bfloat16, mybir.dt.uint32
ALU, ACT, AX = mybir.AluOpType, mybir.ActivationFunctionType, mybir.AxisListType

B, S, D = 2, 512, 512
NT = B * S // P
TB = NT // B
KB = D // P
SC = 1024
NC = SC // P
NH = 16
NE = 8
IMG = 257
MASKED = -1e30
SLOTS = 3
ALLB, LOW, MID, OUTB, HIGH = (0, 1, 2, 3, 4, 5, 6, 7), (0, 1), (2, 3), (2, 3, 0, 1), (4, 5, 6, 7)

CHUNKS = ["A0q", "A0k", "A0v", "A0o", "X0k", "X0v", "X0q", "X0g", "X0o", "F0r"]
CHUNKS += [f"F0{w}{e}" for e in range(NE) for w in "gud"]
CHUNKS += ["A1q0", "A1q1", "A1kv", "A1o0", "A1o1"]
CHUNKS += ["X1ki", "X1vi", "X1k", "X1v", "X1q", "X1o", "F1r", "F1h0"]
for _e in range(NE):
    CHUNKS += [f"F1h{_e + 1}", f"F1d{_e}"]
CHUNKS += [f"F1d{NE}"]
CI = {n: i for i, n in enumerate(CHUNKS)}

COL = dict(gb=0, ub=32, gam=64, wq=68, wk=72, wki=76, img=80, txt=81, rb=82, half=83, mhalf=84,
           mone=85, hm=88, iota=92, ub1=100)


def blocks_of(chunk):
    return 2 if chunk.startswith("F1d") else KB


class Counts:

    def __init__(self, noted=None):
        self.noted, self.now, self.at = noted, {}, {}

    def mark(self, name, key, by):
        self.now[name] = self.now.get(name, 0) + by
        self.at[(name, key)] = self.now[name]

    def place(self, name, key, value):
        assert (name, key) not in self.at, (name, key)
        self.at[(name, key)] = value

    def value(self, name, key):
        return 1 if self.noted is None else self.noted[(name, key)]


def decoder(nc, a, out, counts):
    with ExitStack() as ctx:
        def sbuf(name, shape, dtype=F32):
            return ctx.enter_context(nc.sbuf_tensor(name, shape, dtype))

        sems = {}

        def sem(name):
            if name not in sems:
                sems[name] = ctx.enter_context(nc.semaphore(name))
            return sems[name]

        X = sbuf("X", [P, NT, D])
        XT = sbuf("XT", [P, 2, KB, B * S], F32R)
        WR = sbuf("WR", [P, SLOTS, 2, KB, 512], F32R)
        RAW = sbuf("RAW", [P, KB, 512])
        QS = sbuf("QS", [P, 8, 512], F32R)
        KS = sbuf("KS", [P, 8, 1024], F32R)
        SRC = sbuf("SRC", [P, 4, 2, 512], F32R)
        PB = sbuf("PB", [P, 8, 512])
        VB = sbuf("VB", [P, 2, 1152])
        XN = sbuf("XN", [P, 2, 512])
        NB = sbuf("NB", [P, 2, 512])
        MR = sbuf("MR", [P, 512])
        ident = sbuf("ident", [P, P])
        identb = sbuf("identb", [P, P], BF16)
        mask_qk = sbuf("mask_qk", [P, P], BF16)
        mask_kq = sbuf("mask_kq", [P, P], BF16)
        ones = sbuf("ones", [P, 64])
        onesm = sbuf("onesm", [P, 2, 32])
        small = sbuf("small", [P, 160])
        mv = sbuf("mv", [P, NT, 2])
        st6 = sbuf("st6", [P, NT, 6])
        rs = sbuf("rs", [P, 4, NT])
        ss = sbuf("ss", [P, 8])
        nmx = sbuf("nmx", [P, 4, 4, 2, 3])
        MS = sbuf("MS", [P, 4, 4, 8], F32R)
        KI = sbuf("KI", [P, B, 2, 4], F32R)
        LG = sbuf("LG", [P, NT, 8])
        i8 = sbuf("i8", [P, NT, 8], U32)
        tw = sbuf("tw", [P, 3, NT])
        SCR = sbuf("SCR", [P, NT, 16])
        PS = [ctx.enter_context(nc.psum_tensor(f"bank{i}", [P, 512], F32)) for i in range(8)]

        def flat(t):
            return t.rearrange("p a n -> p (a n)")

        EV = [XN[:, 0, :], XN[:, 1, :], NB[:, 0, :], NB[:, 1, :]]
        Q2 = KS[:, 4:8, :].rearrange("p a (c n) -> p (a c) n", n=512)
        K1 = [KS[:, 0:4, :], SRC[:, :, :, :].rearrange("p a c n -> p a (c n)")]
        AG = QS[:, :, :].rearrange("p (h g) n -> p h g n", h=2)
        AH = KS[:, :, :].rearrange("p (b h c) n -> p b h (c n)", b=2, h=2)
        VX = VB.rearrange("p a n -> p (a n)")[:, 0:1040].rearrange("p (s g n) -> p s g n", s=2, g=4)
        BD = VB.rearrange("p a n -> p (a n)")[:, 1040:2096].rearrange("p (b g n) -> p b g n", b=2, g=4)

        def cs(name, i=0, n=1):
            return small[:, COL[name] + i:COL[name] + i + n]

        def dram(name, shape):
            return nc.dram_tensor(name, shape, F32, kind="Internal").ap()

        QD = {0: dram("q0_hl", (B, 2, 512, 512)), 1: dram("q1_hl", (B, 2, 1024, 512)), 2: dram("q2_hl", (B, 2, 512, 512))}
        KD = {0: dram("k0_hl", (B, 2, 512, 512)), 1: dram("k1_hl", (B, 2, 256, 512)), 2: dram("k2_hl", (B, 2, 512, 1024))}
        VD = {0: dram("v0_d", (B, 4, P, 512)), 1: dram("v1_d", (B, 4, P, 256)), 2: dram("v2_d", (B, 9, P, 512))}

        def mark(name, key, by=1):
            counts.mark(name, key, by)
            return sem(name), by

        def when(name, key):
            return sem(name), counts.value(name, key)

        bank_of, turns, opened, freed_keys = {}, {}, {}, set()

        def next_bank(key, ring):
            b = ring[turns.get(ring, 0) % len(ring)]
            turns[ring] = turns.get(ring, 0) + 1
            bank_of[key] = b
            opened[b] = opened.get(b, 0) + 1
            counts.place(f"freed{b}", key, opened[b])
            return sem(f"freed{b}"), opened[b] - 1

        def bank(key):
            return PS[bank_of[key]]

        def fills(key):
            return mark(f"filled{bank_of[key]}", key)

        def filled(key):
            return when(f"filled{bank_of[key]}", key)

        def frees(key):
            assert key not in freed_keys
            freed_keys.add(key)
            return sem(f"freed{bank_of[key]}"), 1

        def freed(key):
            return when(f"freed{bank_of[key]}", key)

        last_use = {}

        def w(chunk, lo=0, hi=512):
            return lambda hl, kb: WR[:, CI[chunk] % SLOTS, hl, kb, lo:hi]

        def load_chunk(sp, chunk):
            c, n = CI[chunk], blocks_of(chunk)
            if c:
                sp.wait_ge(*when("w_hi", CHUNKS[c - 1]))
                sp.wait_ge(*when("w_lo", CHUNKS[c - 1]))
            sp.dma_start(RAW[:, 0:n, :], a["weights"][c, :, 0:n * 512].rearrange("p (k n) -> p k n", k=n)).then_inc(
                *mark("raw", chunk, 16))

        def scaled(chunk):
            return chunk in ("A1q0", "A1q1", "A1kv")

        def split_hi(v, chunk):
            c, n = CI[chunk], blocks_of(chunk)
            v.wait_ge(*when("raw", chunk))
            if c >= SLOTS:
                v.wait_ge(*filled(last_use[CHUNKS[c - SLOTS]]))
            dst = WR[:, c % SLOTS, 0, 0:n, :]
            if scaled(chunk):
                for kb in range(n):
                    ins = v.tensor_scalar(dst[:, kb, :], RAW[:, kb, :], cs("gam", kb), None, ALU.mult)
            else:
                ins = v.tensor_copy(dst, RAW[:, 0:n, :])
            ins.then_inc(*mark("w_hi", chunk))
            if scaled(chunk):
                split_lo(v, chunk)

        def split_lo(eng, chunk):
            c, n = CI[chunk], blocks_of(chunk)
            eng.wait_ge(*when("w_hi", chunk))
            dst, hi = WR[:, c % SLOTS, 1, 0:n, :], WR[:, c % SLOTS, 0, 0:n, :].bitcast(F32)
            if scaled(chunk):
                for kb in range(n):
                    ins = eng.scalar_tensor_tensor(out=dst[:, kb, :], in0=RAW[:, kb, :], scalar=cs("gam", kb),
                                                   in1=hi[:, kb, :], op0=ALU.mult, op1=ALU.subtract)
            else:
                ins = eng.tensor_tensor(dst, RAW[:, 0:n, :], hi, ALU.subtract)
            ins.then_inc(sem("w_lo"), 1)
            counts.place("w_lo", chunk, c + 1)

        def split_lo_pool(pool, chunk):
            if not scaled(chunk):
                split_lo(pool, chunk)

        def product(pe, dst, lhs, rhs, blocks=KB, first=True, last=True):
            for kb in range(blocks):
                for n, (l, r) in enumerate(((0, 0), (0, 1), (1, 0))):
                    ins = pe.matmul(dst, lhs(l, kb), rhs(r, kb), start=first and kb == 0 and n == 0,
                                    stop=last and kb == blocks - 1 and n == 2)
            return ins

        def xt(b):
            return lambda hl, kb: XT[:, hl, kb, b * S:(b + 1) * S]

        def xtile(t):
            return lambda hl, kb: XT[:, hl, kb, t * P:(t + 1) * P]

        def grid(ps):
            return ps[:, :].rearrange("p (g n) -> p g n", g=KB)

        STAGES = ["A0", "X0", "F0", "A1", "X1", "F1"]
        before = dict(zip(STAGES[1:], STAGES))
        tiles = lambda b: range(b * TB, (b + 1) * TB)
        xt_last = {}

        def ln_tile(s, t):
            if s == "X1":
                return VB[:, 0, t % 2 * 512:t % 2 * 512 + 512]
            return XN[:, t % 2, :] if s == "A0" else PB[:, (2 if s == "F0" else 6) + t % 2, :]

        def ln_turn(pe, s, t, ring=ALLB):
            pe.wait_ge(*when("xn", (s, t)))
            pe.wait_ge(*next_bank((s, "T", t), ring))
            ps = bank((s, "T", t))
            for g in range(KB):
                ins = pe.transpose(ps[:, g * P:(g + 1) * P], ln_tile(s, t)[:, g * P:(g + 1) * P], ident[:])
            ins.then_inc(*fills((s, "T", t)))

        def ln_pe(pe, s, b, ring=ALLB):
            for t in tiles(b):
                ln_turn(pe, s, t, ring)

        def ln_hi(act, s, t):
            if s in before and t % TB == 0:
                act.wait_ge(*filled(xt_last[(before[s], t // TB)]))
            act.wait_ge(*filled((s, "T", t)))
            ps = bank((s, "T", t))
            act.activation(XT[:, 0, :, t * P:(t + 1) * P], grid(ps), ACT.Copy).then_inc(*mark("hi", (s, "T", t)))

        def ln_act(act, s, b):
            for t in tiles(b):
                ln_hi(act, s, t)

        x_key = {t: (f"x_in{t}", t) for t in range(NT)}

        def ln_stats(v, s, b):
            for t in tiles(b):
                v.wait_ge(*when(*x_key[t]))
                v.bn_stats(st6[:, t, :], X[:, t, :]).then_inc(*mark("bn", (s, t)))
            for t in tiles(b):
                v.wait_ge(*when("bn", (s, t)))
                v.bn_aggr(mv[:, t, :], st6[:, t, :]).then_inc(*mark("mv", (s, t)))

        def ln_xn(v, s, t):
            v.wait_ge(*when("rs", (s, t // TB)))
            v.wait_ge(*when("mv", (s, t)))
            if t >= 2:
                v.wait_ge(*filled((s, "T", t - 2)))
            v.tensor_scalar(ln_tile(s, t), X[:, t, :], mv[:, t, 0:1], rs[:, 0, t:t + 1],
                            ALU.subtract, ALU.mult).then_inc(*mark("xn", (s, t)))

        def ln_lo(v, s, t):
            v.wait_ge(*when("hi", (s, "T", t)))
            v.wait_ge(*filled((s, "T", t)))
            ps = bank((s, "T", t))
            v.tensor_tensor(XT[:, 1, :, t * P:(t + 1) * P], grid(ps), XT[:, 0, :, t * P:(t + 1) * P].bitcast(F32),
                            ALU.subtract).then_inc(*frees((s, "T", t)))

        def ln_dve(v, s, b):
            for t in tiles(b):
                ln_xn(v, s, t)
                if t % TB:
                    ln_lo(v, s, t - 1)
            ln_lo(v, s, (b + 1) * TB - 1)

        def ln_pool(pool, s, b):
            tt = slice(b * TB, (b + 1) * TB)
            pool.wait_ge(*when("mv", (s, (b + 1) * TB - 1)))
            var = mv[:, tt, 1]
            half, mhalf, mone = (cs(n).broadcast_to([P, TB]) for n in ("half", "mhalf", "mone"))

            def link(n, ins):
                ins.then_inc(*mark("rs_step", (s, b, n)))
                pool.wait_ge(*when("rs_step", (s, b, n)))

            link(0, pool.tensor_scalar(rs[:, 1, tt], var, 1e-5, None, ALU.add))
            if s != "A1":
                pool.tensor_tensor(rs[:, 0, tt], rs[:, 1, tt], mhalf, ALU.pow).then_inc(*mark("rs", (s, b)))
                return
            link(1, pool.tensor_tensor(rs[:, 0, tt], rs[:, 1, tt], mhalf, ALU.pow))
            link(2, pool.tensor_scalar(rs[:, 2, tt], var, float(D), None, ALU.mult))
            link(3, pool.tensor_tensor(rs[:, 3, tt], rs[:, 2, tt], half, ALU.pow))
            link(4, pool.tensor_tensor(rs[:, 2, tt], rs[:, 3, tt], rs[:, 0, tt], ALU.mult))
            link(5, pool.tensor_scalar(rs[:, 3, tt], rs[:, 2, tt], 1e-12, None, ALU.max))
            link(6, pool.tensor_tensor(rs[:, 2, tt], rs[:, 3, tt], mone, ALU.pow))
            link(7, pool.tensor_tensor(rs[:, 3, tt], rs[:, 2, tt], rs[:, 0, tt], ALU.mult))
            pool.tensor_scalar(rs[:, 0, tt], rs[:, 3, tt], float(D) ** 0.5, None, ALU.mult).then_inc(
                *mark("rs", (s, b)))

        def ln_ready(pe, s, b):
            for t in tiles(b):
                pe.wait_ge(*freed((s, "T", t)))

        def add_to_x(v, t, key, scale=None):
            v.wait_ge(*filled(key))
            ps = bank(key)
            v.wait_ge(*when(*x_key[t]))
            if scale is None:
                ins = v.tensor_tensor(X[:, t, :], ps[:, :], X[:, t, :], ALU.add)
            else:
                ins = v.scalar_tensor_tensor(out=X[:, t, :], in0=ps[:, :], scalar=scale, in1=X[:, t, :],
                                             op0=ALU.mult, op1=ALU.add)
            ins.then_inc(*frees(key))
            x_key[t] = (f"freed{bank_of[key]}", key)

        NX = B * NH // 2
        LAG = 2
        HI_AT = 4
        CHUNK_AT = ({-1: "X0k", 3: "X0v"}, {1: "A1o0", 5: "A1o1", 10: "X1ki"}, {-1: "X1o", 2: "F1r", 8: "F1h0"})
        POOL_CHUNK_AT = ({0: "X0k", 2: "X0v"}, {1: "A1o0", 5: "A1o1", 10: "X1ki"}, {0: "X1o", 1: "F1r", 4: "F1h0"})
        OUT_AFTER = {NX // 2 + 1: 0, NX: 1}
        CFG = {0: dict(st="A0", nk=512, scale=32 ** -0.5, o=["A0o"]),
               1: dict(st="A1", nk=512, scale=64 ** -0.5, o=["A1o0", "A1o1"]),
               2: dict(st="X1", nk=1024, scale=32 ** -0.5, o=["X1o"])}

        def steps(at):
            return [(kt, jj) for kt in range(CFG[at]["nk"] // P) for jj in range(2)]

        def max_products(at):
            return [(i, jj, h) for i in range(4) for jj in range(2) for h in range(2 if at == 2 else 1)]

        def group(at, x):
            return x if at == 1 else x // 2

        def group_end(at, x):
            return at == 1 or x % 2 == 1

        def slot(x, jj):
            return x % 4 * 2 + jj

        def kslot(at, x, jj):
            return (K1[x // 8], (2 * x + jj) % 4) if at == 1 else (KS, slot(x, jj))

        def pb_slot(at, x, n):
            return (x * len(steps(at)) + n) % 8

        def at_pe_max(pe, at, x, prods):
            st = CFG[at]["st"]
            for i, jj, h in prods:
                if (i, jj, h) == (0, 0, 0):
                    pe.wait_ge(*when(f"stack{x % 4}", (at, x)))
                    if at == 1 and x % 8 == 0:
                        pe.wait_ge(*when(f"kstack{x // 8}", (at, x // 8)))
                key = (st, "max", x, i, jj, h)
                pe.wait_ge(*next_bank(key, LOW))
                ps = bank(key)
                kt_, ki = kslot(at, x, jj)
                n0, n = (h * 512, 512) if at == 2 else (0, (i + 1) * P)
                q = slice(i * P, (i + 1) * P)
                if at == 1:
                    pe.matmul(ps[:, 0:n], QS[:, slot(x, jj), q], kt_[:, ki, 0:n], start=True, stop=False)
                    ins = pe.matmul(ps[:, 0:n], Q2[0:64, slot(x, jj), q], kt_[0:64, ki, 512:512 + n], start=False, stop=False)
                else:
                    ins = pe.matmul(ps[:, 0:n], QS[0:96, slot(x, jj), q], kt_[0:96, ki, n0:n0 + n], start=True, stop=at == 2)
                if at != 2:
                    ins = pe.matmul(ps[:, i * P:n], identb[:], mask_qk[:], start=False, stop=True)
                ins.then_inc(*fills(key))

        def at_pe_turn(pe, at, x):
            key = (CFG[at]["st"], "mt", x)
            pe.wait_ge(*when("ms", (at, x)))
            n = 8 if at == 2 else 4
            pe.wait_ge(*next_bank(key, LOW))
            ps = bank(key)
            for i in range(4):
                ins = pe.transpose(ps[0:n, i * P:(i + 1) * P], MS[:, x % 4, i, 0:n].bitcast(F32), ident[:])
            ins.then_inc(*fills(key))

        def at_pe_scores(pe, at, x, n):
            st, (kt, jj) = CFG[at]["st"], steps(at)[n]
            if n == 0:
                pe.wait_ge(*when(f"mrow{x % 4}", (at, x)))
                if x == 0:
                    pe.wait_ge(*when(("key_rows_a0", "key_rows_a1", "key_rows_x1")[at], 0))
                if at == 1 and x == NX // 2:
                    pe.wait_ge(*when("key_rows_a1b", 0))
            key = (st, "s", x, n)
            pe.wait_ge(*next_bank(key, MID))
            ps = bank(key)
            c0 = 0 if at == 2 else kt * P
            kt_, ki = kslot(at, x, jj)
            k, q = slice(kt * P, (kt + 1) * P), slice(c0, 512)
            if at == 1:
                pe.matmul(ps[:, q], kt_[:, ki, k], QS[:, slot(x, jj), q], start=True, stop=False)
                ins = pe.matmul(ps[:, q], kt_[0:66, ki, 512 + kt * P:512 + (kt + 1) * P], Q2[0:66, slot(x, jj), q],
                                start=False, stop=False)
            else:
                rows = 100 if at == 2 else 98
                ins = pe.matmul(ps[:, q], kt_[0:rows, ki, k], QS[0:rows, slot(x, jj), q], start=True, stop=at == 2)
            if at != 2:
                ins = pe.matmul(ps[:, c0:c0 + P], identb[:], mask_kq[:], start=False, stop=True)
            ins.then_inc(*fills(key))

        acc = {}

        def at_pe_values(pe, at, x, n):
            st, (kt, jj) = CFG[at]["st"], steps(at)[n]
            gx, last_kt = group(at, x), CFG[at]["nk"] // P - 1
            new_group = at == 1 or x % 2 == 0
            if n == 0 and new_group:
                if at == 1:
                    if x % 8 == 0:
                        pe.wait_ge(*when(f"vb{x // 8}", (at, x // 8)))
                else:
                    pe.wait_ge(*when(f"vb{gx % 2}", (at, gx)))
            names = {0: [("o", (4,)), ("l", (5,))], 4: [("o2", (6,)), ("l2", (7,))]} if at == 2 else \
                {0: [("o", (4, 6)), ("l", (5, 7))]}
            if new_group:
                for name, ring in names.get(n, []):
                    pe.wait_ge(*next_bank((st, name, gx), ring))
                    acc[name] = bank((st, name, gx))
            pe.wait_ge(*freed((st, "s", x, n)))
            c0 = 0 if at == 2 else kt * P
            prob = PB[:, pb_slot(at, x, n), c0:512]
            width = 64 if at == 1 else 32
            r0 = 64 * jj if at == 1 else 32 * ((2 * x + jj) % 4)
            if at == 2:
                parts = [("", kt, kt == 0, False, ones[:, 0:32])] if kt < 2 else \
                    [("2", kt + 1, False, kt == last_kt, ones[:, 0:32])] if kt > 2 else \
                    [("", 2, False, True, onesm[:, 0, :]), ("2", 3, True, False, onesm[:, 1, :])]
            else:
                parts = [("", kt, kt == 0, kt == last_kt, ones[:, 0:width])]
            l0 = (r0 + 64) % P
            for suffix, vt, first, last, one in parts:
                if at == 1:
                    v = VB[:, x // 8, vt * 256 + (2 * x + jj) % 4 * 64:vt * 256 + (2 * x + jj) % 4 * 64 + 64]
                else:
                    v = VB[:, gx % 2, vt * P + r0:vt * P + r0 + 32]
                pe.matmul(acc["o" + suffix][r0:r0 + width, c0:512], v, prob, start=first, stop=last)
                ins = pe.matmul(acc["l" + suffix][l0:l0 + width, c0:512], one, prob, start=first, stop=last)
            ins.then_inc(*mark("pv", (at, x, n)))

        def at_out(at, b):
            return [(CFG[at]["st"], "y", t, part) for part in range(len(CFG[at]["o"])) for t in tiles(b)]

        def at_pe_out(pe, at, b):
            chunks = CFG[at]["o"]
            pe.wait_ge(*when("att_lo", (at, NX // 2 * (b + 1) - 1 if at == 1 else NX // 4 * (b + 1) - 1)))
            for key in at_out(at, b):
                _, _, t, part = key
                pe.wait_ge(*when("w_hi", chunks[part]))
                pe.wait_ge(*when("w_lo", chunks[part]))
                pe.wait_ge(*next_bank(key, OUTB))
                ps = bank(key)
                half = t % TB * P + (part if at == 1 else b) * S
                product(pe, ps[:, :], lambda hl, kb: XT[:, hl, kb, half:half + P], w(chunks[part])).then_inc(
                    *fills(key))
                last_use[chunks[part]] = key
                xt_last[(CFG[at]["st"], b)] = key
            if at == 1:
                xt_last[("A1", 0)] = key

        def at_pe(pe, at):
            N, M = len(steps(at)), len(max_products(at))
            for x in range(-2, NX + 1):
                prods = max_products(at) if x + 2 < NX else []
                if 0 <= x < NX:
                    for n in range(N):
                        at_pe_scores(pe, at, x, n)
                        if n >= LAG:
                            at_pe_values(pe, at, x, n - LAG)
                        at_pe_max(pe, at, x + 2, prods[n * M // N:(n + 1) * M // N])
                        if n == 3 and x + 1 < NX:
                            at_pe_turn(pe, at, x + 1)
                    for n in range(N - LAG, N):
                        at_pe_values(pe, at, x, n)
                else:
                    early = M // 2 if x == -1 else 0
                    at_pe_max(pe, at, x + 2, prods[:early])
                    if x == -1:
                        at_pe_turn(pe, at, 0)
                    at_pe_max(pe, at, x + 2, prods[early:])
                if at == 2 and x == NX:
                    ln_pe(pe, "F1", 0, OUTB)
                if x in OUT_AFTER:
                    at_pe_out(pe, at, OUT_AFTER[x])

        def at_dve_max(v, at, x, prods):
            for i, jj, h in prods:
                key = (CFG[at]["st"], "max", x, i, jj, h)
                v.wait_ge(*filled(key))
                ps = bank(key)
                cut = [(0, IMG, 0), (IMG, 512, 1)] if at == 2 and h == 0 else [(0, 512, 2)] if at == 2 else [(0, (i + 1) * P, 0)]
                for lo, hi, c in cut:
                    ins = v.tensor_reduce(nmx[:, x % 4, i, jj, c:c + 1], ps[:, lo:hi], AX.X, ALU.max)
                ins.then_inc(*frees(key))

        def at_dve_minus(v, at, x):
            slot_ = x % 4
            for jj in range(2):
                for h in range(2 if at == 2 else 1):
                    v.wait_ge(*freed((CFG[at]["st"], "max", x, 3, jj, h)))
            kinds = 1
            if at == 2:
                kinds = 2
                v.tensor_tensor(nmx[:, slot_, :, :, 1], nmx[:, slot_, :, :, 1], nmx[:, slot_, :, :, 2], ALU.max).then_inc(
                    *mark("nmax", (at, x)))
                v.wait_ge(*when("nmax", (at, x)))
            for k in range(kinds):
                ins = v.tensor_scalar(MS[:, slot_, :, 4 * k:4 * k + 2], nmx[:, slot_, :, :, k], -1.0, None, ALU.mult)
            ins.then_inc(*mark("ms_hi", (at, x)))
            v.wait_ge(*when("ms_hi", (at, x)))
            for k in range(kinds):
                ins = v.scalar_tensor_tensor(out=MS[:, slot_, :, 4 * k + 2:4 * k + 4], in0=nmx[:, slot_, :, :, k], scalar=-1.0,
                                             in1=MS[:, slot_, :, 4 * k:4 * k + 2].bitcast(F32), op0=ALU.mult, op1=ALU.subtract)
            ins.then_inc(*mark("ms", (at, x)))

        def ev(at, gx):
            return [(EV[0], EV[1]), (EV[2], EV[3])] if at == 2 else [(EV[gx % 2 * 2], EV[gx % 2 * 2 + 1])]

        def at_dve_norm(v, at, gx, n, piece):
            l = ev(at, gx)[n][1][:, piece * P:(piece + 1) * P]
            v.wait_ge(*freed((CFG[at]["st"], "l" + "2" * n, gx)))
            v.reciprocal(l, l).then_inc(*mark("rcp", (at, gx, n)))

        def at_pool_norm(pool, at, gx):
            pairs = ev(at, gx)
            for n, (o, l) in enumerate(pairs):
                pool.wait_ge(*when("rcp", (at, gx, n)))
                pool.wait_ge(*freed((CFG[at]["st"], "o" + "2" * n, gx)))
                pool.tensor_tensor(o, o, l, ALU.mult).then_inc(
                    *mark("att" if len(pairs) == 1 else "att_part", (at, gx, n)))
            if at == 2:
                pool.wait_ge(*when("att_part", (at, gx, 1)))
                pool.tensor_tensor(pairs[0][0], pairs[0][0], pairs[1][0], ALU.add).then_inc(*mark("att", (at, gx, 0)))
            pool.wait_ge(*when("hi", (at, "att", gx)))
            pool.tensor_tensor(at_dst(at, gx, 1), pairs[0][0], at_dst(at, gx, 0).bitcast(F32), ALU.subtract).then_inc(
                *mark("att_lo", (at, gx)))

        def at_dst(at, gx, hl):
            if at == 1:
                g = gx % 8
                return XT[:, hl, g % 4, g // 4 * S:(g // 4 + 1) * S]
            return XT[:, hl, gx % 4, gx // 4 * S:(gx // 4 + 1) * S]

        def at_act_hi(act, at, gx):
            act.wait_ge(*when("att", (at, gx, 0)))
            if gx == 0:
                for b in range(B):
                    act.wait_ge(*filled(proj_last[(at, b)]))
            if at == 1 and gx == 8:
                act.wait_ge(*filled(at_out(at, 0)[-1]))
            act.activation(at_dst(at, gx, 0), ev(at, gx)[0][0], ACT.Copy).then_inc(*mark("hi", (at, "att", gx)))

        proj_last = {}

        def at_act(act, at):
            st, N = CFG[at]["st"], len(steps(at))
            for x in range(-2, NX + 1):
                def turn():
                    key = (st, "mt", x + 1)
                    act.wait_ge(*filled(key))
                    ps = bank(key)
                    if x + 1 > 0:
                        act.wait_ge(*when(f"mrow{x % 4}", (at, x)))
                    n = 8 if at == 2 else 4
                    act.activation(MR[0:n, :], ps[0:n, :], ACT.Copy).then_inc(*frees(key))

                def sums(x, k, part):
                    gx, sfx = group(at, x), "2" * k
                    back = gx - 1 if at == 2 else gx - 2
                    if back >= 0:
                        act.wait_ge(*when("att_lo", (at, back)))
                    act.wait_ge(*when("pv", (at, x, 5 if (at, k) == (2, 0) else N - 1)))
                    o, l = ev(at, gx)[k]
                    if part == "o":
                        act.activation(o, bank((st, "o" + sfx, gx))[:, :], ACT.Copy).then_inc(
                            *frees((st, "o" + sfx, gx)))
                        return
                    ps = bank((st, "l" + sfx, gx))
                    act.activation(l[0:64, :], ps[64:P, :], ACT.Copy)
                    act.activation(l[64:P, :], ps[0:64, :], ACT.Copy).then_inc(*frees((st, "l" + sfx, gx)))

                if x == -1:
                    turn()
                if 0 <= x < NX:
                    for n in range(N):
                        kt, jj = steps(at)[n]
                        c0 = 0 if at == 2 else kt * P
                        act.wait_ge(*filled((st, "s", x, n)))
                        ps = bank((st, "s", x, n))
                        if x * N + n >= 8:
                            back = x * N + n - 8
                            act.wait_ge(*when("pv", (at, back // N, back % N)))
                        act.activation(PB[:, pb_slot(at, x, n), c0:512], ps[:, c0:512], ACT.Exp,
                                             scale=CFG[at]["scale"]).then_inc(*frees((st, "s", x, n)))
                        if n == 3 and x + 1 < NX:
                            turn()
                        if n in (1, 2) and x and group_end(at, x - 1):
                            sums(x - 1, at // 2, "lo"[n - 1])
                        if n == HI_AT and x > 1 and group_end(at, x - 2):
                            at_act_hi(act, at, group(at, x - 2))
                        if n in (8, 9) and at == 2 and group_end(at, x):
                            sums(x, 0, "lo"[n - 8])
                elif x == NX:
                    if group_end(at, x - 2):
                        at_act_hi(act, at, group(at, x - 2))
                    for part in "lo":
                        sums(x - 1, at // 2, part)
                    at_act_hi(act, at, group(at, x - 1))
                    if at == 2:
                        ln_act(act, "F1", 0)

        def at_dve(v, at):
            for x in range(-2, NX + 1):
                prods = max_products(at) if x + 2 < NX else []
                M = len(prods)
                norms = {}
                for piece in range(4):
                    if x > 0 and group_end(at, x - 1):
                        norms.setdefault((piece + 3) * M // 7, []).append((group(at, x - 1), at // 2, piece))
                    if at == 2 and 0 < x < NX and group_end(at, x):
                        norms.setdefault((piece + 5) * M // 8, []).append((group(at, x), 0, piece))
                for n in range(M + 1):
                    for gx, k, piece in norms.get(n, []):
                        at_dve_norm(v, at, gx, k, piece)
                    at_dve_max(v, at, x + 2, prods[n:n + 1])
                if prods:
                    at_dve_minus(v, at, x + 2)
                if x in CHUNK_AT[at]:
                    split_hi(v, CHUNK_AT[at][x])
                if at == 2 and x == NX - 1:
                    ln_stats(v, "F1", 0)
                if at == 2 and x == NX:
                    ln_dve(v, "F1", 0)
                if x in OUT_AFTER:
                    for key in at_out(at, OUT_AFTER[x]):
                        add_to_x(v, key[2], key)
                        if key == ("A1", "y", NT - 1, 0):
                            split_hi(v, "X1vi")

        def at_pool(pool, at):
            for gx in range(NX if at == 1 else NX // 2):
                if gx in POOL_CHUNK_AT[at]:
                    split_lo_pool(pool, POOL_CHUNK_AT[at][gx])
                if (at, gx) == (2, NX // 2 - 1):
                    ln_pool(pool, "F1", 0)
                at_pool_norm(pool, at, gx)

        def src_order(at):
            if at == 2:
                return []
            return [(T, b, 2 * mp + h) for T, b, mp in rope_pairs(at) for h in range(2)]

        def rope_pairs(at):
            return [(T, b, m // 2) for T, _, ms in PROJ[at] for b in range(B) for m, _ in ms[::2]]

        PROJ = {0: [("q", "A0q", [(m, m * P) for m in range(4)]), ("k", "A0k", [(m, m * P) for m in range(4)])],
                1: [("q", "A1q0", [(m, m * P) for m in range(4)]), ("q", "A1q1", [(m + 4, m * P) for m in range(4)]),
                    ("k", "A1kv", [(m, m * P) for m in range(2)])]}
        VPROJ = {0: ("A0v", 0, 512), 1: ("A1kv", 256, 512)}

        def src_slot(at, T, b, m):
            return src_order(at).index((T, b, m)) % 4

        def wait_stored(eng, at, T, b):
            if T == "v":
                if at == 2:
                    for c, (jb, tt, kind) in enumerate(JOBS):
                        if jb == b:
                            eng.wait_ge(*when(f"v_stored{c % 2}", (2, c)))
                else:
                    for t in tiles(b):
                        eng.wait_ge(*when(f"v_stored{t % 4}", (at, t)))
            elif at == 2:
                for c, (jb, tt, kind) in enumerate(JOBS + QJOBS):
                    if jb == b and (kind == "q") == (T == "q") and (tt, kind) != (2, "i"):
                        eng.wait_ge(*when(f"src_stored{2 + c % 2}", (2, c)))
            else:
                for (T_, b_, m) in src_order(at):
                    if (T_, b_) == (T, b):
                        eng.wait_ge(*when(f"src_stored{src_slot(at, T, b, m)}", (at, T, b, m)))

        def at_sp_stack(sp, at, x):
            b, h0 = x // 8, x % 8 * 2
            if x >= 4:
                sp.wait_ge(*filled((CFG[at]["st"], "s", x - 4, len(steps(at)) - 1)))
            if x % 8 == 0:
                wait_stored(sp, at, "q", b)
                wait_stored(sp, at, "k", b)
            s0, hd = slot(x, 0), 64 if at == 1 else 32

            def heads(t, hl, h, n):
                return t[b, hl, h * hd:(h + n) * hd, :].rearrange("(h r) t -> r h t", h=n)

            if at == 1:
                if x % 8 == 0:
                    for dst, src in [
                        (K1[b][0:64, :, 0:512].bitcast(F32), heads(KD[1], 0, 0, 4)),
                        (K1[b][64:128, :, 0:512].bitcast(F32), heads(KD[1], 1, 0, 4)),
                        (K1[b][0:64, :, 512:1024].bitcast(F32), heads(KD[1], 0, 0, 4))]:
                        sp.dma_start(dst, src).then_inc(*mark(f"kstack{b}", (at, b), 16))
                for dst, src in [
                    (QS[0:64, s0:s0 + 2, :].bitcast(F32), heads(QD[1], 0, h0, 2)),
                    (QS[64:128, s0:s0 + 2, :].bitcast(F32), heads(QD[1], 0, h0, 2)),
                    (Q2[0:64, s0:s0 + 2, :].bitcast(F32), heads(QD[1], 1, h0, 2))]:
                    sp.dma_start(dst, src).then_inc(*mark(f"stack{x % 4}", (at, x), 16))
                return
            nk = CFG[at]["nk"]
            for dst, src in ([(QS[32 * n:32 * n + 32, s0:s0 + 2, :].bitcast(F32), heads(QD[at], hl, h0, 2)) for n, hl in enumerate((0, 0, 1))]
                 + [(KS[32 * n:32 * n + 32, s0:s0 + 2, 0:nk].bitcast(F32), heads(KD[at], hl, h0, 2)) for n, hl in enumerate((0, 1, 0))]):
                sp.dma_start(dst, src).then_inc(*mark(f"stack{x % 4}", (at, x), 16))

        def at_sp_values(sp, at, x):
            b = x // 8
            if at == 1:
                if x % 8 == 0:
                    wait_stored(sp, at, "v", b)
                    sp.dma_start(VB[:, b, 0:1024].rearrange("p (k n) -> p k n", k=4), VD[1][b].rearrange("k p n -> p k n")).then_inc(
                        *mark(f"vb{b}", (at, b), 16))
            elif x % 2 == 0:
                gx = x // 2
                if x % 8 == 0:
                    wait_stored(sp, at, "v", b)
                if gx >= 2:
                    sp.wait_ge(*when("pv", (at, x - 3, len(steps(at)) - 1)))
                nv = 9 if at == 2 else 4
                sp.dma_start(VB[:, gx % 2, 0:nv * P].rearrange("p (k n) -> p k n", k=nv), VD[at][b, :, :, gx % 4 * P:(gx % 4 + 1) * P].rearrange("k p n -> p k n")).then_inc(
                    *mark(f"vb{gx % 2}", (at, gx), 16))

        def at_sp_rows(sp, at, x):
            s0 = slot(x, 0)
            sp.wait_ge(*freed((CFG[at]["st"], "mt", x)))
            dst, r0 = (Q2, 64) if at == 1 else (QS, 96)
            for dst, src in ([(dst[r0 + r:r0 + r + 1, s0:s0 + 2, :].bitcast(F32), MR[2 * r:2 * r + 2, :])
                                               for r in range(4 if at == 2 else 2)]):
                sp.dma_start(dst, src).then_inc(*mark(f"mrow{x % 4}", (at, x), 16))

        def at_sp(sp, at):
            for x in range(-3, NX):
                if (0 if at == 2 else 1) < x + 3 < NX:
                    at_sp_stack(sp, at, x + 3)
                if 0 <= x + 1 < NX:
                    at_sp_values(sp, at, x + 1)
                    at_sp_rows(sp, at, x + 1)
                if x + 2 in CHUNK_AT[at]:
                    load_chunk(sp, CHUNK_AT[at][x + 2])

        def qkv_pe(pe, at):
            st = CFG[at]["st"]
            for T, chunk, ms in PROJ[at]:
                pe.wait_ge(*when("w_hi", chunk))
                pe.wait_ge(*when("w_lo", chunk))
                for b in range(B):
                    if (chunk, b) == (PROJ[at][0][1], 1):
                        ln_pe(pe, st, 1)
                    ln_ready(pe, st, b)
                    for m, col in ms:
                        key = (st, T, b, m)
                        pe.wait_ge(*next_bank(key, ALLB))
                        ps = bank(key)
                        product(pe, ps[:, :], w(chunk, col, col + P), xt(b)).then_inc(*fills(key))
                        last_use[chunk] = key
            chunk, lo, hi = VPROJ[at]
            pe.wait_ge(*when("w_hi", chunk))
            pe.wait_ge(*when("w_lo", chunk))
            for t in range(NT):
                key = (st, "v", t)
                pe.wait_ge(*next_bank(key, ALLB))
                ps = bank(key)
                product(pe, ps[:, 0:hi - lo], xtile(t), w(chunk, lo, hi)).then_inc(*fills(key))
                last_use[chunk] = key
                proj_last[(at, t // TB)] = key

        def rope(n, i):
            if n % 2 == 0:
                return PB[:, i, :]
            return NB[:, i - 6, :] if i >= 6 else flat(VB)[:, (i - 2) * 512:(i - 1) * 512]

        def qkv_dve(v, at, chunks_after):
            st = CFG[at]["st"]
            cos, sin = PB[:, 0, :], PB[:, 1, :]
            v.wait_ge(*when("rope_tables", at))
            pairs = rope_pairs(at)

            def lo(n):
                T, b, mp = pairs[n]
                for h in range(2):
                    sl = src_slot(at, T, b, 2 * mp + h)
                    v.wait_ge(*when("hi", (at, T, b, 2 * mp + h)))
                    v.tensor_tensor(SRC[:, sl, 1, :], rope(n, 6 + h), SRC[:, sl, 0, :].bitcast(F32), ALU.subtract).then_inc(
                        *mark("src_lo", (at, n, h)))

            for n, (T, b, mp) in enumerate(pairs):
                if n > 1:
                    v.wait_ge(*when("rope_sum", (at, n - 2, 1)))
                for h, (c, s_) in enumerate(((2, 4), (5, 3))):
                    key = (st, T, b, 2 * mp + h)
                    v.wait_ge(*filled(key))
                    ps = bank(key)
                    v.tensor_tensor(rope(n, c), ps[:, :], cos, ALU.mult)
                    v.tensor_tensor(rope(n, s_), ps[:, :], sin, ALU.mult).then_inc(*frees(key))
                if n:
                    lo(n - 1)
                if n + 1 == len(pairs) or pairs[n + 1][0] != T or (T == "q" and at == 1 and mp == 1 and b == 1):
                    for chunk in chunks_after.pop(0):
                        split_hi(v, chunk)
            lo(len(pairs) - 1)

        def qkv_pool(pool, at, chunks_after):
            st = CFG[at]["st"]
            pairs = rope_pairs(at)
            for n, (T, b, mp) in enumerate(pairs):
                for h in range(2):
                    pool.wait_ge(*freed((st, T, b, 2 * mp + h)))
                if n > 1:
                    pool.wait_ge(*when("src_lo", (at, n - 2, 1)))
                pool.tensor_tensor(rope(n, 6), rope(n, 2), rope(n, 3), ALU.subtract).then_inc(
                    *mark("rope_sum", (at, n, 0)))
                pool.tensor_tensor(rope(n, 7), rope(n, 4), rope(n, 5), ALU.add).then_inc(
                    *mark("rope_sum", (at, n, 1)))
                if n + 1 == len(pairs) or pairs[n + 1][0] != T or (T == "q" and at == 1 and mp == 1 and b == 1):
                    for chunk in chunks_after.pop(0):
                        split_lo_pool(pool, chunk)

        def qkv_act(act, at):
            st, order = CFG[at]["st"], src_order(at)
            for n, (T, b, m) in enumerate(order):
                act.wait_ge(*when("rope_sum", (at, n // 2, n % 2)))
                if n >= 4:
                    act.wait_ge(*when(f"src_stored{n % 4}", (at, *order[n - 4])))
                act.activation(SRC[:, n % 4, 0, :], rope(n // 2, 6 + n % 2), ACT.Copy).then_inc(
                    *mark("hi", (at, T, b, m)))
            width = VPROJ[at][2] - VPROJ[at][1]
            for t in range(NT):
                act.wait_ge(*filled((st, "v", t)))
                ps = bank((st, "v", t))
                if t >= 4:
                    act.wait_ge(*when(f"v_stored{t % 4}", (at, t - 4)))
                elif t == 2:
                    act.wait_ge(*when("src_lo", (at, len(order) // 2 - 1, 1)))
                act.activation(EV[t % 4][:, 0:width], ps[:, 0:width], ACT.Copy).then_inc(*frees((st, "v", t)))

        def qkv_sp(sp, at, loads):
            hd2 = CFG[at]["nk"] // 32 if at == 0 else 32
            for n, (T, b, m) in enumerate(src_order(at)):
                if n and src_order(at)[n - 1][:2] == ("k", 0) and b == 1:
                    at_sp_stack(sp, at, 0)
                sp.wait_ge(*when("src_lo", (at, n // 2, n % 2)))
                dram_t = (QD if T == "q" else KD)[at]
                heads = P // hd2
                rows = slice(m // 2 * heads * 2 * hd2, (m // 2 + 1) * heads * 2 * hd2)
                dst = lambda hl: dram_t[b, hl, rows, :].rearrange("(h c f) t -> c h f t", h=heads, c=2)[m % 2]
                for dst, src in ([(dst(hl), SRC[:, n % 4, hl, :].bitcast(F32)) for hl in range(2)]):
                    sp.dma_start(dst, src).then_inc(*mark(f"src_stored{n % 4}", (at, T, b, m), 16))
                if n in loads:
                    load_chunk(sp, loads[n])
            at_sp_stack(sp, at, 1)
            width = VPROJ[at][2] - VPROJ[at][1]
            for t in range(NT):
                sp.wait_ge(*freed((CFG[at]["st"], "v", t)))
                sp.dma_start(VD[at][t // TB, t % TB], EV[t % 4][:, 0:width]).then_inc(
                    *mark(f"v_stored{t % 4}", (at, t), 16))

        NCT = B * NC

        def x0_pe(pe):
            ctile = lambda c: (lambda hl, kb: SRC[:, c % 4, hl, kb * P:(kb + 1) * P])
            pe.wait_ge(*when("w_hi", "X0k"))
            pe.wait_ge(*when("w_lo", "X0k"))
            pe.wait_ge(*when("w_hi", "X0v"))
            pe.wait_ge(*when("w_lo", "X0v"))

            def summary(c):
                pe.wait_ge(*freed(("X0", "k", c)))
                pe.wait_ge(*freed(("X0", "v", c)))
                if c % NC == 0:
                    for g in range(KB):
                        pe.wait_ge(*next_bank(("X0", "kv", c // NC, g), (4 + g,)))
                        acc[g] = bank(("X0", "kv", c // NC, g))
                for g in range(KB):
                    ins = pe.matmul(acc[g][:, 0:130], PB[:, 4 + c % 2, g * P:(g + 1) * P], VX[:, c % 2, g, :],
                                    start=c % NC == 0, stop=c % NC == NC - 1)
                ins.then_inc(*mark("kv_step", c))

            for c in range(NCT + 1):
                if c < NCT:
                    pe.wait_ge(*when("ct_lo", ("X0", c)))
                    for T, ring, chunk in (("k", LOW, "X0k"), ("v", MID, "X0v")):
                        key = ("X0", T, c)
                        pe.wait_ge(*next_bank(key, ring))
                        ps = bank(key)
                        product(pe, ps[:, :], ctile(c), w(chunk)).then_inc(*fills(key))
                        last_use[chunk] = key
                    if 2 <= c < NT + 2:
                        ln_turn(pe, "X0", c - 2, MID)
                if c:
                    summary(c - 1)
            for b in range(B):
                ln_ready(pe, "X0", b)
                pe.wait_ge(*when("w_hi", "X0q"))
                pe.wait_ge(*when("w_lo", "X0q"))
                for m in range(KB):
                    key = ("X0", "q", b, m)
                    pe.wait_ge(*next_bank(key, LOW + MID))
                    ps = bank(key)
                    product(pe, ps[:, :], w("X0q", m * P, (m + 1) * P), xt(b)).then_inc(*fills(key))
                    last_use["X0q"] = key
                pe.wait_ge(*when("w_hi", "X0g"))
                pe.wait_ge(*when("w_lo", "X0g"))

                def gate(t):
                    key = ("X0", "g", t)
                    pe.wait_ge(*next_bank(key, LOW + MID))
                    ps = bank(key)
                    product(pe, ps[:, :], xtile(t), w("X0g")).then_inc(*fills(key))
                    last_use["X0g"] = xt_last[("X0", b)] = key

                def attend(t):
                    if t % TB == 0:
                        for g in range(KB):
                            pe.wait_ge(*freed(("X0", "q", b, g)))
                            pe.wait_ge(*freed(("X0", "kv", b, g)))
                    for h in range(2):
                        key = ("X0", "a", t, h)
                        pe.wait_ge(*next_bank(key, (4, 5, 6, 7)))
                        ps = bank(key)
                        for g in range(2):
                            ins = pe.matmul(ps[:, 132 * g:132 * g + 132], PB[:, 4 + 2 * h + g, t % TB * P:(t % TB + 1) * P],
                                            BD[:, b, 2 * h + g, :], start=True, stop=True)
                        ins.then_inc(*fills(key))

                def turn(t):
                    pe.wait_ge(*when("gated", t))
                    key = ("X0", "agT", t)
                    pe.wait_ge(*next_bank(key, (4, 5, 6, 7)))
                    ps = bank(key)
                    for g in range(KB):
                        ins = pe.transpose(ps[:, g * P:(g + 1) * P], XN[:, t % 2, g * P:(g + 1) * P], ident[:])
                    ins.then_inc(*fills(key))

                for t in tiles(b):
                    gate(t)
                    attend(t)
                    if t % TB:
                        turn(t - 1)
                turn(b * TB + TB - 1)
                if b == B - 1:
                    ln_pe(pe, "F0", 0, HIGH)
                pe.wait_ge(*when("w_hi", "X0o"))
                pe.wait_ge(*when("w_lo", "X0o"))
                for t in tiles(b):
                    pe.wait_ge(*freed(("X0", "agT", t)))
                    key = ("X0", "y", t)
                    pe.wait_ge(*next_bank(key, LOW + MID))
                    ps = bank(key)
                    q = slice(t % TB * P, (t % TB + 1) * P)
                    product(pe, ps[:, :], lambda hl, kb: AG[:, hl, kb, q], w("X0o")).then_inc(*fills(key))
                    last_use["X0o"] = key

        def ctile_dve(v, s, c, slots, free_key):
            v.wait_ge(*when(f"ct{c % 2}", (s, c)))
            if free_key is not None:
                v.wait_ge(*filled(free_key))
            dst = SRC[:, c % slots]
            v.tensor_copy(dst[:, 0, :], PB[:, c % 2, :]).then_inc(*mark("ct_hi", (s, c)))
            v.wait_ge(*when("ct_hi", (s, c)))
            v.tensor_tensor(dst[:, 1, :], PB[:, c % 2, :], dst[:, 0, :].bitcast(F32), ALU.subtract).then_inc(
                *mark("ct_lo", (s, c)))

        def x0_dve(v):
            v.wait_ge(*when("pv", (0, NX - 1, len(steps(0)) - 1)))
            v.memset(VX[:, :, :, 128:130], 1.0).then_inc(*mark("vx_ones", 0))
            split_hi(v, "X0q")

            def ct(c):
                ctile_dve(v, "X0", c, 4, ("X0", "v", c - 4) if c >= 4 else None)

            ct(0)
            ln_stats(v, "X0", 0)
            for c in range(NCT):
                v.wait_ge(*filled(("X0", "k", c)))
                ps = bank(("X0", "k", c))
                v.tensor_scalar(PB[:, 2, :], ps[:, :], 0.0, None, ALU.min).then_inc(*mark("k_min", c))
                if c + 1 < NCT:
                    ct(c + 1)
                v.wait_ge(*when("k_exp", c))
                if c >= 2:
                    v.wait_ge(*when("kv_step", c - 2))
                v.scalar_tensor_tensor(out=PB[:, 4 + c % 2, :], in0=ps[:, :], scalar=0.0, in1=PB[:, 3, :],
                                             op0=ALU.max, op1=ALU.add).then_inc(*frees(("X0", "k", c)))
                if c == 3:
                    ln_stats(v, "X0", 1)
                if 1 <= c < NT + 1:
                    ln_xn(v, "X0", c - 1)
                if 3 <= c < NT + 3:
                    ln_lo(v, "X0", c - 3)
                if c % NC == 0 and c:
                    blocks(c // NC - 1, v)
            split_hi(v, "X0g")
            blocks(B - 1, v)
            split_hi(v, "X0o")
            for b in range(B):
                if b == B - 1:
                    ln_stats(v, "F0", 0)
                for m in range(KB):
                    key = ("X0", "q", b, m)
                    v.wait_ge(*filled(key))
                    ps = bank(key)
                    v.tensor_scalar(PB[:, 2, :], ps[:, :], 0.0, None, ALU.min).then_inc(*mark("q_min", (b, m)))
                    v.wait_ge(*when("q_exp", (b, m)))
                    if b and m == 0:
                        v.wait_ge(*filled(("X0", "a", TB - 1, 1)))
                    elif m == 0:
                        v.wait_ge(*when("kv_step", NCT - 1))
                    v.scalar_tensor_tensor(out=PB[:, 4 + m, :], in0=ps[:, :], scalar=0.0, in1=PB[:, 3, :],
                                                 op0=ALU.max, op1=ALU.add).then_inc(*frees(key))
                if b == B - 1:
                    split_hi(v, "F0r")
                for t in tiles(b):
                    v.wait_ge(*filled(("X0", "g", t)))
                    ps = bank(("X0", "g", t))
                    if t:
                        v.wait_ge(*when("sigm", t - 1))
                    else:
                        v.wait_ge(*when("bg_in", 0))
                    v.tensor_tensor(PB[:, 0, :], ps[:, :], NB[:, 0, :], ALU.add).then_inc(*frees(("X0", "g", t)))
                    z = NB[:, 1, 0:16]
                    for h in range(2):
                        if t:
                            v.wait_ge(*freed(("X0", "a", t - 1, h)))
                        v.wait_ge(*filled(("X0", "a", t, h)))
                        ps = bank(("X0", "a", t, h))
                        pv_ = ps[:, 0:264].rearrange("p (g n) -> p g n", g=2)
                        v.tensor_scalar(z[:, 8 * h:8 * h + 8].rearrange("p (g n) -> p g n", g=2), pv_[:, :, 128:132],
                                               1e-6, None, ALU.add).then_inc(*mark("z_den", (t, h)))
                    v.wait_ge(*when("z_den", (t, 1)))
                    v.reciprocal(z, z).then_inc(*mark("z", t))
                    v.wait_ge(*when("z", t))
                    if t >= 2:
                        v.wait_ge(*filled(("X0", "agT", t - 2)))
                    else:
                        v.wait_ge(*when("att_lo", (0, NX // 2 - 1)))
                    for h in range(2):
                        ps = bank(("X0", "a", t, h))
                        for g in range(2):
                            src = ps[:, 132 * g:132 * g + P].rearrange("p (j n) -> p j n", j=4)
                            zz = z[:, 8 * h + 4 * g:8 * h + 4 * g + 4].unsqueeze(2).broadcast_to([P, 4, 32])
                            dst = XN[:, t % 2, (2 * h + g) * P:(2 * h + g + 1) * P].rearrange("p (j n) -> p j n", j=4)
                            ins = v.tensor_tensor(dst, src, zz, ALU.mult)
                        ins.then_inc(*frees(("X0", "a", t, h)))
                    if t % TB:
                        lo_ag(t - 1, v)
                lo_ag(b * TB + TB - 1, v)
                if b == B - 1:
                    ln_dve(v, "F0", 0)
                    split_hi(v, "F0g0")
                for t in tiles(b):
                    add_to_x(v, t, ("X0", "y", t))

        def blocks(b, v):
            v.wait_ge(*when("kv_step", b * NC + NC - 1))
            for g in range(KB):
                ps = bank(("X0", "kv", b, g))
                v.tensor_tensor(BD[:, b, g, 0:P], ps[:, 0:P], MR[:, 0:P], ALU.mult)
                v.tensor_scalar(BD[:, b, g, P:132], cs("hm", 0, 4), ps[:, P:P + 1], None, ALU.mult).then_inc(
                    *frees(("X0", "kv", b, g)))

        def lo_ag(t, v):
            q = slice(t % TB * P, (t % TB + 1) * P)
            v.wait_ge(*when("hi", ("X0", "agT", t)))
            v.wait_ge(*filled(("X0", "agT", t)))
            ps = bank(("X0", "agT", t))
            v.tensor_tensor(AG[:, 1, :, q], grid(ps), AG[:, 0, :, q].bitcast(F32), ALU.subtract).then_inc(
                *frees(("X0", "agT", t)))

        def x0_act(act):
            for c in range(NCT):
                act.wait_ge(*when("k_min", c))
                if c:
                    act.wait_ge(*freed(("X0", "k", c - 1)))
                act.activation(PB[:, 3, :], PB[:, 2, :], ACT.Exp).then_inc(*mark("k_exp", c))
                act.wait_ge(*filled(("X0", "v", c)))
                ps = bank(("X0", "v", c))
                if c == 0:
                    act.wait_ge(*when("vx_ones", 0))
                if c >= 2:
                    act.wait_ge(*when("kv_step", c - 2))
                act.activation(VX[:, c % 2, :, 0:P], grid(ps), ACT.Copy).then_inc(*frees(("X0", "v", c)))
                if 2 <= c < NT + 2:
                    ln_hi(act, "X0", c - 2)

            def hi(t):
                q = slice(t % TB * P, (t % TB + 1) * P)
                act.wait_ge(*filled(("X0", "agT", t)))
                ps = bank(("X0", "agT", t))
                if t == TB:
                    act.wait_ge(*filled(("X0", "y", TB - 1)))
                if t == 0:
                    act.wait_ge(*filled(("A0", "s", NX - 1, len(steps(0)) - 1)))
                act.activation(AG[:, 0, :, q], grid(ps), ACT.Copy).then_inc(*mark("hi", ("X0", "agT", t)))

            for b in range(B):
                for m in range(KB):
                    act.wait_ge(*when("q_min", (b, m)))
                    if b or m:
                        act.wait_ge(*freed(("X0", "q", b, m - 1) if m else ("X0", "q", b - 1, KB - 1)))
                    act.activation(PB[:, 3, :], PB[:, 2, :], ACT.Exp).then_inc(*mark("q_exp", (b, m)))
                for t in tiles(b):
                    act.wait_ge(*freed(("X0", "g", t)))
                    if t:
                        act.wait_ge(*when("gated", t - 1))
                    act.activation(PB[:, 1, :], PB[:, 0, :], ACT.Sigmoid).then_inc(*mark("sigm", t))
                    if t % TB:
                        hi(t - 1)
                hi(b * TB + TB - 1)
            ln_act(act, "F0", 0)

        def x0_pool(pool):
            ln_pool(pool, "X0", 0)
            split_lo_pool(pool, "X0q")
            ln_pool(pool, "X0", 1)
            split_lo_pool(pool, "X0g")
            split_lo_pool(pool, "X0o")
            for b in range(B):
                if b == B - 1:
                    ln_pool(pool, "F0", 0)
                    split_lo_pool(pool, "F0r")
                for t in tiles(b):
                    pool.wait_ge(*when("sigm", t))
                    for h in range(2):
                        pool.wait_ge(*freed(("X0", "a", t, h)))
                    pool.tensor_tensor(XN[:, t % 2, :], XN[:, t % 2, :], PB[:, 1, :], ALU.mult).then_inc(
                        *mark("gated", t))

        def load_ctile(sp, s, c, b, tt):
            sp.dma_start(grid(PB[:, c % 2, :]), a["ctxT"][b, :, :, tt * P:(tt + 1) * P]).then_inc(
                *mark(f"ct{c % 2}", (s, c), 16))

        def x0_sp(sp):
            sp.wait_ge(*when("pv", (0, NX - 1, len(steps(0)) - 1)))
            sp.dma_start(MR[:, 0:P], a["bdmask"]).then_inc(*mark("bdmask_in", 0, 16))
            for c in range(NCT):
                if c >= 2:
                    sp.wait_ge(*when("ct_lo", ("X0", c - 2)))
                load_ctile(sp, "X0", c, c // NC, c % NC)
                if c == 1:
                    load_chunk(sp, "X0g")
            sp.wait_ge(*when("att_lo", (0, NX // 2 - 1)))
            sp.dma_start(NB[:, 0, :], a["bg"]).then_inc(*mark("bg_in", 0, 16))
            load_chunk(sp, "X0o")
            load_chunk(sp, "F0r")
            load_chunk(sp, "F0g0")

        m8 = XN[:, 1, 0:64].rearrange("p (t e) -> p t e", t=NT)
        i8f = XN[:, 1, 64:128].rearrange("p (t e) -> p t e", t=NT)
        oh = XN[:, 1, 128:256].rearrange("p (k t e) -> p k t e", k=2, t=NT)
        SCP = XN[:, 0, :].rearrange("p (t e) -> p t e", t=TB)
        LT = (XN[0:8, 0, :], NB[0:8, 1, :])

        def router_pe(pe, s, b):
            chunk = s + "r"
            ln_ready(pe, s, b)
            pe.wait_ge(*when("w_hi", chunk))
            pe.wait_ge(*when("w_lo", chunk))
            pe.wait_ge(*next_bank((s, "lg", b), HIGH))
            ps = bank((s, "lg", b))
            product(pe, ps[:, :], w(chunk, 0, P), xt(b)).then_inc(*fills((s, "lg", b)))
            last_use[chunk] = (s, "lg", b)

        def router_turn(pe, s, b):
            pe.wait_ge(*freed((s, "lg", b)))
            pe.wait_ge(*next_bank((s, "lt", b), HIGH))
            ps = bank((s, "lt", b))
            for i in range(TB):
                ins = pe.transpose(ps[:, 8 * i:8 * i + 8], LT[b][:, i * P:(i + 1) * P], ident[0:8, 0:8])
            ins.then_inc(*fills((s, "lt", b)))

        def router_act(act, s, b):
            act.wait_ge(*filled((s, "lg", b)))
            ps = bank((s, "lg", b))
            if s == "F0":
                ins = act.activation(LT[b], ps[0:8, :], ACT.Identity, bias=cs("rb")[0:8, :])
            else:
                ins = act.activation(LT[b], ps[0:8, :], ACT.Sigmoid)
            ins.then_inc(*frees((s, "lg", b)))

        def router_dve(v, s):
            step = [0]

            def link(ins):
                step[0] += 1
                ins.then_inc(*mark("route", (s, step[0])))
                v.wait_ge(*when("route", (s, step[0])))

            for b in range(B):
                v.wait_ge(*filled((s, "lt", b)))
                ps = bank((s, "lt", b))
                v.tensor_copy(LG[:, b * TB:(b + 1) * TB, :], ps[:, 0:8 * TB].rearrange("p (t e) -> p t e", t=TB)).then_inc(
                    *frees((s, "lt", b)))
            for b in range(B):
                v.wait_ge(*freed((s, "lt", b)))
            for t in range(NT):
                ins = v.max(m8[:, t, :], LG[:, t, :])
            link(ins)
            for t in range(NT):
                ins = v.max_index(i8[:, t, :], m8[:, t, :], LG[:, t, :])
            link(ins)
            link(v.tensor_copy(i8f, i8[:, :, :]))
            iota = cs("iota", 0, 8).unsqueeze(1).broadcast_to([P, NT, 8])
            for k in range(2):
                ins = v.tensor_tensor(oh[:, k], iota, i8f[:, :, k:k + 1].broadcast_to([P, NT, 8]), ALU.is_equal)
            link(ins)
            best, second = m8[:, :, 0:1], m8[:, :, 1:2]
            if s == "F0":
                link(v.tensor_tensor(tw[:, 0, :], m8[:, :, 1], m8[:, :, 0], ALU.subtract))
                v.wait_ge(*when("tw_exp", 0))
                link(v.tensor_scalar(tw[:, 2, :], tw[:, 1, :], 1.0, None, ALU.add))
                link(v.reciprocal(tw[:, 0, :], tw[:, 2, :]))
                link(v.tensor_tensor(tw[:, 2, :], tw[:, 1, :], tw[:, 0, :], ALU.mult))
                best, second = tw[:, 0, :].unsqueeze(2), tw[:, 2, :].unsqueeze(2)
            for k, weight in enumerate((best, second)):
                ins = v.tensor_tensor(oh[:, k], oh[:, k], weight.broadcast_to([P, NT, 8]), ALU.mult)
            link(ins)
            ins = v.tensor_tensor(SCR[:, :, 0:8], oh[:, 0], oh[:, 1], ALU.add)
            link(ins)
            v.memset(SCR[:, :, 8:9], 1.0).then_inc(*mark("scores", s))

        F0N = [(e, b, m) for e in range(NE) for b in range(B) for m in range(KB)]

        def f0_pe(pe):
            def up(e, b, m, T, ring=ALLB):
                chunk, key = f"F0{T}{e}", ("F0", T, e, b, m)
                pe.wait_ge(*when("w_hi", chunk))
                pe.wait_ge(*when("w_lo", chunk))
                pe.wait_ge(*next_bank(key, ring))
                ps = bank(key)
                product(pe, ps[:, :], w(chunk, m * P, (m + 1) * P), xt(b)).then_inc(*fills(key))
                last_use[chunk] = xt_last[("F0", b)] = key

            router_pe(pe, "F0", 0)
            for m in range(KB):
                up(0, 0, m, "g", OUTB)
            ln_pe(pe, "F0", 1, HIGH)
            router_pe(pe, "F0", 1)
            for b in range(B):
                router_turn(pe, "F0", b)
            for m in range(KB):
                up(0, 0, m, "u", HIGH)
            for e in range(NE):
                for b in range(B):
                    for m in range(KB):
                        for T in "gu":
                            if (e, b) != (0, 0):
                                up(e, b, m, T)
                if e == 0:
                    for b in range(B):
                        pe.wait_ge(*when("scp", b))
                        pe.wait_ge(*next_bank(("F0", "scT", b), ALLB))
                        ps = bank(("F0", "scT", b))
                        for i in range(TB):
                            ins = pe.transpose(ps[:, i * P:(i + 1) * P], SCP[:, i, :], ident[:])
                        ins.then_inc(*fills(("F0", "scT", b)))
                        pe.wait_ge(*freed(("F0", "scT", b)))
                        for t in tiles(b):
                            if t == 0:
                                pe.wait_ge(*when("db_in", 0))
                            pe.wait_ge(*next_bank(("F0", "db", t), ALLB))
                            ps = bank(("F0", "db", t))
                            pe.matmul(ps[:, :], NB[:, 1, t % TB * P:(t % TB + 1) * P], NB[:, 0, :], start=True,
                                      stop=True).then_inc(*fills(("F0", "db", t)))
                for b in range(B):
                    chunk = f"F0d{e}"
                    pe.wait_ge(*when("w_hi", chunk))
                    pe.wait_ge(*when("w_lo", chunk))
                    pe.wait_ge(*when("act_lo", (e, b, KB - 1)))
                    for t in tiles(b):
                        key = ("F0", "d", e, t)
                        pe.wait_ge(*next_bank(key, ALLB))
                        ps = bank(key)
                        lhs = lambda hl, kb: AH[:, b, hl, kb * 512 + t % TB * P:kb * 512 + (t % TB + 1) * P]
                        product(pe, ps[:, :], lhs, w(chunk)).then_inc(*fills(key))
                        last_use[chunk] = key

        def f0_dve(v):
            ln_stats(v, "F0", 1)
            split_hi(v, "F0u0")
            ln_dve(v, "F0", 1)
            v.tensor_scalar(cs("ub1", 0, 32), cs("ub", 0, 32), 1.0, None, ALU.add).then_inc(*mark("ub1", 0))
            router_dve(v, "F0")
            split_hi(v, "F0d0")

            def bias():
                for b in range(B):
                    if b:
                        v.wait_ge(*filled(("F0", "scT", 0)))
                    else:
                        v.memset(XN[:, 0, :], 0.0).then_inc(*mark("scp0", 0))
                        v.wait_ge(*when("scp0", 0))
                        v.wait_ge(*when("scores", "F0"))
                    v.tensor_copy(SCP[:, :, 0:8], SCR[:, b * TB:(b + 1) * TB, 0:8]).then_inc(*mark("scp", b))
                for t in range(NT):
                    add_to_x(v, t, ("F0", "db", t))

            def product_of(n):
                e, b, m = F0N[n]
                k = n % 2
                v.wait_ge(*when("glu", n))
                v.wait_ge(*freed(("F0", "u", e, b, m)))
                if n >= 2:
                    v.wait_ge(*when("act_lo", F0N[n - 2]))
                v.scalar_tensor_tensor(out=PB[:, 6 + k, :], in0=PB[:, 4 + k, :], scalar=8.0, in1=PB[:, 2 + k, :],
                                              op0=ALU.min, op1=ALU.mult).then_inc(*mark("act_f", n))

            for n, (e, b, m) in enumerate(F0N):
                k = n % 2
                v.wait_ge(*filled(("F0", "g", e, b, m)))
                ps = bank(("F0", "g", e, b, m))
                if n >= 2:
                    v.wait_ge(*when("glu", n - 2))
                v.tensor_scalar(PB[:, k, :], ps[:, :], cs("gb", e * 4 + m), 7.0, ALU.add, ALU.min).then_inc(
                    *frees(("F0", "g", e, b, m)))
                v.wait_ge(*filled(("F0", "u", e, b, m)))
                ps = bank(("F0", "u", e, b, m))
                if n >= 2:
                    v.wait_ge(*when("act_f", n - 2))
                else:
                    v.wait_ge(*when("ub1", 0))
                v.tensor_scalar(PB[:, 4 + k, :], ps[:, :], cs("ub1", e * 4 + m), -6.0, ALU.add, ALU.max).then_inc(
                    *frees(("F0", "u", e, b, m)))
                if b or m:
                    product_of(n - 1)
                if (b, m) == (B - 1, KB - 1):
                    product_of(n)
                    if e == 0:
                        bias()
                    nxt = CHUNKS[CI[f"F0g{e}"] + 3:CI[f"F0g{e}"] + 6]
                    split_hi(v, nxt[0])
                    split_hi(v, nxt[1])
                    for t in range(NT):
                        if (e, t) == (NE - 1, TB):
                            ln_stats(v, "A1", 0)
                            ln_dve(v, "A1", 0)
                        add_to_x(v, t, ("F0", "d", e, t), SCR[:, t, e:e + 1])
                    split_hi(v, nxt[2])

        def f0_act(act):
            router_act(act, "F0", 0)
            ln_act(act, "F0", 1)
            router_act(act, "F0", 1)
            act.wait_ge(*when("route", ("F0", 5)))
            act.activation(tw[:, 1, :], tw[:, 0, :], ACT.Exp).then_inc(*mark("tw_exp", 0))
            def bias():
                for b in range(B):
                    act.wait_ge(*filled(("F0", "scT", b)))
                    ps = bank(("F0", "scT", b))
                    if b:
                        act.wait_ge(*filled(("F0", "db", TB - 1)))
                    act.activation(NB[:, 1, :], ps[:, :], ACT.Copy).then_inc(*frees(("F0", "scT", b)))

            def hi(n):
                e, b, m = F0N[n]
                act.wait_ge(*when("act_f", n))
                if e and m == 0:
                    act.wait_ge(*filled(("F0", "d", e - 1, b * TB + TB - 1)))
                if n == 0:
                    act.wait_ge(*filled(("A0", "s", NX - 1, len(steps(0)) - 1)))
                act.activation(AH[:, b, 0, m * 512:(m + 1) * 512], PB[:, 6 + n % 2, :], ACT.Copy).then_inc(
                    *mark("act_hi", n))

            for n, (e, b, m) in enumerate(F0N):
                act.wait_ge(*freed(("F0", "g", e, b, m)))
                if n >= 2:
                    act.wait_ge(*when("act_f", n - 2))
                act.activation(PB[:, 2 + n % 2, :], PB[:, n % 2, :], ACT.Sigmoid, scale=1.702).then_inc(*mark("sig", n))
                if b or m:
                    hi(n - 1)
                if (b, m) == (B - 1, KB - 1):
                    hi(n)
                    if e == 0:
                        bias()

        def f0_pool(pool):
            split_lo_pool(pool, "F0g0")
            ln_pool(pool, "F0", 1)
            split_lo_pool(pool, "F0u0")
            split_lo_pool(pool, "F0d0")

            def lo(n):
                e, b, m = F0N[n]
                pool.wait_ge(*when("act_hi", n))
                pool.tensor_tensor(AH[:, b, 1, m * 512:(m + 1) * 512], PB[:, 6 + n % 2, :],
                                          AH[:, b, 0, m * 512:(m + 1) * 512].bitcast(F32), ALU.subtract).then_inc(
                                              *mark("act_lo", (e, b, m)))

            for n, (e, b, m) in enumerate(F0N):
                pool.wait_ge(*when("sig", n))
                pool.tensor_tensor(PB[:, 2 + n % 2, :], PB[:, 2 + n % 2, :], PB[:, n % 2, :], ALU.mult).then_inc(
                    *mark("glu", n))
                if b or m:
                    lo(n - 1)
                if (b, m) == (B - 1, KB - 1):
                    lo(n)
                    if e == NE - 1:
                        ln_pool(pool, "A1", 0)
                    for chunk in CHUNKS[CI[f"F0g{e}"] + 3:CI[f"F0g{e}"] + 6]:
                        split_lo_pool(pool, chunk)

        def f0_sp(sp):
            sp.wait_ge(*filled(("X0", "agT", NT - 1)))
            sp.wait_ge(*when("z", NT - 1))
            sp.wait_ge(*freed(("X0", "a", NT - 1, 1)))
            sp.wait_ge(*freed(("X0", "g", NT - 1)))
            sp.dma_start(NB[:, 0, :], a["down_bias"]).then_inc(*mark("db_in", 0, 16))
            for c in range(CI["F0g0"] + 1, CI["A1kv"] + 1):
                load_chunk(sp, CHUNKS[c])

        JOBS = [(b, t, "i") for b in range(B) for t in range(3)] + [(b, t, "t") for b in range(B) for t in range(2, NC)]
        QJOBS = [(t // TB, t % TB, "q") for t in range(NT)]
        ALLJ = JOBS + QJOBS

        def x1_pe(pe):
            def turn(c):
                pe.wait_ge(*when("n", c))
                key = ("X1", "nT", c)
                pe.wait_ge(*next_bank(key, (4, 5, 6, 7)))
                ps = bank(key)
                for g in range(KB):
                    ins = pe.transpose(ps[:, g * P:(g + 1) * P], XN[:, c % 2, g * P:(g + 1) * P], ident[:])
                ins.then_inc(*fills(key))

            for c, (b, tt, kind) in enumerate(ALLJ):
                if kind == "q":
                    if c == len(JOBS):
                        turn(c - 1)
                    if tt == 0:
                        ln_ready(pe, "X1", b)
                    parts = [("k", "X1q", xtile(c - len(JOBS)))]
                else:
                    pe.wait_ge(*when("ct_lo", ("X1", c)))
                    ct = (lambda c: lambda hl, kb: SRC[:, c % 2, hl, kb * P:(kb + 1) * P])(c)
                    parts = [(T, f"X1{T}i" if kind == "i" else f"X1{T}", ct) for T in "kv"]
                for T, chunk, lhs in parts:
                    pe.wait_ge(*when("w_hi", chunk))
                    pe.wait_ge(*when("w_lo", chunk))
                    key = ("X1", T, c)
                    pe.wait_ge(*next_bank(key, LOW if T == "k" else MID))
                    ps = bank(key)
                    product(pe, ps[:, :], lhs, w(chunk)).then_inc(*fills(key))
                    last_use[chunk] = key
                    if kind == "q":
                        proj_last[(2, b)] = key
                if 2 <= c < NT + 2:
                    ln_turn(pe, "X1", c - 2, HIGH)
                if c and c != len(JOBS):
                    turn(c - 1)
            turn(len(ALLJ) - 1)

        row_buf = lambda c: VB[:, 1, 0:512] if c % 2 else PB[:, 6, :]
        squares = lambda c: VB[:, 1, 512:1024] if c % 2 else MR[:, :]
        sq = lambda c: ss[:, c % 2 * 4:c % 2 * 4 + 4]

        def x1_dve(v):
            v.wait_ge(*when("att_lo", (1, NX - 1)))
            v.wait_ge(*when("pv", (1, NX - 1, len(steps(1)) - 1)))

            def ct(c):
                ctile_dve(v, "X1", c, 2, ("X1", "v", c - 2) if c >= 2 else None)

            def norm_weight(c):
                b, tt, kind = ALLJ[c]
                v.wait_ge(*filled(("X1", "nT", c)))
                ps = bank(("X1", "nT", c))
                if c:
                    if ALLJ[c - 1][1:] != (2, "i"):
                        v.wait_ge(*when("src_lo", (2, c - 1)))
                wt = cs({"i": "wki", "t": "wk", "q": "wq"}[kind], 0, 4).unsqueeze(2).broadcast_to([P, KB, P])
                v.tensor_tensor(grid(PB[:, 7, :]), grid(ps), wt, ALU.mult).then_inc(*frees(("X1", "nT", c)))
                if (tt, kind) == (2, "i"):
                    v.wait_ge(*freed(("X1", "nT", c)))
                    col = grid(PB[:, 7, :])[:, :, 0]
                    v.tensor_copy(KI[:, b, 0, :], col).then_inc(*mark("ki_hi", b))
                    v.wait_ge(*when("ki_hi", b))
                    v.tensor_tensor(KI[:, b, 1, :], col, KI[:, b, 0, :].bitcast(F32), ALU.subtract).then_inc(
                        *mark("ki", b))
                    return

            def norm_lo(c):
                b, tt, kind = ALLJ[c]
                if (tt, kind) == (2, "i"):
                    return
                dst = SRC[:, 2 + c % 2]
                v.wait_ge(*when("hi", (2, c)))
                ins = v.tensor_tensor(dst[:, 1, :], PB[:, 7, :], dst[:, 0, :].bitcast(F32), ALU.subtract)
                if (tt, kind) == (2, "t"):
                    ins.then_inc(*mark("lo_first", c))
                    v.wait_ge(*when("lo_first", c))
                    v.wait_ge(*when("ki", b))
                    for hl in range(2):
                        ins = v.tensor_copy(grid(dst[:, hl, :])[:, :, 0], KI[:, b, hl, :].bitcast(F32))
                ins.then_inc(*mark("src_lo", (2, c)))

            ct(0)
            v.wait_ge(*when("kvb_in", 0))
            ln_stats(v, "X1", 0)
            for c, (b, tt, kind) in enumerate(ALLJ):
                if c == len(JOBS):
                    norm_weight(c - 1)
                    norm_lo(c - 1)
                    v.wait_ge(*when("ob_in", 0))
                    for t in range(NT):
                        v.wait_ge(*when("xn", ("X1", t)))
                        v.tensor_tensor(X[:, t, :], X[:, t, :], PB[:, 3, :], ALU.add).then_inc(*mark("x_bias", t))
                        x_key[t] = ("x_bias", t)
                    v.wait_ge(*when("qb_in", 0))
                bias = {"i": 2, "t": 4, "q": 2}[kind]
                v.wait_ge(*filled(("X1", "k", c)))
                ps = bank(("X1", "k", c))
                if c > 1:
                    v.wait_ge(*when("n", c - 2))
                v.tensor_tensor(row_buf(c), ps[:, :], PB[:, bias, :], ALU.add).then_inc(*frees(("X1", "k", c)))
                if c == 5:
                    split_hi(v, "X1v")
                if kind != "q":
                    if c + 1 < len(JOBS):
                        ct(c + 1)
                    v.wait_ge(*filled(("X1", "v", c)))
                    ps = bank(("X1", "v", c))
                    if c >= 2:
                        v.wait_ge(*when(f"v_stored{c % 2}", (2, c - 2)))
                    if tt == 2:
                        v.tensor_tensor(NB[:, c % 2, :], ps[:, :], PB[:, bias + 1, :], ALU.add).then_inc(
                            *mark("v_row", c))
                        v.wait_ge(*when("v_row", c))
                        ins = v.tensor_scalar(NB[:, c % 2, :], NB[:, c % 2, :], cs("img" if kind == "i" else "txt"), None, ALU.mult)
                    else:
                        ins = v.tensor_tensor(NB[:, c % 2, :], ps[:, :], PB[:, bias + 1, :], ALU.add)
                    ins.then_inc(*frees(("X1", "v", c)))
                if c and c != len(JOBS):
                    norm_weight(c - 1)
                v.wait_ge(*when("rk", c))
                if c >= 2:
                    v.wait_ge(*filled(("X1", "nT", c - 2)))
                v.tensor_scalar(XN[:, c % 2, :], row_buf(c), sq(c)[:, 2:3], None, ALU.mult).then_inc(*mark("n", c))
                if c and c != len(JOBS):
                    norm_lo(c - 1)
                if c == 3:
                    ln_stats(v, "X1", 1)
                if 1 <= c < NT + 1:
                    ln_xn(v, "X1", c - 1)
                if 3 <= c < NT + 3:
                    ln_lo(v, "X1", c - 3)
                if c == 9:
                    split_hi(v, "X1q")
                if c == 2:
                    split_hi(v, "X1k")
            norm_weight(len(ALLJ) - 1)
            norm_lo(len(ALLJ) - 1)

        def x1_act(act):
            def hi(c):
                if ALLJ[c][1:] == (2, "i"):
                    return
                act.wait_ge(*freed(("X1", "nT", c)))
                prev = [p for p in range(c) if p % 2 == c % 2 and ALLJ[p][1:] != (2, "i")]
                if prev:
                    act.wait_ge(*when(f"src_stored{2 + c % 2}", (2, prev[-1])))
                act.activation(SRC[:, 2 + c % 2, 0, :], PB[:, 7, :], ACT.Copy).then_inc(*mark("hi", (2, c)))

            act.wait_ge(*freed(("A1", "mt", NX - 1)))
            for c in range(len(ALLJ)):
                if c == len(JOBS):
                    hi(c - 1)
                act.wait_ge(*freed(("X1", "k", c)))
                if c > 1:
                    act.wait_ge(*when("rk", c - 2))
                elif c == 0:
                    act.wait_ge(*when(f"mrow{(NX - 1) % 4}", (1, NX - 1)))
                act.activation(squares(c), row_buf(c), ACT.Square, accum_out=sq(c)[:, 0:1]).then_inc(*mark("sq", c))
                if 2 <= c < NT + 2:
                    ln_hi(act, "X1", c - 2)
                if c and c != len(JOBS):
                    hi(c - 1)
            hi(len(ALLJ) - 1)

        def x1_pool(pool):
            ln_pool(pool, "X1", 0)
            for c in range(len(ALLJ)):
                if c == 4:
                    ln_pool(pool, "X1", 1)
                pool.wait_ge(*when("sq", c))
                pool.tensor_scalar(sq(c)[:, 1:2], sq(c)[:, 0:1], 1.0 / D, 1e-6, ALU.mult, ALU.add).then_inc(
                    *mark("ms2", c))
                pool.wait_ge(*when("ms2", c))
                if c > 1:
                    pool.wait_ge(*when("n", c - 2))
                pool.tensor_tensor(sq(c)[:, 2:3], sq(c)[:, 1:2], cs("mhalf"), ALU.pow).then_inc(*mark("rk", c))
                if c == 5:
                    split_lo_pool(pool, "X1v")
                if c == 9:
                    split_lo_pool(pool, "X1q")
                if c == 2:
                    split_lo_pool(pool, "X1k")

        def x1_sp(sp):
            sp.wait_ge(*when("pv", (1, NX - 1, len(steps(1)) - 1)))
            for c in range(2):
                load_ctile(sp, "X1", c, *JOBS[c][:2])
            for dst, src in ([(PB[:, 2 + n, :], a[x]) for n, x in enumerate(("ki_b", "vi_b", "k_b", "v_b"))]):
                sp.dma_start(dst, src).then_inc(*mark("kvb_in", 0, 16))
            sp.dma_start(VB[:, :, 1024:1152], a["pattern"]).then_inc(*mark("pattern_in", 0, 16))
            load_chunk(sp, "X1k")

            def store(c):
                b, tt, kind = ALLJ[c]
                if (tt, kind) != (2, "i"):
                    sp.wait_ge(*when("src_lo", (2, c)))
                    dram_t = (QD if kind == "q" else KD)[2]
                    for dst, src in ([(dram_t[b, hl, :, tt * P:(tt + 1) * P].rearrange("(g p) t -> p g t", g=KB),
                           grid(SRC[:, 2 + c % 2, hl, :]).bitcast(F32)) for hl in range(2)]):
                        sp.dma_start(dst, src).then_inc(*mark(f"src_stored{2 + c % 2}", (2, c), 16))

            for c, (b, tt, kind) in enumerate(JOBS):
                if c + 2 < len(JOBS):
                    sp.wait_ge(*when("ct_lo", ("X1", c)))
                    load_ctile(sp, "X1", c + 2, *JOBS[c + 2][:2])
                sp.wait_ge(*freed(("X1", "v", c)))
                sp.dma_start(VD[2][b, tt + (kind == "t")], NB[:, c % 2, :]).then_inc(
                    *mark(f"v_stored{c % 2}", (2, c), 16))
                if c:
                    store(c - 1)
                if c == 2:
                    load_chunk(sp, "X1v")
                    sp.wait_ge(*when("pattern_in", 0))
                    for r in range(2):
                        sp.dma_start(KS[96:100, 4 * r:4 * r + 4, :].bitcast(F32), VB[:, r, 1024:1152]).then_inc(
                            *mark("key_rows_x1", 0, 16))
                if c == 5:
                    sp.wait_ge(*freed(("X1", "k", 5)))
                    sp.dma_start(PB[:, 2, :], a["q_b"]).then_inc(*mark("qb_in", 0, 16))
                    sp.dma_start(PB[:, 3, :], a["o_b"]).then_inc(*mark("ob_in", 0, 16))
                    load_chunk(sp, "X1q")
            store(len(JOBS) - 1)
            for c in range(len(JOBS), len(ALLJ)):
                store(c)
                if c == len(JOBS) + 4:
                    at_sp_stack(sp, 2, 0)

        def f1_pe(pe):
            def hidden(e, t, ring=ALLB):
                pe.wait_ge(*when("w_hi", f"F1h{e}"))
                pe.wait_ge(*when("w_lo", f"F1h{e}"))
                key = ("F1", "h", e, t)
                pe.wait_ge(*next_bank(key, ring))
                ps = bank(key)
                product(pe, ps[:, :], xtile(t), w(f"F1h{e}")).then_inc(*fills(key))
                last_use[f"F1h{e}"] = key

            router_pe(pe, "F1", 0)
            for t in tiles(0):
                hidden(0, t, OUTB)
            ln_pe(pe, "F1", 1, HIGH)
            router_pe(pe, "F1", 1)
            for b in range(B):
                router_turn(pe, "F1", b)

            def turn(e, tp):
                key = ("F1", "aT", e, tp)
                for t in (2 * tp, 2 * tp + 1):
                    pe.wait_ge(*freed(("F1", "h", e, t)))
                pe.wait_ge(*next_bank(key, ALLB))
                ps = bank(key)
                for kb in range(2):
                    for t in (2 * tp, 2 * tp + 1):
                        ins = pe.transpose(ps[:, kb * 256 + t % 2 * P:kb * 256 + t % 2 * P + P],
                                           PB[:, 2 + t % 4, kb * P:(kb + 1) * P], ident[:])
                ins.then_inc(*fills(key))

            for e in range(NE + 2):
                for t in range(NT):
                    if e <= NE and (e or t >= TB):
                        hidden(e, t)
                    n = e * NT + t
                    if t % 2 and 3 <= n <= NE * NT + NT + 1:
                        turn((n - 3) // NT, (n - 3) % NT // 2)
                    if e:
                        chunk, key = f"F1d{e - 1}", ("F1", "d", e - 1, t)
                        pe.wait_ge(*when("w_hi", chunk))
                        pe.wait_ge(*when("w_lo", chunk))
                        pe.wait_ge(*freed(("F1", "aT", e - 1, t // 2)))
                        pe.wait_ge(*next_bank(key, ALLB))
                        ps = bank(key)
                        par = (e - 1) % 2
                        lhs = lambda hl, kb: AH[:, par, hl, kb * 1024 + t * P:kb * 1024 + (t + 1) * P]
                        product(pe, ps[:, :], lhs, w(chunk), blocks=2).then_inc(*fills(key))
                        last_use[chunk] = key

        def f1_ah(e, hl, tp):
            return AH[:, e % 2, hl, :].rearrange("p (k n) -> p k n", k=2)[:, :, tp * 256:(tp + 1) * 256]

        def f1_dve(v):
            ln_stats(v, "F1", 1)
            ln_dve(v, "F1", 1)
            split_hi(v, "F1h1")
            router_dve(v, "F1")
            v.wait_ge(*when("scores", "F1"))
            for e in range(NE + 2):
                if e:
                    split_hi(v, f"F1d{e - 1}") if e > 1 else None
                for t in range(NT):
                    if e <= NE:
                        v.wait_ge(*filled(("F1", "h", e, t)))
                        ps = bank(("F1", "h", e, t))
                        v.wait_ge(*when("silu", (e, t)))
                        n = e * NT + t
                        if n >= 4:
                            v.wait_ge(*filled(("F1", "aT", (n - 4) // NT, (n - 4) % NT // 2)))
                        v.scalar_tensor_tensor(out=PB[:, 2 + t % 4, 0:256], in0=ps[:, 256:512], scalar=SCR[:, t, e:e + 1],
                                                     in1=PB[:, t % 2, 0:256], op0=ALU.mult, op1=ALU.mult).then_inc(
                                                         *frees(("F1", "h", e, t)))
                    n = e * NT + t
                    if t % 2 and 3 <= n <= NE * NT + NT + 1:
                        e2, tp = (n - 3) // NT, (n - 3) % NT // 2
                        key = ("F1", "aT", e2, tp)
                        v.wait_ge(*when("hi", key))
                        v.wait_ge(*filled(key))
                        ps = bank(key)
                        v.tensor_tensor(f1_ah(e2, 1, tp), ps[:, :].rearrange("p (k n) -> p k n", k=2),
                                              f1_ah(e2, 0, tp).bitcast(F32), ALU.subtract).then_inc(*frees(key))
                    if e:
                        add_to_x(v, t, ("F1", "d", e - 1, t))
                    if e == 0 and t == 0:
                        split_hi(v, "F1d0")
                    if e and t == 1 and e + 1 <= NE:
                        split_hi(v, f"F1h{e + 1}")

        def f1_act(act):
            router_act(act, "F1", 0)
            ln_act(act, "F1", 1)
            router_act(act, "F1", 1)
            act.wait_ge(*when("scores", "F1"))
            for e in range(NE + 2):
                for t in range(NT):
                    n = e * NT + t
                    if e <= NE:
                        act.wait_ge(*filled(("F1", "h", e, t)))
                        ps = bank(("F1", "h", e, t))
                        if n >= 2:
                            act.wait_ge(*freed(("F1", "h", (n - 2) // NT, (n - 2) % NT)))
                        act.activation(PB[:, t % 2, 0:256], ps[:, 0:256], ACT.Silu, scale=SCR[:, t, e:e + 1]).then_inc(
                            *mark("silu", (e, t)))
                    if t % 2 and 3 <= n <= NE * NT + NT + 1:
                        e2, tp = (n - 3) // NT, (n - 3) % NT // 2
                        key = ("F1", "aT", e2, tp)
                        act.wait_ge(*filled(key))
                        ps = bank(key)
                        if e2 >= 2 and tp == 0:
                            act.wait_ge(*filled(("F1", "d", e2 - 2, NT - 1)))
                        if n == 3:
                            act.wait_ge(*filled(("X1", "s", NX - 1, len(steps(2)) - 1)))
                        act.activation(f1_ah(e2, 0, tp), ps[:, :].rearrange("p (k n) -> p k n", k=2), ACT.Copy).then_inc(
                            *mark("hi", key))

        def f1_pool(pool):
            ln_pool(pool, "F1", 1)
            split_lo_pool(pool, "F1h1")
            split_lo_pool(pool, "F1d0")
            for e in range(1, NE + 1):
                if e > 1:
                    split_lo_pool(pool, f"F1d{e - 1}")
                if e + 1 <= NE:
                    split_lo_pool(pool, f"F1h{e + 1}")
            split_lo_pool(pool, f"F1d{NE}")

        block = ctx.enter_context(nc.Block())

        @block.tensor
        def _(pe):
            pe.wait_ge(*when("const", "pool"))
            ln_pe(pe, "A0", 0)
            qkv_pe(pe, 0)
            at_pe(pe, 0)
            x0_pe(pe)
            f0_pe(pe)
            ln_pe(pe, "A1", 0)
            qkv_pe(pe, 1)
            at_pe(pe, 1)
            x1_pe(pe)
            at_pe(pe, 2)
            f1_pe(pe)

        @block.vector
        def _(v):
            v.wait_ge(*when("small_in", 0))
            ln_stats(v, "A0", 0)
            split_hi(v, "A0q")
            ln_dve(v, "A0", 0)
            ln_stats(v, "A0", 1)
            split_hi(v, "A0k")
            ln_dve(v, "A0", 1)
            split_hi(v, "A0v")
            v.wait_ge(*when("const", "pool"))
            qkv_dve(v, 0, [["A0o"], []])
            at_dve(v, 0)
            x0_dve(v)
            f0_dve(v)
            ln_stats(v, "A1", 1)
            ln_dve(v, "A1", 1)
            qkv_dve(v, 1, [[], [], []])
            at_dve(v, 1)
            x1_dve(v)
            at_dve(v, 2)
            f1_dve(v)

        @block.scalar
        def _(act):
            act.wait_ge(*when("small_in", 0))
            for b in range(B):
                ln_act(act, "A0", b)
            qkv_act(act, 0)
            at_act(act, 0)
            x0_act(act)
            f0_act(act)
            for b in range(B):
                ln_act(act, "A1", b)
            qkv_act(act, 1)
            at_act(act, 1)
            x1_act(act)
            at_act(act, 2)
            f1_act(act)

        @block.gpsimd
        def _(pool):
            step = [0]

            def link(ins):
                step[0] += 1
                ins.then_inc(*mark("const_step", step[0]))
                pool.wait_ge(*when("const_step", step[0]))

            for t, value in ((ident, 0.0), (identb, 0.0), (mask_qk, 0.0), (mask_kq, 0.0), (ones, 1.0)):
                link(pool.memset(t[:], value))
            for t in (ident, identb):
                link(pool.affine_select(out=t[:], in_=t[:], compare_op=ALU.not_equal, fill=1.0, base=0,
                                        pattern=[[-1, P]], channel_multiplier=1))
            link(pool.affine_select(out=mask_qk[:], in_=mask_qk[:], compare_op=ALU.is_ge, fill=MASKED, base=0,
                                    pattern=[[-1, P]], channel_multiplier=1))
            link(pool.affine_select(out=mask_kq[:], in_=mask_kq[:], compare_op=ALU.is_ge, fill=MASKED, base=0,
                                    pattern=[[1, P]], channel_multiplier=-1))
            pool.wait_ge(*when("small_in", 0))
            for k, name in enumerate(("img", "txt")):
                ins = pool.tensor_scalar(onesm[:, k, :], ones[:, 0:32], cs(name), None, ALU.mult)
            ins.then_inc(*mark("const", "pool"))
            ln_pool(pool, "A0", 0)
            split_lo_pool(pool, "A0q")
            ln_pool(pool, "A0", 1)
            split_lo_pool(pool, "A0k")
            split_lo_pool(pool, "A0v")
            qkv_pool(pool, 0, [["A0o"], []])
            at_pool(pool, 0)
            x0_pool(pool)
            f0_pool(pool)
            ln_pool(pool, "A1", 1)
            qkv_pool(pool, 1, [[], [], []])
            at_pool(pool, 1)
            split_lo_pool(pool, "X1vi")
            x1_pool(pool)
            at_pool(pool, 2)
            f1_pool(pool)

        @block.sync
        def _(sp):
            sp.dma_start(small[:, 0:100], a["small"]).then_inc(*mark("small_in", 0, 16))
            for t in range(NT):
                if t == TB:
                    load_chunk(sp, "A0q")
                sp.dma_start(X[:, t, :], a["x"][t]).then_inc(*mark(f"x_in{t}", t, 16))
            sp.wait_ge(*when("const", "pool"))
            for r in range(2):
                sp.dma_start(KS[96 + r:97 + r, :, :].bitcast(F32), ones[:, :]).then_inc(
                    *mark("key_rows_a0", 0, 16))
            sp.dma_start(PB[:, 0:2, :], a["rope0"]).then_inc(*mark("rope_tables", 0, 16))
            for c in ("A0k", "A0v", "A0o"):
                load_chunk(sp, c)
            qkv_sp(sp, 0, {})
            at_sp(sp, 0)
            load_chunk(sp, "X0q")
            x0_sp(sp)
            f0_sp(sp)
            sp.wait_ge(*when("act_lo", F0N[-1]))
            sp.dma_start(PB[:, 0:2, :], a["rope1"]).then_inc(*mark("rope_tables", 1, 16))
            sp.wait_ge(*filled(("F0", "d", NE - 1, NT - 1)))
            for r, h in np.ndindex(2, 4):
                sp.dma_start(K1[0][64 + r:65 + r, h, 512:1024].bitcast(F32), ones[0:8, :]).then_inc(
                    *mark("key_rows_a1", 0, 16))
            qkv_sp(sp, 1, {})
            for T, b in (("q", 0), ("q", 1), ("k", 0), ("k", 1)):
                wait_stored(sp, 1, T, b)
            for r, h in np.ndindex(2, 4):
                sp.dma_start(K1[1][64 + r:65 + r, h, 512:1024].bitcast(F32), ones[0:8, :]).then_inc(
                    *mark("key_rows_a1b", 0, 16))
            at_sp(sp, 1)
            load_chunk(sp, "X1vi")
            x1_sp(sp)
            at_sp(sp, 2)
            for c in range(CI["F1h0"] + 1, len(CHUNKS)):
                load_chunk(sp, CHUNKS[c])
            for t in range(NT):
                sp.wait_ge(*when(*x_key[t]))
                sp.dma_start(out[t], X[:, t, :]).then_inc(*mark("out_stored", t, 16))
            sp.wait_ge(*when("out_stored", NT - 1))
            assert freed_keys == set(bank_of), set(bank_of) - freed_keys


def rope_table(dim, rows, base=10000.0):
    f32 = np.float32
    if dim == 32:
        inv = f32(1.0) / np.power(f32(base), np.arange(0, dim, 2, dtype=f32) / f32(dim))
    else:
        inv = np.power(f32(base), -(np.arange(0, dim, 2, dtype=f32) / f32(dim)))
    angle = np.arange(S, dtype=f32)[:, None] * inv.astype(f32)[None, :]
    table = np.stack([np.cos(angle).T, np.sin(angle).T], axis=1).astype(f32)
    return np.ascontiguousarray(np.tile(table, (P // (dim // 2), 1, 1)))


def laid_out(i):
    def chunk(m):
        k = m.shape[0] // P
        c = np.ascontiguousarray(m.reshape(k, P, 512).transpose(1, 0, 2)).reshape(P, k * 512)
        if k < KB:
            c = np.concatenate([c, np.zeros((P, (KB - k) * 512), c.dtype)], axis=1)
        return c

    def halves(m, heads, dim, per):
        return m.reshape(m.shape[0], heads // per, per, 2, dim // 2).transpose(0, 1, 3, 2, 4).reshape(m.shape[0], -1)

    w = {}
    w["A0q"], w["A0k"] = halves(i["L0_attn_wq"], 16, 32, 8), halves(i["L0_attn_wk"], 16, 32, 8)
    w["A0v"], w["A0o"] = i["L0_attn_wv"], i["L0_attn_wo"]
    w["X0k"], w["X0v"] = i["L0_xattn_Wkv"][:512].T, i["L0_xattn_Wkv"][512:].T
    w["X0q"], w["X0g"], w["X0o"] = i["L0_xattn_Wq"].T, i["L0_xattn_Wg"].T, i["L0_xattn_Wo"].T

    def router(m):
        r = np.zeros((512, 512), m.dtype)
        r[:, :8] = m.T
        return r

    w["F0r"], w["F1r"] = router(i["L0_ffn_router_weight"]), router(i["L1_ffn_gate_w"])
    for e in range(NE):
        w[f"F0g{e}"], w[f"F0u{e}"] = i["L0_ffn_gate_up_proj"][e][:, 0::2], i["L0_ffn_gate_up_proj"][e][:, 1::2]
        w[f"F0d{e}"] = i["L0_ffn_down_proj"][e]
        w[f"F1h{e}"] = np.concatenate([i["L1_ffn_w1"][e].T, i["L1_ffn_w3"][e].T], axis=1)
        w[f"F1d{e}"] = i["L1_ffn_w2"][e].T
    w[f"F1h{NE}"] = np.concatenate([i["L1_ffn_ws1"].T, i["L1_ffn_ws3"].T], axis=1)
    w[f"F1d{NE}"] = i["L1_ffn_ws2"].T
    qkv = i["L1_attn_w_qkv"]
    q = halves(qkv[:, :1024], 16, 64, 4)
    w["A1q0"], w["A1q1"] = q[:, :512], q[:, 512:]
    w["A1kv"] = np.concatenate([halves(qkv[:, 1024:1280], 4, 64, 4), qkv[:, 1280:]], axis=1)
    w["A1o0"], w["A1o1"] = i["L1_attn_w_out"][:512], i["L1_attn_w_out"][512:]
    for n, k in (("ki", "k_img_w"), ("vi", "v_img_w"), ("k", "k_w"), ("v", "v_w"), ("q", "q_w"), ("o", "o_w")):
        w["X1" + n] = i["L1_xattn_" + k].T

    f32 = np.float32
    small = np.zeros((P, 100), f32)

    def by_block(name, v):
        small[:, COL[name]:COL[name] + v.size // P] = v.reshape(-1, P).T

    gu = i["L0_ffn_gate_up_proj_bias"]
    by_block("gb", np.ascontiguousarray(gu[:, 0::2]))
    by_block("ub", np.ascontiguousarray(gu[:, 1::2]))
    for name, key in (("gam", "L1_attn_gamma"), ("wq", "L1_xattn_norm_q_w"), ("wk", "L1_xattn_norm_k_w"),
                      ("wki", "L1_xattn_norm_k_img_w")):
        by_block(name, i[key])
    small[0, COL["img"]] = 1
    small[1:, COL["txt"]] = 1
    small[:8, COL["rb"]] = i["L0_ffn_router_bias"]
    small[:, COL["half"]], small[:, COL["mhalf"]], small[:, COL["mone"]] = 0.5, -0.5, -1.0
    for j in range(4):
        small[32 * j:32 * j + 32, COL["hm"] + j] = 1
    small[:, COL["iota"]:COL["iota"] + 8] = np.arange(8)
    pattern = np.zeros((4, SC), f32)
    pattern[0:2, :IMG] = 1
    pattern[2:4, IMG:] = 1
    pattern = np.ascontiguousarray(np.broadcast_to(pattern[:, None, :], (4, 4, SC))).reshape(P, 1, 128)
    pattern = np.repeat(pattern, 2, axis=1)
    bdmask = np.zeros((P, P), f32)
    for j in range(4):
        bdmask[32 * j:32 * j + 32, 32 * j:32 * j + 32] = 1
    down_bias = np.zeros((P, 512), f32)
    down_bias[:NE] = i["L0_ffn_down_proj_bias"]
    rows = lambda v: np.ascontiguousarray(np.broadcast_to(v, (P, 512)))
    return {
        "x": i["x"].reshape(NT, P, D), "ctxT": np.ascontiguousarray(
            i["ctx_2048"].transpose(0, 2, 1).reshape(B, KB, P, SC).transpose(0, 2, 1, 3)),
        "weights": np.stack([chunk(np.ascontiguousarray(w[n])) for n in CHUNKS]),
        "small": small, "pattern": pattern, "bdmask": bdmask, "down_bias": down_bias,
        "rope0": rope_table(32, 8), "rope1": rope_table(64, 4),
        "bg": rows(i["L0_xattn_bg"]), "q_b": rows(i["L1_xattn_q_b"]), "o_b": rows(i["L1_xattn_o_b"]),
        "k_b": rows(i["L1_xattn_k_b"]), "v_b": rows(i["L1_xattn_v_b"]),
        "ki_b": rows(i["L1_xattn_k_img_b"]), "vi_b": rows(i["L1_xattn_v_img_b"]),
    }


def build(arrays, make):
    noted = None
    for _ in range(2):
        nc = make()
        args = {n: nc.dram_tensor(n + "_in", v.shape, F32, kind="ExternalInput").ap() for n, v in arrays.items()}
        out = nc.dram_tensor("out_0_dram", (NT, P, D), F32, kind="ExternalOutput").ap()
        counts = Counts(noted)
        decoder(nc, args, out, counts)
        assert noted is None or noted == counts.at
        noted = counts.at
    return nc


def kernel(**inputs):
    import concourse.bacc as bacc
    from concourse.bass_utils import run_bass_kernel_spmd

    arrays = laid_out({k: np.asarray(v) for k, v in inputs.items()})
    nc = build(arrays, lambda: bacc.Bacc("TRN2", target_bir_lowering=False, num_devices=1))
    r = run_bass_kernel_spmd(nc, [{n + "_in": v for n, v in arrays.items()}], core_ids=[0])
    return r.results[0]["out_0_dram"].reshape(B, S, D)
```
